# Optimizing a Trainium2 kernel written in Bass

```python
import numpy as np
import jax
import jax.numpy as jnp

def _softmax(x, axis=-1):
    return jax.nn.softmax(x, axis=axis)

def _gelu(x):
    return jax.nn.gelu(x, approximate=True)

def _silu(x):
    return jax.nn.silu(x)

def _sigmoid(x):
    return jax.nn.sigmoid(x)

def _layernorm(x, axis=-1, eps=1e-05):
    m = jnp.mean(x, axis=axis, keepdims=True)
    v = jnp.var(x, axis=axis, keepdims=True)
    return (x - m) / jnp.sqrt(v + eps)

def _scatter_add(tgt, idx, src, axis=0):
    return tgt.at[idx].add(src)

def _segment_sum(src, seg, n):
    return jax.ops.segment_sum(src, seg, n)
kernel_name = 'mk_xattn_seq_d4_seqx_r4_3f62eb'

def setup_inputs(seed: int=0):
    np.random.seed(seed)
    _w = jnp.asarray

    def _rec_inputs():
        import jax
        import jax.numpy as jnp
        _rk = jax.random.key(seed)
        x = -0.0002928 + 1 * jax.random.normal(jax.random.fold_in(_rk, 1), (8, 512, 256), jnp.float32)
        _lenS = 512 - jax.random.randint(jax.random.fold_in(_rk, 7), (8,), 0, max(1, 512 // 4) + 1, jnp.int32)
        _lenS2 = 64 - jax.random.randint(jax.random.fold_in(_rk, 8), (8,), 0, max(1, 64 // 4) + 1, jnp.int32)
        _ctx_768P = jax.random.normal(jax.random.fold_in(_rk, 11), (8, 16, 192), jnp.float32)
        _ctx_768c = jax.random.dirichlet(jax.random.fold_in(_rk, 511), 0.3 * jnp.ones((16,), jnp.float32), (8, 64))
        _ctx_768t = jnp.einsum('bsk,bkd->bsd', _ctx_768c, _ctx_768P)
        _ctx_768t = _ctx_768t * jax.lax.rsqrt(jnp.mean(jnp.square(_ctx_768t)) + 1e-12) * 0.953939
        ctx_768 = -0.00423632 + 0.9977 * (_ctx_768t + 0.3 * jax.random.normal(jax.random.fold_in(_rk, 611), (8, 64, 192), jnp.float32))
        return (x, ctx_768)
    x, ctx_768 = _rec_inputs()

    def _L0_xattn_setup():
        import jax, jax.numpy as jnp
        import numpy as np
        DIM, HEADS, DHEAD, CTX_DIM = (256, 16, 64, 192)
        INNER = HEADS * DHEAD
        FF_HID = 4 * DIM
        EPS = 1e-05

        def _ln(x, g, b):
            mu = jnp.mean(x, axis=-1, keepdims=True)
            var = jnp.mean(jnp.square(x - mu), axis=-1, keepdims=True)
            return (x - mu) * jax.lax.rsqrt(var + EPS) * g + b

        def _attn(x, ctx, Wq, Wk, Wv, Wo, bo):
            b, n, _ = x.shape
            m = ctx.shape[1]
            q = (x @ Wq).reshape(b, n, HEADS, DHEAD)
            k = (ctx @ Wk).reshape(b, m, HEADS, DHEAD)
            v = (ctx @ Wv).reshape(b, m, HEADS, DHEAD)
            scale = DHEAD ** (-0.5)
            sim = jnp.einsum('bihd,bjhd->bhij', q, k) * scale
            attn = jax.nn.softmax(sim, axis=-1)
            out = jnp.einsum('bhij,bjhd->bihd', attn, v).reshape(b, n, INNER)
            return out @ Wo + bo
        key = jax.random.key(seed)
        ks = jax.random.split(key, 24)

        def w(k, shape, fan_in):
            return jax.random.normal(k, shape, jnp.float32) * fan_in ** (-0.5)
        inp = {'x': jax.random.normal(ks[0], (2, 512, DIM), jnp.float32), 'context': jax.random.normal(ks[1], (2, 77, CTX_DIM), jnp.float32), 'Wq1': w(ks[2], (DIM, INNER), DIM), 'Wk1': w(ks[3], (DIM, INNER), DIM), 'Wv1': w(ks[4], (DIM, INNER), DIM), 'Wo1': w(ks[5], (INNER, DIM), INNER), 'bo1': jnp.zeros((DIM,), jnp.float32), 'Wq2': w(ks[6], (DIM, INNER), DIM), 'Wk2': w(ks[7], (CTX_DIM, INNER), CTX_DIM), 'Wv2': w(ks[8], (CTX_DIM, INNER), CTX_DIM), 'Wo2': w(ks[9], (INNER, DIM), INNER), 'bo2': jnp.zeros((DIM,), jnp.float32), 'Wp': w(ks[10], (DIM, 2 * FF_HID), DIM), 'bp': jnp.zeros((2 * FF_HID,), jnp.float32), 'W2': w(ks[11], (FF_HID, DIM), FF_HID), 'b2': jnp.zeros((DIM,), jnp.float32), 'g1': jnp.ones((DIM,), jnp.float32), 'be1': jnp.zeros((DIM,), jnp.float32), 'g2': jnp.ones((DIM,), jnp.float32), 'be2': jnp.zeros((DIM,), jnp.float32), 'g3': jnp.ones((DIM,), jnp.float32), 'be3': jnp.zeros((DIM,), jnp.float32)}
        return inp
    _L0_xattn_all = _L0_xattn_setup()
    _L0_xattn_in = {k: v for k, v in _L0_xattn_all.items() if k in ('Wq1', 'Wk1', 'Wv1', 'Wo1', 'bo1', 'Wq2', 'Wk2', 'Wv2', 'Wo2', 'bo2', 'Wp', 'bp', 'W2', 'b2', 'g1', 'be1', 'g2', 'be2', 'g3', 'be3')}
    del _L0_xattn_all

    def _L1_xattn_setup():
        import jax, jax.numpy as jnp
        import numpy as np
        B_, S_, P_, D_ = (2, 128, 64, 256)
        L_ = 4
        DI_ = 2 * D_
        DS_ = 16
        DC_ = 4
        DR_ = D_ // 16
        PCD_ = 192

        def rmsnorm(x, w, eps=1e-05):
            return x * jax.lax.rsqrt(jnp.mean(x * x, axis=-1, keepdims=True) + eps) * w

        def mamba_block(x, ip_w, cw, cb, xp_w, dtp_w, dtp_b, A_log, Dp, op_w):
            B, S, _ = x.shape
            xz = jnp.einsum('bsd,ed->bse', x, ip_w)
            xi, z = jnp.split(xz, 2, axis=-1)
            xt = xi.transpose(0, 2, 1)
            conv = jax.lax.conv_general_dilated(xt, cw[:, None, :], (1,), [(DC_ - 1, 0)], feature_group_count=DI_) + cb[:, None]
            xi = jax.nn.silu(conv.transpose(0, 2, 1))
            xdbl = jnp.einsum('bse,fe->bsf', xi, xp_w)
            dt, Bm, Cm = jnp.split(xdbl, [DR_, DR_ + DS_], axis=-1)
            dt = jax.nn.softplus(jnp.einsum('bsr,er->bse', dt, dtp_w) + dtp_b)
            A = -jnp.exp(A_log)
            dA = jnp.exp(dt[..., None] * A)
            dBu = dt[..., None] * Bm[:, :, None, :] * xi[..., None]

            def step(h, t):
                da, dbu, c = t
                h = da * h + dbu
                return (h, jnp.einsum('bes,bs->be', h, c))
            h0 = jnp.zeros((B, DI_, DS_), x.dtype)
            _, ys = jax.lax.scan(step, h0, (dA.transpose(1, 0, 2, 3), dBu.transpose(1, 0, 2, 3), Cm.transpose(1, 0, 2)))
            y = ys.transpose(1, 0, 2) + xi * Dp
            y = y * jax.nn.silu(z)
            return jnp.einsum('bse,de->bsd', y, op_w)
        key = jax.random.key(seed)
        ks = jax.random.split(key, 12)
        n = lambda k, s, sc=0.02: jax.random.normal(k, s, dtype=jnp.float32) * sc
        A_log = jnp.log(jnp.broadcast_to(jnp.arange(1, DS_ + 1, dtype=jnp.float32), (L_, DI_, DS_)))
        return {'x': jax.random.normal(ks[0], (B_, S_, D_), dtype=jnp.float32), 'prepend_cond': jax.random.normal(ks[1], (B_, P_, PCD_), dtype=jnp.float32), 'pre_w1': n(ks[2], (PCD_, D_)), 'pre_w2': n(ks[3], (D_, D_)), 'norm_w': jnp.ones((L_, D_), jnp.float32), 'in_proj_w': n(ks[4], (L_, 2 * DI_, D_)), 'conv_w': n(ks[5], (L_, DI_, DC_), 0.1), 'conv_b': jnp.zeros((L_, DI_), jnp.float32), 'x_proj_w': n(ks[6], (L_, DR_ + 2 * DS_, DI_)), 'dt_proj_w': n(ks[7], (L_, DI_, DR_), 0.1), 'dt_proj_b': jax.random.uniform(ks[8], (L_, DI_), jnp.float32, -4.0, -2.0), 'A_log': A_log, 'D_param': jnp.ones((L_, DI_), jnp.float32), 'out_proj_w': n(ks[9], (L_, D_, DI_)), 'final_norm_w': jnp.ones((D_,), jnp.float32)}
    _L1_xattn_all = _L1_xattn_setup()
    _L1_xattn_in = {k: v for k, v in _L1_xattn_all.items() if k in ('pre_w1', 'pre_w2', 'norm_w', 'in_proj_w', 'conv_w', 'conv_b', 'x_proj_w', 'dt_proj_w', 'dt_proj_b', 'A_log', 'D_param', 'out_proj_w', 'final_norm_w')}
    del _L1_xattn_all

    def _L2_xattn_setup():
        import jax, jax.numpy as jnp
        import numpy as np
        DIM1, DIM2, H = (256, 192, 16)
        HID = 4 * DIM1
        EPS = 1e-05

        def layernorm(x, w, b):
            mu = jnp.mean(x, axis=-1, keepdims=True)
            var = jnp.mean((x - mu) ** 2, axis=-1, keepdims=True)
            return (x - mu) * jax.lax.rsqrt(var + EPS) * w + b
        key = jax.random.key(seed)
        ks = jax.random.split(key, 12)
        s1 = 1.0 / np.sqrt(DIM1)
        s2 = 1.0 / np.sqrt(DIM2)
        sh = 1.0 / np.sqrt(HID)
        return {'x': jax.random.normal(ks[0], (4, 256, DIM1), jnp.float32), 'y': jax.random.normal(ks[1], (4, 256, DIM2), jnp.float32), 'ln1_w': jnp.ones((DIM1,), jnp.float32), 'ln1_b': jnp.zeros((DIM1,), jnp.float32), 'ln2_w': jnp.ones((DIM2,), jnp.float32), 'ln2_b': jnp.zeros((DIM2,), jnp.float32), 'ln3_w': jnp.ones((DIM1,), jnp.float32), 'ln3_b': jnp.zeros((DIM1,), jnp.float32), 'Wq': jax.random.uniform(ks[2], (DIM1, DIM1), jnp.float32, -s1, s1), 'Wkv': jax.random.uniform(ks[3], (DIM2, 2 * DIM1), jnp.float32, -s2, s2), 'Wproj': jax.random.uniform(ks[4], (DIM1, DIM1), jnp.float32, -s1, s1), 'bproj': jnp.zeros((DIM1,), jnp.float32), 'W1': jax.random.uniform(ks[5], (DIM1, HID), jnp.float32, -s1, s1), 'b1': jnp.zeros((HID,), jnp.float32), 'W2': jax.random.uniform(ks[6], (HID, DIM1), jnp.float32, -sh, sh), 'b2': jnp.zeros((DIM1,), jnp.float32)}
    _L2_xattn_all = _L2_xattn_setup()
    _L2_xattn_in = {k: v for k, v in _L2_xattn_all.items() if k in ('ln1_w', 'ln1_b', 'ln2_w', 'ln2_b', 'ln3_w', 'ln3_b', 'Wq', 'Wkv', 'Wproj', 'bproj', 'W1', 'b1', 'W2', 'b2')}
    del _L2_xattn_all

    def _L3_xattn_setup():
        import jax, jax.numpy as jnp
        import numpy as np
        EPS = 1e-05

        def _layer_norm(x, gamma, beta):
            mu = jnp.mean(x, axis=-1, keepdims=True)
            var = jnp.mean(jnp.square(x - mu), axis=-1, keepdims=True)
            return (x - mu) * jax.lax.rsqrt(var + EPS) * gamma + beta
        key = jax.random.key(seed)
        ks = jax.random.split(key, 12)
        B, Nq, Nkv = (8, 512, 512)
        E, Q, KV = (256, 256, 192)

        def lin(k, fan_in, shape):
            bound = 1.0 / np.sqrt(fan_in)
            return jax.random.uniform(k, shape, jnp.float32, -bound, bound)
        return {'q_feat': jax.random.normal(ks[0], (B, Nq, Q), jnp.float32), 'kv_feat': jax.random.normal(ks[1], (B, Nkv, KV), jnp.float32), 'Wq': lin(ks[2], Q, (E, Q)), 'bq': lin(ks[3], Q, (E,)), 'Wk': lin(ks[4], KV, (E, KV)), 'bk': lin(ks[5], KV, (E,)), 'Wv': lin(ks[6], KV, (E, KV)), 'bv': lin(ks[7], KV, (E,)), 'Wd': lin(ks[8], E, (E, E)), 'bd': lin(ks[9], E, (E,)), 'g_q': jnp.ones((Q,), jnp.float32), 'be_q': jnp.zeros((Q,), jnp.float32), 'g_kv': jnp.ones((KV,), jnp.float32), 'be_kv': jnp.zeros((KV,), jnp.float32)}
    _L3_xattn_all = _L3_xattn_setup()
    _L3_xattn_in = {k: v for k, v in _L3_xattn_all.items() if k in ('Wq', 'bq', 'Wk', 'bk', 'Wv', 'bv', 'Wd', 'bd', 'g_q', 'be_q', 'g_kv', 'be_kv')}
    del _L3_xattn_all
    return {'x': x, 'ctx_768': ctx_768, 'L0_xattn_Wq1': _L0_xattn_in['Wq1'], 'L0_xattn_Wk1': _L0_xattn_in['Wk1'], 'L0_xattn_Wv1': _L0_xattn_in['Wv1'], 'L0_xattn_Wo1': _L0_xattn_in['Wo1'], 'L0_xattn_bo1': _L0_xattn_in['bo1'], 'L0_xattn_Wq2': _L0_xattn_in['Wq2'], 'L0_xattn_Wk2': _L0_xattn_in['Wk2'], 'L0_xattn_Wv2': _L0_xattn_in['Wv2'], 'L0_xattn_Wo2': _L0_xattn_in['Wo2'], 'L0_xattn_bo2': _L0_xattn_in['bo2'], 'L0_xattn_Wp': _L0_xattn_in['Wp'], 'L0_xattn_bp': _L0_xattn_in['bp'], 'L0_xattn_W2': _L0_xattn_in['W2'], 'L0_xattn_b2': _L0_xattn_in['b2'], 'L0_xattn_g1': _L0_xattn_in['g1'], 'L0_xattn_be1': _L0_xattn_in['be1'], 'L0_xattn_g2': _L0_xattn_in['g2'], 'L0_xattn_be2': _L0_xattn_in['be2'], 'L0_xattn_g3': _L0_xattn_in['g3'], 'L0_xattn_be3': _L0_xattn_in['be3'], 'L1_xattn_pre_w1': _L1_xattn_in['pre_w1'], 'L1_xattn_pre_w2': _L1_xattn_in['pre_w2'], 'L1_xattn_norm_w': _L1_xattn_in['norm_w'], 'L1_xattn_in_proj_w': _L1_xattn_in['in_proj_w'], 'L1_xattn_conv_w': _L1_xattn_in['conv_w'], 'L1_xattn_conv_b': _L1_xattn_in['conv_b'], 'L1_xattn_x_proj_w': _L1_xattn_in['x_proj_w'], 'L1_xattn_dt_proj_w': _L1_xattn_in['dt_proj_w'], 'L1_xattn_dt_proj_b': _L1_xattn_in['dt_proj_b'], 'L1_xattn_A_log': _L1_xattn_in['A_log'], 'L1_xattn_D_param': _L1_xattn_in['D_param'], 'L1_xattn_out_proj_w': _L1_xattn_in['out_proj_w'], 'L1_xattn_final_norm_w': _L1_xattn_in['final_norm_w'], 'L2_xattn_ln1_w': _L2_xattn_in['ln1_w'], 'L2_xattn_ln1_b': _L2_xattn_in['ln1_b'], 'L2_xattn_ln2_w': _L2_xattn_in['ln2_w'], 'L2_xattn_ln2_b': _L2_xattn_in['ln2_b'], 'L2_xattn_ln3_w': _L2_xattn_in['ln3_w'], 'L2_xattn_ln3_b': _L2_xattn_in['ln3_b'], 'L2_xattn_Wq': _L2_xattn_in['Wq'], 'L2_xattn_Wkv': _L2_xattn_in['Wkv'], 'L2_xattn_Wproj': _L2_xattn_in['Wproj'], 'L2_xattn_bproj': _L2_xattn_in['bproj'], 'L2_xattn_W1': _L2_xattn_in['W1'], 'L2_xattn_b1': _L2_xattn_in['b1'], 'L2_xattn_W2': _L2_xattn_in['W2'], 'L2_xattn_b2': _L2_xattn_in['b2'], 'L3_xattn_Wq': _L3_xattn_in['Wq'], 'L3_xattn_bq': _L3_xattn_in['bq'], 'L3_xattn_Wk': _L3_xattn_in['Wk'], 'L3_xattn_bk': _L3_xattn_in['bk'], 'L3_xattn_Wv': _L3_xattn_in['Wv'], 'L3_xattn_bv': _L3_xattn_in['bv'], 'L3_xattn_Wd': _L3_xattn_in['Wd'], 'L3_xattn_bd': _L3_xattn_in['bd'], 'L3_xattn_g_q': _L3_xattn_in['g_q'], 'L3_xattn_be_q': _L3_xattn_in['be_q'], 'L3_xattn_g_kv': _L3_xattn_in['g_kv'], 'L3_xattn_be_kv': _L3_xattn_in['be_kv']}

def reference(x, ctx_768, L0_xattn_Wq1, L0_xattn_Wk1, L0_xattn_Wv1, L0_xattn_Wo1, L0_xattn_bo1, L0_xattn_Wq2, L0_xattn_Wk2, L0_xattn_Wv2, L0_xattn_Wo2, L0_xattn_bo2, L0_xattn_Wp, L0_xattn_bp, L0_xattn_W2, L0_xattn_b2, L0_xattn_g1, L0_xattn_be1, L0_xattn_g2, L0_xattn_be2, L0_xattn_g3, L0_xattn_be3, L1_xattn_pre_w1, L1_xattn_pre_w2, L1_xattn_norm_w, L1_xattn_in_proj_w, L1_xattn_conv_w, L1_xattn_conv_b, L1_xattn_x_proj_w, L1_xattn_dt_proj_w, L1_xattn_dt_proj_b, L1_xattn_A_log, L1_xattn_D_param, L1_xattn_out_proj_w, L1_xattn_final_norm_w, L2_xattn_ln1_w, L2_xattn_ln1_b, L2_xattn_ln2_w, L2_xattn_ln2_b, L2_xattn_ln3_w, L2_xattn_ln3_b, L2_xattn_Wq, L2_xattn_Wkv, L2_xattn_Wproj, L2_xattn_bproj, L2_xattn_W1, L2_xattn_b1, L2_xattn_W2, L2_xattn_b2, L3_xattn_Wq, L3_xattn_bq, L3_xattn_Wk, L3_xattn_bk, L3_xattn_Wv, L3_xattn_bv, L3_xattn_Wd, L3_xattn_bd, L3_xattn_g_q, L3_xattn_be_q, L3_xattn_g_kv, L3_xattn_be_kv):
    import jax
    import jax.numpy as jnp

    def _L0_xattn_ref(x, context, Wq1, Wk1, Wv1, Wo1, bo1, Wq2, Wk2, Wv2, Wo2, bo2, Wp, bp, W2, b2, g1, be1, g2, be2, g3, be3):
        import jax, jax.numpy as jnp
        import numpy as np
        DIM, HEADS, DHEAD, CTX_DIM = (256, 16, 64, 192)
        INNER = HEADS * DHEAD
        FF_HID = 4 * DIM
        EPS = 1e-05

        def _ln(x, g, b):
            mu = jnp.mean(x, axis=-1, keepdims=True)
            var = jnp.mean(jnp.square(x - mu), axis=-1, keepdims=True)
            return (x - mu) * jax.lax.rsqrt(var + EPS) * g + b

        def _attn(x, ctx, Wq, Wk, Wv, Wo, bo):
            b, n, _ = x.shape
            m = ctx.shape[1]
            q = (x @ Wq).reshape(b, n, HEADS, DHEAD)
            k = (ctx @ Wk).reshape(b, m, HEADS, DHEAD)
            v = (ctx @ Wv).reshape(b, m, HEADS, DHEAD)
            scale = DHEAD ** (-0.5)
            sim = jnp.einsum('bihd,bjhd->bhij', q, k) * scale
            attn = jax.nn.softmax(sim, axis=-1)
            out = jnp.einsum('bhij,bjhd->bihd', attn, v).reshape(b, n, INNER)
            return out @ Wo + bo
        h = _ln(x, g1, be1)
        x = _attn(h, h, Wq1, Wk1, Wv1, Wo1, bo1) + x
        h = _ln(x, g2, be2)
        x = _attn(h, context, Wq2, Wk2, Wv2, Wo2, bo2) + x
        h = _ln(x, g3, be3)
        y = h @ Wp + bp
        a, gate = (y[..., :FF_HID], y[..., FF_HID:])
        x = a * jax.nn.gelu(gate, approximate=False) @ W2 + b2 + x
        return x

    def _L1_xattn_ref(x, prepend_cond, pre_w1, pre_w2, norm_w, in_proj_w, conv_w, conv_b, x_proj_w, dt_proj_w, dt_proj_b, A_log, D_param, out_proj_w, final_norm_w):
        import jax, jax.numpy as jnp
        import numpy as np
        B_, S_, P_, D_ = (2, 128, 64, 256)
        L_ = 4
        DI_ = 2 * D_
        DS_ = 16
        DC_ = 4
        DR_ = D_ // 16
        PCD_ = 192

        def rmsnorm(x, w, eps=1e-05):
            return x * jax.lax.rsqrt(jnp.mean(x * x, axis=-1, keepdims=True) + eps) * w

        def mamba_block(x, ip_w, cw, cb, xp_w, dtp_w, dtp_b, A_log, Dp, op_w):
            B, S, _ = x.shape
            xz = jnp.einsum('bsd,ed->bse', x, ip_w)
            xi, z = jnp.split(xz, 2, axis=-1)
            xt = xi.transpose(0, 2, 1)
            conv = jax.lax.conv_general_dilated(xt, cw[:, None, :], (1,), [(DC_ - 1, 0)], feature_group_count=DI_) + cb[:, None]
            xi = jax.nn.silu(conv.transpose(0, 2, 1))
            xdbl = jnp.einsum('bse,fe->bsf', xi, xp_w)
            dt, Bm, Cm = jnp.split(xdbl, [DR_, DR_ + DS_], axis=-1)
            dt = jax.nn.softplus(jnp.einsum('bsr,er->bse', dt, dtp_w) + dtp_b)
            A = -jnp.exp(A_log)
            dA = jnp.exp(dt[..., None] * A)
            dBu = dt[..., None] * Bm[:, :, None, :] * xi[..., None]

            def step(h, t):
                da, dbu, c = t
                h = da * h + dbu
                return (h, jnp.einsum('bes,bs->be', h, c))
            h0 = jnp.zeros((B, DI_, DS_), x.dtype)
            _, ys = jax.lax.scan(step, h0, (dA.transpose(1, 0, 2, 3), dBu.transpose(1, 0, 2, 3), Cm.transpose(1, 0, 2)))
            y = ys.transpose(1, 0, 2) + xi * Dp
            y = y * jax.nn.silu(z)
            return jnp.einsum('bse,de->bsd', y, op_w)
        p = jax.nn.silu(prepend_cond @ pre_w1) @ pre_w2
        h = jnp.concatenate([p, x], axis=1)
        for l in range(L_):
            h = h + mamba_block(rmsnorm(h, norm_w[l]), in_proj_w[l], conv_w[l], conv_b[l], x_proj_w[l], dt_proj_w[l], dt_proj_b[l], A_log[l], D_param[l], out_proj_w[l])
        h = rmsnorm(h, final_norm_w)
        return h[:, P_:, :]

    def _L2_xattn_ref(x, y, ln1_w, ln1_b, ln2_w, ln2_b, ln3_w, ln3_b, Wq, Wkv, Wproj, bproj, W1, b1, W2, b2):
        import jax, jax.numpy as jnp
        import numpy as np
        DIM1, DIM2, H = (256, 192, 16)
        HID = 4 * DIM1
        EPS = 1e-05

        def layernorm(x, w, b):
            mu = jnp.mean(x, axis=-1, keepdims=True)
            var = jnp.mean((x - mu) ** 2, axis=-1, keepdims=True)
            return (x - mu) * jax.lax.rsqrt(var + EPS) * w + b
        B, N1, C1 = x.shape
        hd = C1 // H
        scale = hd ** (-0.5)
        xn = layernorm(x, ln1_w, ln1_b)
        yn = layernorm(y, ln2_w, ln2_b)
        q = (xn @ Wq).reshape(B, N1, H, hd).transpose(0, 2, 1, 3)
        kv = (yn @ Wkv).reshape(B, y.shape[1], 2, H, hd)
        k = kv[:, :, 0].transpose(0, 2, 1, 3)
        v = kv[:, :, 1].transpose(0, 2, 1, 3)
        attn = jax.nn.softmax(jnp.einsum('bhqd,bhkd->bhqk', q, k) * scale, axis=-1)
        o = jnp.einsum('bhqk,bhkd->bhqd', attn, v).transpose(0, 2, 1, 3).reshape(B, N1, C1)
        x = x + (o @ Wproj + bproj)
        h = jax.nn.gelu(layernorm(x, ln3_w, ln3_b) @ W1 + b1, approximate=False)
        x = x + (h @ W2 + b2)
        return x

    def _L3_xattn_ref(q_feat, kv_feat, Wq, bq, Wk, bk, Wv, bv, Wd, bd, g_q, be_q, g_kv, be_kv):
        import jax, jax.numpy as jnp
        import numpy as np
        EPS = 1e-05

        def _layer_norm(x, gamma, beta):
            mu = jnp.mean(x, axis=-1, keepdims=True)
            var = jnp.mean(jnp.square(x - mu), axis=-1, keepdims=True)
            return (x - mu) * jax.lax.rsqrt(var + EPS) * gamma + beta
        qn = _layer_norm(q_feat, g_q, be_q)
        kvn = _layer_norm(kv_feat, g_kv, be_kv)
        q = jnp.einsum('bnq,eq->bne', qn, Wq) + bq
        k = jnp.einsum('bmk,ek->bme', kvn, Wk) + bk
        v = jnp.einsum('bmk,ek->bme', kvn, Wv) + bv
        scores = jnp.einsum('bne,bme->bnm', q, k)
        attn = jax.nn.softmax(scores, axis=-1)
        ctx = jnp.einsum('bnm,bme->bne', attn, v)
        hidden = jnp.einsum('bne,fe->bnf', ctx, Wd) + bd
        return q_feat + hidden
    x = _L0_xattn_ref(x, ctx_768, L0_xattn_Wq1, L0_xattn_Wk1, L0_xattn_Wv1, L0_xattn_Wo1, L0_xattn_bo1, L0_xattn_Wq2, L0_xattn_Wk2, L0_xattn_Wv2, L0_xattn_Wo2, L0_xattn_bo2, L0_xattn_Wp, L0_xattn_bp, L0_xattn_W2, L0_xattn_b2, L0_xattn_g1, L0_xattn_be1, L0_xattn_g2, L0_xattn_be2, L0_xattn_g3, L0_xattn_be3)
    x = _L1_xattn_ref(x, ctx_768, L1_xattn_pre_w1, L1_xattn_pre_w2, L1_xattn_norm_w, L1_xattn_in_proj_w, L1_xattn_conv_w, L1_xattn_conv_b, L1_xattn_x_proj_w, L1_xattn_dt_proj_w, L1_xattn_dt_proj_b, L1_xattn_A_log, L1_xattn_D_param, L1_xattn_out_proj_w, L1_xattn_final_norm_w)
    x = _L2_xattn_ref(x, ctx_768, L2_xattn_ln1_w, L2_xattn_ln1_b, L2_xattn_ln2_w, L2_xattn_ln2_b, L2_xattn_ln3_w, L2_xattn_ln3_b, L2_xattn_Wq, L2_xattn_Wkv, L2_xattn_Wproj, L2_xattn_bproj, L2_xattn_W1, L2_xattn_b1, L2_xattn_W2, L2_xattn_b2)
    x = _L3_xattn_ref(x, ctx_768, L3_xattn_Wq, L3_xattn_bq, L3_xattn_Wk, L3_xattn_bk, L3_xattn_Wv, L3_xattn_bv, L3_xattn_Wd, L3_xattn_bd, L3_xattn_g_q, L3_xattn_be_q, L3_xattn_g_kv, L3_xattn_be_kv)
    return x

_drawn_inputs = setup_inputs


def setup_inputs(seed=0):
    import zlib

    import numpy as np

    out = dict(_drawn_inputs(seed))
    spreads = {'L0_xattn_bo1': (0.0, 0.1),
     'L0_xattn_bo2': (0.0, 0.1),
     'L0_xattn_bp': (0.0, 0.1),
     'L0_xattn_b2': (0.0, 0.1),
     'L0_xattn_g1': (1.0, 0.2),
     'L0_xattn_be1': (0.0, 0.1),
     'L0_xattn_g2': (1.0, 0.2),
     'L0_xattn_be2': (0.0, 0.324),
     'L0_xattn_g3': (1.0, 0.2),
     'L0_xattn_be3': (0.0, 0.1),
     'L1_xattn_norm_w': (1.0, 0.6),
     'L1_xattn_conv_b': (0.0, 0.8),
     'L1_xattn_D_param': (1.0, 0.6),
     'L1_xattn_final_norm_w': (1.0, 0.2),
     'L2_xattn_ln1_w': (1.0, 0.6),
     'L2_xattn_ln1_b': (0.0, 2.0),
     'L2_xattn_ln2_w': (1.0, 0.2),
     'L2_xattn_ln2_b': (0.0, 0.281),
     'L2_xattn_ln3_w': (1.0, 0.2),
     'L2_xattn_ln3_b': (0.0, 0.404),
     'L2_xattn_bproj': (0.0, 0.1),
     'L2_xattn_b1': (0.0, 0.1),
     'L2_xattn_b2': (0.0, 0.1),
     'L3_xattn_g_q': (1.0, 0.2),
     'L3_xattn_be_q': (0.0, 0.1),
     'L3_xattn_g_kv': (1.0, 0.2),
     'L3_xattn_be_kv': (0.0, 0.282)}
    factors = {'L1_xattn_pre_w1': 8.0,
     'L1_xattn_pre_w2': 8.0,
     'L1_xattn_in_proj_w': 7.905,
     'L1_xattn_conv_w': 8.0,
     'L1_xattn_x_proj_w': 8.0,
     'L1_xattn_dt_proj_w': 8.0,
     'L1_xattn_dt_proj_b': 8.0,
     'L1_xattn_A_log': 8.0,
     'L1_xattn_out_proj_w': 7.831,
     'L3_xattn_bq': 2.687,
     'L3_xattn_bk': 64.0,
     'L3_xattn_bv': 2.79}
    for name, (base, spread) in spreads.items():
        noise = np.random.default_rng([zlib.crc32(name.encode()), seed]).standard_normal(out[name].shape)
        drawn = base * np.exp(spread * noise) if base else spread * noise
        out[name] = jnp.asarray(drawn.astype(out[name].dtype))
    for name, factor in factors.items():
        out[name] = (out[name] * factor).astype(out[name].dtype)
    return out
```

```python
from contextlib import ExitStack

import concourse.bass as bass
from concourse import mybir

F32 = mybir.dt.float32
ALU = mybir.AluOpType
ACT = mybir.ActivationFunctionType
AX = mybir.AxisListType

P = 128
B, T, D, DC = 8, 512, 256, 192
PRE, S1 = 64, 576
KD = D // P
M = 64
H0, DH0 = 16, 64
INNER = H0 * DH0
HID = 4 * D
LAYERS, DI, DS, DTR, TAPS = 4, 512, 16, 16, 4
KI = DI // P
EPS = 1e-5
TC = 192
NCH = S1 // TC
CROWS = (P, DC - P)

VEC_SIZES = [
    ("bo1", 2), ("bo2", 2), ("bp", 16), ("b2_0", 2), ("g1", 2), ("be1", 2), ("g2", 2), ("be2", 2), ("g3", 2), ("be3", 2),
    ("final", 2),
    ("l1w", 2), ("l1b", 2), ("l2w", 2), ("l2b", 2), ("l3w", 2), ("l3b", 2), ("bproj", 2), ("b1", 8), ("b2_2", 2),
    ("bq", 2), ("bk", 2), ("bv", 2), ("bd", 2), ("gq", 2), ("beq", 2), ("gkv", 2), ("bekv", 2),
]
VEC = {}
_at = 0
for _n, _c in VEC_SIZES:
    VEC[_n] = (_at, _c)
    _at += _c
NVEC = _at


class Count:

    def __init__(self, n=0):
        self.before, self.n = 0, n

    def __call__(self, ahead=0):
        return self.before + (self.n + ahead)

    def add(self, k=1):
        self.n += k

    def round(self, i, share, start=0):
        self.before, self.n = i * share + start, 0


class Core:

    def __init__(self, nc, ctx, dram):
        self.nc, self.ctx, self.dram = nc, ctx, dram
        sb = lambda name, shape: ctx.enter_context(nc.sbuf_tensor(name, shape, F32))
        self.X = sb("X", [P, KD, B, S1])
        self.C = sb("C", [P, 2, B * M])
        self.vec = sb("vec", [P, NVEC])
        self.ident = sb("ident", [P, P])
        self.mean_d = sb("mean_d", [P, P])
        self.mean_c = sb("mean_c", [P, P])
        self.weights = [sb("weights0", [P, 8192]), sb("weights1", [P, 8192])]
        self.work = sb("work", [P, 25728])
        self.banks = ctx.enter_context(nc.psum_tensor("banks", [P, 8, 512], F32))
        self.lane_v, self.lane_s = self.banks[:, 6, :], self.banks[:, 7, :]
        self.eps = sb("eps", [P, 1])
        self.one = sb("one", [P, KI])
        self.const_ready = self.sem("const_ready")
        self.loaded = self.sem("loaded")
        self.w_loaded = [self.sem("w0_loaded"), self.sem("w1_loaded")]
        self.context_lanes, self.context_norm = Lanes(self, "context"), Norm(self, "context")
        self.w_count = [0, 0]

    def sem(self, name):
        return self.ctx.enter_context(self.nc.semaphore(name))

    def v(self, name, j=0, n=1):
        at = VEC[name][0] + j
        return self.vec[:, at:at + n]

    def area(self, at, *shape):
        n = 1
        for s in shape:
            n *= s
        names = "abcd"[:len(shape)]
        view = self.work[:, at:at + n]
        if len(shape) > 1:
            view = view.rearrange(f"p ({' '.join(names)}) -> p {' '.join(names)}", **dict(zip(names[1:], shape[1:])))
        return view, at + n


def wview(core, side, at, rows, n):
    return core.weights[side][:, at:at + rows * n].rearrange("p (k n) -> p k n", k=rows)


class Lanes:

    def __init__(self, core, stage):
        self.v_full, self.v_free = core.sem(f"{stage}_v_full"), core.sem(f"{stage}_v_free")
        self.s_full, self.s_free = core.sem(f"{stage}_s_full"), core.sem(f"{stage}_s_free")


class Norm:

    def __init__(self, core, stage):
        self.squared = core.sem(f"{stage}_squared")
        self.rstd = core.sem(f"{stage}_rstd")
        self.scaled = core.sem(f"{stage}_scaled")
        self.ready = core.sem(f"{stage}_normed")


def load_weights(e, core, side, parts):
    for at, src in parts:
        rows, cols = src.shape
        full = rows // P
        for k in range(0, full, 4):
            m = min(4, full - k)
            e.dma_start(wview(core, side, at + k * cols, m, cols), src[k * P:(k + m) * P, :].rearrange("(k p) n -> p k n", p=P)) \
                .then_inc(core.w_loaded[side], 16)
            core.w_count[side] += 16
        if rows % P:
            e.dma_start(core.weights[side][0:rows % P, at + full * cols:at + (full + 1) * cols], src[full * P:rows, :]) \
                .then_inc(core.w_loaded[side], 16)
            core.w_count[side] += 16



def norm_pe(e, core, nm, ln, V, S, n, x, mean, squared, N):
    e.wait_ge(ln.v_free, V())
    for k, (r, ap) in enumerate(x):
        mm = e.matmul(core.lane_v[:, 0:N], mean[0:r, :], ap, start=(k == 0), stop=(k == len(x) - 1))
    mm.then_inc(ln.v_full, 1)
    V.add()
    e.wait_ge(ln.s_free, S())
    e.wait_ge(nm.squared, n + 1)
    for k, (r, _) in enumerate(x):
        mm = e.matmul(core.lane_s[:, 0:N], mean[0:r, :], squared[0:r, k, :], start=(k == 0), stop=(k == len(x) - 1))
    mm.then_inc(ln.s_full, 1)
    S.add()


def norm_dve(e, core, nm, ln, V, S, n, x, centred, std, out, g, N):
    e.wait_ge(ln.v_full, V(1))
    for k, (r, ap) in enumerate(x):
        last = e.tensor_tensor(centred[0:r, k, :], ap, core.lane_v[0:r, 0:N], ALU.subtract)
    last.then_inc(ln.v_free, 1)
    V.add()
    S.add()
    e.wait_ge(ln.s_free, S())
    e.reciprocal(std, std).then_inc(nm.rstd, 1)
    e.wait_ge(nm.rstd, n + 1)
    for k, (r, _) in enumerate(x):
        last = e.scalar_tensor_tensor(out=out[0:r, k, :], in0=centred[0:r, k, :], scalar=core.v(g, k)[0:r, :],
                                      in1=std[0:r, :], op0=ALU.mult, op1=ALU.mult)
    last.then_inc(nm.scaled, 1)


def norm_act(e, core, nm, ln, V, S, n, rows, centred, squared, std, out, be, N):
    V.add()
    e.wait_ge(ln.v_free, V())
    for k, r in enumerate(rows):
        last = e.activation(squared[0:r, k, :], centred[0:r, k, :], ACT.Square)
    last.then_inc(nm.squared, 1)
    e.wait_ge(ln.s_full, S(1))
    e.activation(std, core.lane_s[:, 0:N], ACT.Sqrt, bias=core.eps[:]).then_inc(ln.s_free, 1)
    S.add()
    e.wait_ge(nm.scaled, n + 1)
    for k, r in enumerate(rows):
        last = e.activation(out[0:r, k, :], out[0:r, k, :], ACT.Identity, bias=core.v(be, k)[0:r, :])
    last.then_inc(nm.ready, 1)


UNITS = 2


def self_attention(core):
    at = 0
    normed, at = core.area(at, KD, T)
    centred, at = core.area(at, KD, T)
    squared, at = core.area(at, KD, T)
    std, at = core.area(at, T)
    q, at = core.area(at, 8, T)
    k_, at = core.area(at, 8, T)
    v_, at = core.area(at, 4, INNER)
    probs, at = core.area(at, 4, 2, T)
    probsT, at = core.area(at, 2, 4, T)
    nmax, at = core.area(at, 4, 2)
    sums, at = core.area(at, 4, 2)
    rsum, at = core.area(at, 4, 2)
    wq, wk, wv, wo = (wview(core, 0, 2048 * j, 2 if j < 3 else 8, INNER if j < 3 else D) for j in range(4))
    ln, nm = Lanes(core, "self"), Norm(core, "self")
    s_full = core.sem("self_scores")
    nmax_ready = core.sem("self_nmax")
    exp_done = core.sem("self_exp")
    rsum_ready = core.sem("self_rsum")
    p_ready = core.sem("self_probs")
    t_full = core.sem("self_t_full")
    tv_free, ts_free = core.sem("self_tv_free"), core.sem("self_ts_free")
    V_SHARE, S_SHARE = 1 + 12 + 4 + 2, 1 + 12 + 4
    x_in = lambda b: [(P, core.X[:, k, b, PRE:S1]) for k in range(KD)]

    with core.nc.Block() as block:
        @block.sync
        def _(e):
            d = core.dram
            load_weights(e, core, 1, [(0, d["L0_xattn_Wq2"]), (2048, d["L0_xattn_Wk2"]), (4096, d["L0_xattn_Wv2"]),
                                      (6144, d["L0_xattn_Wo2"])])

        @block.tensor
        def _(e):
            V, S = Count(), Count()
            e.wait_ge(core.const_ready, CONSTS)
            e.wait_ge(core.loaded, LOADS)
            e.wait_ge(core.w_loaded[0], core.w_count[0])
            with e.Fori(0, B) as b:
                V.round(b, V_SHARE)
                S.round(b, S_SHARE)
                norm_pe(e, core, nm, ln, V, S, b, x_in(b), core.mean_d, squared, T)
                e.wait_ge(nm.ready, b + 1)
                for w in (wq, wk):
                    for m in range(8):
                        lane, free, full, c = ((core.lane_v, ln.v_free, ln.v_full, V), (core.lane_s, ln.s_free, ln.s_full, S))[m % 2]
                        e.wait_ge(free, c())
                        for k in range(KD):
                            mm = e.matmul(lane, w[:, k, m * P:(m + 1) * P], normed[:, k, :], start=(k == 0), stop=(k == KD - 1))
                        mm.then_inc(full, 1)
                        c.add()
                for t in range(4):
                    for half in range(2):
                        lane, free, full, c = ((core.lane_v, ln.v_free, ln.v_full, V), (core.lane_s, ln.s_free, ln.s_full, S))[half]
                        e.wait_ge(free, c())
                        for k in range(KD):
                            mm = e.matmul(lane, normed[:, k, t * P:(t + 1) * P], wv[:, k, half * 512:half * 512 + 512],
                                          start=(k == 0), stop=(k == KD - 1))
                        mm.then_inc(full, 1)
                        c.add()
                e.wait_ge(ln.v_free, V())
                e.wait_ge(ln.s_free, S())
                for h in range(H0 + 1):
                    if h < H0:
                        r = DH0 * (h % 2)
                        for u in range(UNITS):
                            n = b * (H0 * UNITS) + (h * UNITS + u)
                            if h > 0:
                                e.wait_ge(exp_done, n - 1)
                            for j in range(2):
                                t = 2 * u + j
                                mm = e.matmul(core.banks[:, t, :], q[r:r + DH0, h // 2, t * P:(t + 1) * P],
                                              k_[r:r + DH0, h // 2, :], start=True, stop=True)
                            mm.then_inc(s_full, 1)
                    if h > 0:
                        g = h - 1
                        for t in range(4):
                            e.wait_ge(p_ready, b * (H0 * UNITS) + (g * UNITS + t // 2 + 1))
                            e.wait_ge((tv_free, ts_free)[t % 2], b * (2 * H0) + (2 * g + t // 2))
                            for kt in range(4):
                                mm = e.transpose(core.banks[:, 4 + t % 2, kt * P:(kt + 1) * P],
                                                 probs[:, 2 * (g % 2) + t // 2, t % 2, kt * P:(kt + 1) * P], core.ident[:])
                            mm.then_inc(t_full, 1)
                        e.wait_ge(tv_free, b * (2 * H0) + 2 * (g + 1))
                        e.wait_ge(ts_free, b * (2 * H0) + 2 * (g + 1))
                        lane, free, full, c = ((core.lane_v, ln.v_free, ln.v_full, V), (core.lane_s, ln.s_free, ln.s_full, S))[g // 2 % 2]
                        if g % 2 == 0:
                            e.wait_ge(free, c())
                        r = DH0 * (g % 2)
                        for kt in range(4):
                            mm = e.matmul(lane[r:r + DH0, :], v_[:, kt, g * DH0:(g + 1) * DH0], probsT[:, g % 2, kt, :],
                                          start=(kt == 0), stop=(kt == 3))
                        if g % 2 == 1:
                            mm.then_inc(full, 1)
                            c.add()
                e.wait_ge(ln.v_free, V())
                e.wait_ge(ln.s_free, S())
                for m in range(KD):
                    e.wait_ge(ln.v_free, V())
                    for k in range(8):
                        mm = e.matmul(core.lane_v, wo[:, k, m * P:(m + 1) * P], q[:, k, :], start=(k == 0), stop=(k == 7))
                    mm.then_inc(ln.v_full, 1)
                    V.add()

        @block.vector
        def _(e):
            V, S = Count(), Count()
            e.wait_ge(core.loaded, LOADS)
            with e.Fori(0, B) as b:
                V.round(b, V_SHARE)
                S.round(b, S_SHARE)
                norm_dve(e, core, nm, ln, V, S, b, x_in(b), centred, std, normed, "g1", T)
                for w in range(2):
                    for m in range(0, 8, 2):
                        e.wait_ge(ln.v_full, V(1))
                        if w == 0:
                            e.tensor_scalar(q[:, m, :], core.lane_v, DH0 ** -0.5, None, ALU.mult).then_inc(ln.v_free, 1)
                        else:
                            e.tensor_copy(k_[:, m, :], core.lane_v).then_inc(ln.v_free, 1)
                        V.add()
                for t in range(4):
                    e.wait_ge(ln.v_full, V(1))
                    e.tensor_copy(v_[:, t, 0:512], core.lane_v).then_inc(ln.v_free, 1)
                    V.add()
                for h in range(H0 + 1):
                    if h < H0:
                        for u in range(UNITS):
                            n = b * (H0 * UNITS) + (h * UNITS + u)
                            e.wait_ge(s_full, n + 1)
                            e.tensor_reduce(nmax[:, 2 * (h % 2) + u, :], core.banks[:, 2 * u:2 * u + 2, :], AX.X, ALU.max,
                                            negate=True).then_inc(nmax_ready, 1)
                    if h > 0:
                        g = h - 1
                        for t in (0, 2):
                            e.wait_ge(t_full, b * (4 * H0) + (4 * g + t + 1))
                            e.tensor_copy(probsT[:, g % 2, :, t * P:(t + 1) * P],
                                          core.banks[:, 4, :].rearrange("p (k q) -> p k q", k=4)).then_inc(tv_free, 1)
                    if h < H0:
                        for u in range(UNITS):
                            n = b * (H0 * UNITS) + (h * UNITS + u)
                            slot = 2 * (h % 2) + u
                            e.wait_ge(exp_done, n + 1)
                            e.reciprocal(rsum[:, slot, :], sums[:, slot, :]).then_inc(rsum_ready, 1)
                            e.wait_ge(rsum_ready, n + 1)
                            for j in range(2):
                                last = e.tensor_scalar(probs[:, slot, j, :], probs[:, slot, j, :], rsum[:, slot, j:j + 1],
                                                       None, ALU.mult)
                            last.then_inc(p_ready, 1)
                    if h > 0 and g % 4 == 1:
                        e.wait_ge(ln.v_full, V(1))
                        e.tensor_copy(q[:, g // 2, :], core.lane_v).then_inc(ln.v_free, 1)
                        V.add()
                for m in range(KD):
                    e.wait_ge(ln.v_full, V(1))
                    x = core.X[:, m, b, PRE:S1]
                    e.scalar_tensor_tensor(out=x, in0=core.lane_v, scalar=core.v("bo1", m), in1=x,
                                           op0=ALU.add, op1=ALU.add).then_inc(ln.v_free, 1)
                    V.add()

        @block.scalar
        def _(e):
            V, S = Count(), Count()
            e.wait_ge(core.loaded, LOADS)
            e.wait_ge(core.const_ready, CONSTS)
            with e.Fori(0, B) as b:
                V.round(b, V_SHARE)
                S.round(b, S_SHARE)
                norm_act(e, core, nm, ln, V, S, b, [P] * KD, centred, squared, std, normed, "be1", T)
                for w in range(2):
                    for m in range(1, 8, 2):
                        e.wait_ge(ln.s_full, S(1))
                        e.activation((q, k_)[w][:, m, :], core.lane_s, ACT.Copy, scale=(DH0 ** -0.5, 1.0)[w]).then_inc(ln.s_free, 1)
                        S.add()
                for t in range(4):
                    e.wait_ge(ln.s_full, S(1))
                    e.activation(v_[:, t, 512:1024], core.lane_s, ACT.Copy).then_inc(ln.s_free, 1)
                    S.add()
                for h in range(H0 + 1):
                    for u in range(UNITS):
                        if h < H0:
                            n = b * (H0 * UNITS) + (h * UNITS + u)
                            slot = 2 * (h % 2) + u
                            e.wait_ge(nmax_ready, n + 1)
                            for j in range(2):
                                last = e.activation(probs[:, slot, j, :], core.banks[:, 2 * u + j, :], ACT.Exp,
                                                    bias=nmax[:, slot, j:j + 1], accum_out=sums[:, slot, j:j + 1])
                            last.then_inc(exp_done, 1)
                        if h > 0:
                            g, t = h - 1, 2 * u + 1
                            e.wait_ge(t_full, b * (4 * H0) + (4 * g + t + 1))
                            e.activation(probsT[:, g % 2, :, t * P:(t + 1) * P],
                                         core.banks[:, 5, :].rearrange("p (k q) -> p k q", k=4), ACT.Copy).then_inc(ts_free, 1)
                    if h > 0 and g % 4 == 3:
                        e.wait_ge(ln.s_full, S(1))
                        e.activation(q[:, g // 2, :], core.lane_s, ACT.Copy).then_inc(ln.s_free, 1)
                        S.add()

def lanes_of(core, ln, V, S):
    return ((core.lane_v, ln.v_free, ln.v_full, V), (core.lane_s, ln.s_free, ln.s_full, S))


def norm_context(core, nth, g, be, out, squared, std):
    ln, nm = core.context_lanes, core.context_norm
    x = [(r, core.C[0:r, k, :]) for k, r in enumerate(CROWS)]
    N = B * M
    counts = lambda: (Count(nth), Count(nth))
    with core.nc.Block() as block:
        @block.tensor
        def _(e):
            norm_pe(e, core, nm, ln, *counts(), nth, x, core.mean_c, squared, N)

        @block.vector
        def _(e):
            norm_dve(e, core, nm, ln, *counts(), nth, x, out, std, out, g, N)

        @block.scalar
        def _(e):
            norm_act(e, core, nm, ln, *counts(), nth, CROWS, out, squared, std, out, be, N)


def cross_attention(core, name, side, weights, heads, width, norm, bias, ctx_norm, prefetch):
    hpt, inner = P // width, heads * width
    tiles, chunks = inner // P, heads // 2
    per_tile = chunks // tiles
    at = 0
    normed, at = core.area(at, KD, T)
    centred, at = core.area(at, KD, T)
    squared, at = core.area(at, KD, T)
    std, at = core.area(at, T)
    q, at = core.area(at, tiles, T)
    probs, at = core.area(at, 2, heads * M)
    probsT, at = core.area(at, chunks, T)
    kblk, at = core.area(at, tiles, hpt * M)
    vblk, at = core.area(at, chunks, P)
    kmask, at = core.area(at, hpt, M)
    vmask, at = core.area(at, per_tile, P)
    ctx2, at = core.area(at, 2, 2, M)
    rowmax, at = core.area(at, 2, heads)
    rowsum, at = core.area(at, 2, heads)
    if ctx_norm:
        context, at = core.area(at, 2, B * M)
        norm_context(core, 0, ctx_norm[0], ctx_norm[1], context, squared, std)
    else:
        context = core.C
    wq, wk, wv, wo = (wview(core, side, c, r, n) for c, r, n in weights)
    ln, nm = Lanes(core, name), Norm(core, name)
    masks_ready, vmask_ready = core.sem(f"{name}_kmask"), core.sem(f"{name}_vmask")
    ctx_ready = core.sem(f"{name}_ctx_ready")
    s_full = core.sem(f"{name}_scores")
    max_done, shifted = core.sem(f"{name}_max"), core.sem(f"{name}_shifted")
    exp_done = core.sem(f"{name}_exp")
    sum_done, rsum_ready = core.sem(f"{name}_sum"), core.sem(f"{name}_rsum")
    p_ready = core.sem(f"{name}_probs")
    t_full = core.sem(f"{name}_t_full")
    tv_free, ts_free = core.sem(f"{name}_tv_free"), core.sem(f"{name}_ts_free")
    V_GROUPS = inner // 512 if inner > 512 else 1
    v_cols = inner // V_GROUPS
    V_SHARE, S_SHARE = 1 + 1 + V_GROUPS + tiles + 2, 1 + tiles
    QT = T // P
    x_in = lambda b: [(P, core.X[:, k, b, PRE:S1]) for k in range(KD)]

    with core.nc.Block() as block:
        @block.sync
        def _(e):
            prefetch(e)

        @block.gpsimd
        def _(e):
            e.memset(kmask, 1.0).then_inc(masks_ready, 1)
            e.wait_ge(masks_ready, 1)
            e.affine_select(out=kmask, in_=kmask, compare_op=ALU.is_ge, fill=0.0, base=0,
                            pattern=[[-width, hpt], [0, M]], channel_multiplier=1).then_inc(masks_ready, 1)
            e.wait_ge(masks_ready, 2)
            e.affine_select(out=kmask, in_=kmask, compare_op=ALU.is_ge, fill=0.0, base=width - 1,
                            pattern=[[width, hpt], [0, M]], channel_multiplier=-1).then_inc(masks_ready, 1)
            with e.Fori(0, B) as b:
                e.wait_ge(ln.v_free, b * V_SHARE)
                for j in range(2):
                    for k, r in enumerate(CROWS):
                        own = context[0:r, k, bass.ts(b, M)]
                        last = e.tensor_tensor(ctx2[0:r, k, j, :], own, core.one[0:r, 0:1].to_broadcast([r, M]), ALU.mult)
                last.then_inc(ctx_ready, 1)

        @block.tensor
        def _(e):
            V, S = Count(), Count()
            e.wait_ge(core.w_loaded[side], core.w_count[side])
            with e.Fori(0, B) as b:
                V.round(b, V_SHARE)
                S.round(b, S_SHARE)
                lanes = lanes_of(core, ln, V, S)
                norm_pe(e, core, nm, ln, V, S, b, x_in(b), core.mean_d, squared, T)
                e.wait_ge(ctx_ready, b + 1)
                e.wait_ge(ln.v_free, V())
                for m in range(tiles):
                    for k, r in enumerate(CROWS):
                        mm = e.matmul(core.lane_v[:, m * M:(m + 1) * M], wk[0:r, k, m * P:(m + 1) * P],
                                      ctx2[0:r, k, 0, :], start=(k == 0), stop=(k == 1))
                mm.then_inc(ln.v_full, 1)
                V.add()
                for g in range(V_GROUPS):
                    e.wait_ge(ln.v_free, V())
                    for k, r in enumerate(CROWS):
                        mm = e.matmul(core.lane_v[:, 0:v_cols], ctx2[0:r, k, :, :].rearrange("p a m -> p (a m)"),
                                      wv[0:r, k, g * v_cols:(g + 1) * v_cols], start=(k == 0), stop=(k == 1))
                    mm.then_inc(ln.v_full, 1)
                    V.add()
                e.wait_ge(nm.ready, b + 1)
                for m in range(tiles):
                    lane, free, full, c = lanes[m % 2]
                    e.wait_ge(free, c())
                    for k in range(KD):
                        mm = e.matmul(lane, wq[:, k, m * P:(m + 1) * P], normed[:, k, :], start=(k == 0), stop=(k == KD - 1))
                    mm.then_inc(full, 1)
                    c.add()
                e.wait_ge(ln.v_free, V())
                e.wait_ge(ln.s_free, S())
                for i in range(QT + 1):
                    if i < QT:
                        if i >= 2:
                            e.wait_ge(shifted, b * QT + (i - 1))
                        for m in range(tiles):
                            c0 = m * hpt * M
                            mm = e.matmul(core.banks[:, 2 * (i % 2) + c0 // 512, c0 % 512:c0 % 512 + hpt * M],
                                          q[:, m, i * P:(i + 1) * P], kblk[:, m, :], start=True, stop=True)
                        mm.then_inc(s_full, 1)
                    if i > 0:
                        t = i - 1
                        e.wait_ge(p_ready, b * QT + (t + 1))
                        e.wait_ge(tv_free, b * QT + t)
                        e.wait_ge(ts_free, b * QT + t)
                        for c in range(chunks):
                            mm = e.transpose(core.banks[:, 4 + c // 4, c % 4 * P:(c % 4 + 1) * P],
                                             probs[:, t % 2, c * P:(c + 1) * P], core.ident[:])
                        mm.then_inc(t_full, 1)
                e.wait_ge(tv_free, b * QT + QT)
                e.wait_ge(ts_free, b * QT + QT)
                for m in range(tiles):
                    lane, free, full, c = lanes[m % 2]
                    e.wait_ge(free, c())
                    for j in range(per_tile):
                        mm = e.matmul(lane, vblk[:, m * per_tile + j, :], probsT[:, m * per_tile + j, :],
                                      start=(j == 0), stop=(j == per_tile - 1))
                    mm.then_inc(full, 1)
                    c.add()
                e.wait_ge(ln.v_free, V())
                e.wait_ge(ln.s_free, S())
                for m in range(KD):
                    e.wait_ge(ln.v_free, V())
                    for k in range(tiles):
                        mm = e.matmul(core.lane_v, wo[:, k, m * P:(m + 1) * P], q[:, k, :], start=(k == 0), stop=(k == tiles - 1))
                    mm.then_inc(ln.v_full, 1)
                    V.add()

        @block.vector
        def _(e):
            V, S = Count(), Count()
            e.memset(vmask, 0.0).then_inc(vmask_ready, 1)
            e.wait_ge(vmask_ready, 1)
            for h in range(2):
                for c in range(per_tile):
                    f = (2 * c + h) * width
                    last = e.memset(vmask[h * M:(h + 1) * M, c, f:f + width], 1.0)
            last.then_inc(vmask_ready, 1)
            e.wait_ge(vmask_ready, 2)
            e.wait_ge(masks_ready, 3)
            with e.Fori(0, B) as b:
                V.round(b, V_SHARE)
                S.round(b, S_SHARE)
                norm_dve(e, core, nm, ln, V, S, b, x_in(b), centred, std, normed, norm[0], T)
                e.wait_ge(ln.v_full, V(1))
                e.tensor_tensor(kblk.rearrange("p t (h m) -> p t h m", h=hpt),
                                core.lane_v[:, 0:tiles * M].rearrange("p (t m) -> p t m", t=tiles).unsqueeze(2)
                                .to_broadcast([P, tiles, hpt, M]),
                                kmask.unsqueeze(1).to_broadcast([P, tiles, hpt, M]), ALU.mult).then_inc(ln.v_free, 1)
                V.add()
                for g in range(V_GROUPS):
                    gt = v_cols // P
                    shape = [P, gt, per_tile, P]
                    e.wait_ge(ln.v_full, V(1))
                    e.tensor_tensor(vblk[:, g * gt * per_tile:(g + 1) * gt * per_tile, :].rearrange("p (t c) f -> p t c f", t=gt),
                                    core.lane_v[:, 0:v_cols].rearrange("p (t f) -> p t f", t=gt).unsqueeze(2).to_broadcast(shape),
                                    vmask.unsqueeze(1).to_broadcast(shape), ALU.mult).then_inc(ln.v_free, 1)
                    V.add()
                for m in range(0, tiles, 2):
                    e.wait_ge(ln.v_full, V(1))
                    e.tensor_scalar(q[:, m, :], core.lane_v, width ** -0.5, None, ALU.mult).then_inc(ln.v_free, 1)
                    V.add()
                for i in range(QT + 2):
                    if i >= 2:
                        t = i - 2
                        e.wait_ge(t_full, b * QT + (t + 1))
                        e.tensor_copy(probsT[:, 0:4, t * P:(t + 1) * P],
                                      core.banks[:, 4, :].rearrange("p (c q) -> p c q", c=4)).then_inc(tv_free, 1)
                    if i < QT:
                        s = i % 2
                        scores = core.banks[:, 2 * s:2 * s + 2, :].rearrange("p a n -> p (a n)").rearrange("p (h m) -> p h m", h=heads)
                        e.wait_ge(s_full, b * QT + (i + 1))
                        e.tensor_reduce(rowmax[:, s, :], scores, AX.X, ALU.max).then_inc(max_done, 1)
                        e.wait_ge(max_done, b * QT + (i + 1))
                        e.tensor_tensor(probs[:, s, :].rearrange("p (h m) -> p h m", h=heads), scores,
                                        rowmax[:, s, :].unsqueeze(2).to_broadcast([P, heads, M]), ALU.subtract).then_inc(shifted, 1)
                    if 1 <= i <= QT:
                        t = i - 1
                        s = t % 2
                        view = probs[:, s, :].rearrange("p (h m) -> p h m", h=heads)
                        e.wait_ge(exp_done, b * QT + (t + 1))
                        e.tensor_reduce(rowsum[:, s, :], view, AX.X, ALU.add).then_inc(sum_done, 1)
                        e.wait_ge(sum_done, b * QT + (t + 1))
                        e.reciprocal(rowsum[:, s, :], rowsum[:, s, :]).then_inc(rsum_ready, 1)
                        e.wait_ge(rsum_ready, b * QT + (t + 1))
                        e.tensor_tensor(view, view, rowsum[:, s, :].unsqueeze(2).to_broadcast([P, heads, M]), ALU.mult) \
                            .then_inc(p_ready, 1)
                for m in range(0, tiles, 2):
                    e.wait_ge(ln.v_full, V(1))
                    e.tensor_copy(q[:, m, :], core.lane_v).then_inc(ln.v_free, 1)
                    V.add()
                for m in range(KD):
                    e.wait_ge(ln.v_full, V(1))
                    x = core.X[:, m, b, PRE:S1]
                    e.scalar_tensor_tensor(out=x, in0=core.lane_v, scalar=core.v(bias, m), in1=x,
                                           op0=ALU.add, op1=ALU.add).then_inc(ln.v_free, 1)
                    V.add()

        @block.scalar
        def _(e):
            V, S = Count(), Count()
            with e.Fori(0, B) as b:
                V.round(b, V_SHARE)
                S.round(b, S_SHARE)
                norm_act(e, core, nm, ln, V, S, b, [P] * KD, centred, squared, std, normed, norm[1], T)
                for m in range(1, tiles, 2):
                    e.wait_ge(ln.s_full, S(1))
                    e.activation(q[:, m, :], core.lane_s, ACT.Copy, scale=width ** -0.5).then_inc(ln.s_free, 1)
                    S.add()
                for i in range(QT + 2):
                    if i < QT:
                        e.wait_ge(shifted, b * QT + (i + 1))
                        e.activation(probs[:, i % 2, :], probs[:, i % 2, :], ACT.Exp).then_inc(exp_done, 1)
                    if i >= 2:
                        t = i - 2
                        e.wait_ge(t_full, b * QT + (t + 1))
                        e.activation(probsT[:, 4:8, t * P:(t + 1) * P],
                                     core.banks[:, 5, :].rearrange("p (c q) -> p c q", c=4), ACT.Copy).then_inc(ts_free, 1)
                for m in range(1, tiles, 2):
                    e.wait_ge(ln.s_full, S(1))
                    e.activation(q[:, m, :], core.lane_s, ACT.Copy).then_inc(ln.s_free, 1)
                    S.add()


def cross_attention_0(core):
    d = core.dram
    cross_attention(core, "cross0", 1, [(0, 2, INNER), (2048, 2, INNER), (4096, 2, INNER), (6144, 8, D)], H0, DH0,
                    ("g2", "be2"), "bo2", None,
                    lambda e: load_weights(e, core, 0, [(0, d["L0_xattn_Wp"]), (4096, d["L0_xattn_W2"])]))


def feed_forward(core, name, side, w1, w2, norm, b1, b2, gated, prefetch):
    at = 0
    normed, at = core.area(at, KD, T)
    centred, at = core.area(at, KD, T)
    squared, at = core.area(at, KD, T)
    std, at = core.area(at, T)
    hidden, at = core.area(at, 8, T)
    gate, at = core.area(at, 2, T)
    ln, nm = Lanes(core, name), Norm(core, name)
    gelu_done = core.sem(f"{name}_gelu")
    V_SHARE, S_SHARE = (1 + 8 + 2, 1 + 8) if gated else (1 + 4 + 2, 1 + 4)
    x_in = lambda b: [(P, core.X[:, k, b, PRE:S1]) for k in range(KD)]
    if gated:
        groups = [g for m in range(8) for g in ((1, 8 + m), (0, m))]
    else:
        groups = [(m % 2, m) for m in range(8)]

    with core.nc.Block() as block:
        @block.sync
        def _(e):
            prefetch(e)

        @block.tensor
        def _(e):
            V, S = Count(), Count()
            e.wait_ge(core.w_loaded[side], core.w_count[side])
            with e.Fori(0, B) as b:
                V.round(b, V_SHARE)
                S.round(b, S_SHARE)
                lanes = lanes_of(core, ln, V, S)
                norm_pe(e, core, nm, ln, V, S, b, x_in(b), core.mean_d, squared, T)
                e.wait_ge(nm.ready, b + 1)
                for which, m in groups:
                    lane, free, full, c = lanes[which]
                    e.wait_ge(free, c())
                    for k in range(KD):
                        mm = e.matmul(lane, w1[:, k, m * P:(m + 1) * P], normed[:, k, :], start=(k == 0), stop=(k == KD - 1))
                    mm.then_inc(full, 1)
                    c.add()
                e.wait_ge(ln.v_free, V())
                e.wait_ge(ln.s_free, S())
                if not gated:
                    e.wait_ge(gelu_done, 4 * b + 4)
                for m in range(KD):
                    e.wait_ge(ln.v_free, V())
                    for k in range(8):
                        mm = e.matmul(core.lane_v, w2[:, k, m * P:(m + 1) * P], hidden[:, k, :], start=(k == 0), stop=(k == 7))
                    mm.then_inc(ln.v_full, 1)
                    V.add()

        @block.vector
        def _(e):
            V, S = Count(), Count()
            with e.Fori(0, B) as b:
                V.round(b, V_SHARE)
                S.round(b, S_SHARE)
                norm_dve(e, core, nm, ln, V, S, b, x_in(b), centred, std, normed, norm[0], T)
                for which, m in groups:
                    if which == 1:
                        S.add()
                        continue
                    e.wait_ge(ln.v_full, V(1))
                    if gated:
                        e.wait_ge(ln.s_free, S())
                        e.scalar_tensor_tensor(out=hidden[:, m, :], in0=core.lane_v, scalar=core.v(b1, m), in1=gate[:, m % 2, :],
                                               op0=ALU.add, op1=ALU.mult).then_inc(ln.v_free, 1)
                    else:
                        e.tensor_scalar(hidden[:, m, :], core.lane_v, core.v(b1, m), None, ALU.add).then_inc(ln.v_free, 1)
                    V.add()
                for m in range(KD):
                    e.wait_ge(ln.v_full, V(1))
                    x = core.X[:, m, b, PRE:S1]
                    e.scalar_tensor_tensor(out=x, in0=core.lane_v, scalar=core.v(b2, m), in1=x,
                                           op0=ALU.add, op1=ALU.add).then_inc(ln.v_free, 1)
                    V.add()

        @block.scalar
        def _(e):
            V, S = Count(), Count()
            with e.Fori(0, B) as b:
                V.round(b, V_SHARE)
                S.round(b, S_SHARE)
                norm_act(e, core, nm, ln, V, S, b, [P] * KD, centred, squared, std, normed, norm[1], T)
                for which, m in groups:
                    if which == 1:
                        e.wait_ge(ln.s_full, S(1))
                        if gated:
                            if m - 8 >= 2:
                                e.wait_ge(ln.v_free, V(-1))
                            to = gate[:, m % 2, :]
                        else:
                            to = hidden[:, m, :]
                        e.activation(to, core.lane_s, ACT.Gelu, bias=core.v(b1, m)).then_inc(ln.s_free, 1)
                        S.add()
                    else:
                        V.add()
                        if not gated:
                            e.wait_ge(ln.v_free, V())
                            e.activation(hidden[:, m, :], hidden[:, m, :], ACT.Gelu).then_inc(gelu_done, 1)


def feed_forward_0(core):
    d = core.dram
    feed_forward(core, "ff0", 0, wview(core, 0, 0, 2, 2048), wview(core, 0, 4096, 8, D), ("g3", "be3"), "bp", "b2_0", True,
                 lambda e: load_mamba(e, core, 0))


def cross_attention_2(core):
    cross_attention(core, "cross2", 0, [(0, 2, D), (512, 2, D), (1024, 2, D), (1536, 2, D)], 16, 16,
                    ("l1w", "l1b"), "bproj", ("l2w", "l2b"), lambda e: load_last(e, core))


def feed_forward_2(core):
    feed_forward(core, "ff2", 0, wview(core, 0, 2048, 2, HID), wview(core, 0, 4096, 8, D), ("l3w", "l3b"), "b1", "b2_2", False,
                 lambda e: None)


def load_second(e, core):
    d = core.dram
    kv = d["L2_xattn_Wkv"]
    load_weights(e, core, 0, [(0, d["L2_xattn_Wq"]), (512, kv[:, 0:D]), (1024, kv[:, D:2 * D]), (1536, d["L2_xattn_Wproj"]),
                              (2048, d["L2_xattn_W1"]), (4096, d["L2_xattn_W2"])])


def load_last(e, core):
    d = core.dram
    load_weights(e, core, 1, [(0, d["L3_Wq"]), (512, d["L3_Wk"]), (1024, d["L3_Wv"]), (1536, d["L3_Wd"])])


def last_attention(core):
    at = 0
    normed, at = core.area(at, KD, T)
    centred, at = core.area(at, KD, T)
    squared, at = core.area(at, KD, T)
    std, at = core.area(at, T)
    context, at = core.area(at, 2, B * M)
    q, at = core.area(at, KD, T)
    kT, at = core.area(at, KD, M)
    v_, at = core.area(at, D)
    ctx1, at = core.area(at, 2, M)
    probs, at = core.area(at, 4, M)
    probsT, at = core.area(at, T)
    mixed, at = core.area(at, KD, T)
    rowmax, at = core.area(at, 4)
    rowsum, at = core.area(at, 4)
    name = "last"
    norm_context(core, 1, "gkv", "bekv", context, squared, std)
    wq, wk, wv, wd = (wview(core, 1, 512 * j, 2, D) for j in range(4))
    ln, nm = Lanes(core, name), Norm(core, name)
    ctx_ready = core.sem(f"{name}_ctx_ready")
    s_full = core.sem(f"{name}_scores")
    max_done, shifted = core.sem(f"{name}_max"), core.sem(f"{name}_shifted")
    exp_done = core.sem(f"{name}_exp")
    sum_done, rsum_ready, p_ready = core.sem(f"{name}_sum"), core.sem(f"{name}_rsum"), core.sem(f"{name}_probs")
    t_full, t_free = core.sem(f"{name}_t_full"), core.sem(f"{name}_t_free")
    V_SHARE, S_SHARE = 1 + 2 + 1 + 1 + 2, 1 + 1 + 1
    x_in = lambda b: [(P, core.X[:, k, b, PRE:S1]) for k in range(KD)]
    QT = T // P

    with core.nc.Block() as block:
        @block.gpsimd
        def _(e):
            with e.Fori(0, B) as b:
                e.wait_ge(ln.v_free, b * V_SHARE)
                for k, r in enumerate(CROWS):
                    own = context[0:r, k, bass.ts(b, M)]
                    last = e.tensor_tensor(ctx1[0:r, k, :], own, core.one[0:r, 0:1].to_broadcast([r, M]), ALU.mult)
                last.then_inc(ctx_ready, 1)

        @block.tensor
        def _(e):
            V, S = Count(), Count()
            e.wait_ge(core.w_loaded[1], core.w_count[1])
            with e.Fori(0, B) as b:
                V.round(b, V_SHARE)
                S.round(b, S_SHARE)
                lanes = lanes_of(core, ln, V, S)
                norm_pe(e, core, nm, ln, V, S, b, x_in(b), core.mean_d, squared, T)
                e.wait_ge(ctx_ready, b + 1)
                e.wait_ge(ln.v_free, V())
                for m in range(KD):
                    for k, r in enumerate(CROWS):
                        mm = e.matmul(core.lane_v[:, m * M:(m + 1) * M], wk[0:r, k, m * P:(m + 1) * P], ctx1[0:r, k, :],
                                      start=(k == 0), stop=(k == 1))
                mm.then_inc(ln.v_full, 1)
                V.add()
                e.wait_ge(ln.v_free, V())
                for k, r in enumerate(CROWS):
                    mm = e.matmul(core.lane_v[0:M, 0:D], ctx1[0:r, k, :], wv[0:r, k, :], start=(k == 0), stop=(k == 1))
                mm.then_inc(ln.v_full, 1)
                V.add()
                e.wait_ge(nm.ready, b + 1)
                for m in range(KD):
                    lane, free, full, c = lanes[m % 2]
                    e.wait_ge(free, c())
                    for k in range(KD):
                        mm = e.matmul(lane, wq[:, k, m * P:(m + 1) * P], normed[:, k, :], start=(k == 0), stop=(k == KD - 1))
                    mm.then_inc(full, 1)
                    c.add()
                e.wait_ge(ln.v_free, V())
                e.wait_ge(ln.s_free, S())
                for t in range(QT):
                    for k in range(KD):
                        mm = e.matmul(core.banks[:, 0, t * M:(t + 1) * M], q[:, k, t * P:(t + 1) * P], kT[:, k, :],
                                      start=(k == 0), stop=(k == KD - 1))
                mm.then_inc(s_full, 1)
                e.wait_ge(p_ready, b + 1)
                for t in range(QT):
                    mm = e.matmul(core.banks[0:M, 4, t * P:(t + 1) * P], probs[:, t, :], core.ident[:], start=True, stop=True)
                mm.then_inc(t_full, 1)
                e.wait_ge(t_free, b + 1)
                for m in range(KD):
                    lane, free, full, c = lanes[m % 2]
                    e.wait_ge(free, c())
                    e.matmul(lane, v_[0:M, m * P:(m + 1) * P], probsT[0:M, :], start=True, stop=True).then_inc(full, 1)
                    c.add()
                e.wait_ge(ln.v_free, V())
                e.wait_ge(ln.s_free, S())
                for m in range(KD):
                    e.wait_ge(ln.v_free, V())
                    for k in range(KD):
                        mm = e.matmul(core.lane_v, wd[:, k, m * P:(m + 1) * P], mixed[:, k, :], start=(k == 0), stop=(k == KD - 1))
                    mm.then_inc(ln.v_full, 1)
                    V.add()

        @block.vector
        def _(e):
            V, S = Count(), Count()
            with e.Fori(0, B) as b:
                V.round(b, V_SHARE)
                S.round(b, S_SHARE)
                norm_dve(e, core, nm, ln, V, S, b, x_in(b), centred, std, normed, "gq", T)
                e.wait_ge(ln.v_full, V(1))
                for m in range(KD):
                    last = e.tensor_scalar(kT[:, m, :], core.lane_v[:, m * M:(m + 1) * M], core.v("bk", m), None, ALU.add)
                last.then_inc(ln.v_free, 1)
                V.add()
                e.wait_ge(ln.v_full, V(1))
                e.tensor_copy(v_[0:M, :], core.lane_v[0:M, 0:D]).then_inc(ln.v_free, 1)
                V.add()
                e.wait_ge(ln.v_full, V(1))
                e.tensor_scalar(q[:, 0, :], core.lane_v, core.v("bq", 0), None, ALU.add).then_inc(ln.v_free, 1)
                V.add()
                scores = core.banks[:, 0, 0:QT * M].rearrange("p (t m) -> p t m", t=QT)
                e.wait_ge(s_full, b + 1)
                e.tensor_reduce(rowmax, scores, AX.X, ALU.max).then_inc(max_done, 1)
                e.wait_ge(max_done, b + 1)
                e.tensor_tensor(probs, scores, rowmax.unsqueeze(2).to_broadcast([P, QT, M]), ALU.subtract).then_inc(shifted, 1)
                e.wait_ge(exp_done, b + 1)
                e.tensor_reduce(rowsum, probs, AX.X, ALU.add).then_inc(sum_done, 1)
                e.wait_ge(sum_done, b + 1)
                e.reciprocal(rowsum, rowsum).then_inc(rsum_ready, 1)
                e.wait_ge(rsum_ready, b + 1)
                e.tensor_tensor(probs, probs, rowsum.unsqueeze(2).to_broadcast([P, QT, M]), ALU.mult).then_inc(p_ready, 1)
                e.wait_ge(t_full, b + 1)
                e.tensor_copy(probsT[0:M, :], core.banks[0:M, 4, :]).then_inc(t_free, 1)
                e.wait_ge(ln.v_full, V(1))
                e.tensor_scalar(mixed[:, 0, :], core.lane_v, core.v("bv", 0), None, ALU.add).then_inc(ln.v_free, 1)
                V.add()
                for m in range(KD):
                    e.wait_ge(ln.v_full, V(1))
                    x = core.X[:, m, b, PRE:S1]
                    e.scalar_tensor_tensor(out=x, in0=core.lane_v, scalar=core.v("bd", m), in1=x,
                                           op0=ALU.add, op1=ALU.add).then_inc(ln.v_free, 1)
                    V.add()

        @block.scalar
        def _(e):
            V, S = Count(), Count()
            with e.Fori(0, B) as b:
                V.round(b, V_SHARE)
                S.round(b, S_SHARE)
                norm_act(e, core, nm, ln, V, S, b, [P] * KD, centred, squared, std, normed, "beq", T)
                e.wait_ge(ln.s_full, S(1))
                e.activation(q[:, 1, :], core.lane_s, ACT.Identity, bias=core.v("bq", 1)).then_inc(ln.s_free, 1)
                S.add()
                e.wait_ge(shifted, b + 1)
                e.activation(probs, probs, ACT.Exp).then_inc(exp_done, 1)
                e.wait_ge(ln.s_full, S(1))
                e.activation(mixed[:, 1, :], core.lane_s, ACT.Identity, bias=core.v("bv", 1)).then_inc(ln.s_free, 1)
                S.add()


CHUNKS = B * NCH
STEPS = LAYERS * CHUNKS
BODY = 12
SET = BODY // 2
UN, US = 16, 4
CREDIT = UN
LW = {"norm": (0, 2), "conv_b": (2, 4), "conv_w": (6, 16), "dt_b": (22, 4), "D": (26, 4), "A_log": (30, 64)}
NLW = 94
W_LOADS = 5
FAR = 1e25
A_MAX = -1e-22
MW = (0, 2048, 2240, 2752, 3776)


def load_layer(e, core, side, layer, sem):
    d, w = core.dram, core.weights[1]
    o = [4096 * side + c for c in MW]
    view = lambda c, k, n: w[:, c:c + k * n].rearrange("p (k n) -> p k n", k=k)
    one = lambda a: a[bass.ds(layer, 1)].rearrange("l r n -> (l r) n")
    tiles = lambda a: one(a).rearrange("(k p) n -> p k n", p=P)
    e.dma_start(view(o[0], KD, 2 * DI), tiles(d["in_w"])).then_inc(sem, 16)
    e.dma_start(view(o[1], KI, 48), tiles(d["x_w"])).then_inc(sem, 16)
    e.dma_start(w[0:DTR, o[2]:o[2] + DI], one(d["dt_w"])).then_inc(sem, 16)
    e.dma_start(view(o[3], KI, D), tiles(d["out_w"])).then_inc(sem, 16)
    e.dma_start(w[:, o[4]:o[4] + NLW], one(d["layer_vec"])).then_inc(sem, 16)


def load_mamba(e, core, _):
    core.side_loaded = [core.sem("side0_loaded"), core.sem("side1_loaded")]
    for side in range(2):
        load_layer(e, core, side, 0, core.side_loaded[side])


def prepend(core):
    w1, w2 = wview(core, 0, 6144, 2, D), wview(core, 0, 6656, 2, D)
    hidden, _ = core.area(0, KD, B * M)
    ln = Lanes(core, "pre")
    with core.nc.Block() as block:
        @block.sync
        def _(e):
            load_weights(e, core, 0, [(6144, core.dram["L1_xattn_pre_w1"]), (6656, core.dram["L1_xattn_pre_w2"])])

        @block.tensor
        def _(e):
            e.wait_ge(core.w_loaded[0], core.w_count[0])
            for m in range(KD):
                e.wait_ge(ln.s_free, m)
                for k, r in enumerate(CROWS):
                    mm = e.matmul(core.lane_s, w1[0:r, k, m * P:(m + 1) * P], core.C[0:r, k, :], start=(k == 0), stop=(k == 1))
                mm.then_inc(ln.s_full, 1)
            e.wait_ge(ln.s_free, KD)
            for m in range(KD):
                e.wait_ge(ln.v_free, m)
                for k in range(KD):
                    mm = e.matmul(core.lane_v, w2[:, k, m * P:(m + 1) * P], hidden[:, k, :], start=(k == 0), stop=(k == KD - 1))
                mm.then_inc(ln.v_full, 1)

        @block.scalar
        def _(e):
            for m in range(KD):
                e.wait_ge(ln.s_full, m + 1)
                e.activation(hidden[:, m, :], core.lane_s, ACT.Silu).then_inc(ln.s_free, 1)

        @block.vector
        def _(e):
            for m in range(KD):
                e.wait_ge(ln.v_full, m + 1)
                e.tensor_copy(core.X[:, m, :, 0:PRE], core.lane_v.rearrange("p (b t) -> p b t", b=B)).then_inc(ln.v_free, 1)


def mamba(core):
    at = 0
    bc, at = core.area(at, 2, 2 * DS, TC)
    x, at = core.area(at, 2, KI, TC)
    z, at = core.area(at, 2, KI, TC)
    u, at = core.area(at, 2, KI, TC)
    dt, at = core.area(at, 2, KI, TC + 1)
    t1, at = core.area(at, KI, TC)
    t2, at = core.area(at, KI, TC)
    t3, at = core.area(at, KI, TC)
    fed, at = core.area(at, 4, US, TC + 1)
    spread = core.weights[0]
    diag = spread[:, 0:4096].rearrange("p (s k j n) -> p s k j n", s=2, k=KI, j=TAPS)
    hc = spread[:, 4096:7168].rearrange("p (q s t) -> p q s t", q=4, s=US)
    raw = spread[:, 7168:7168 + KI * (TC + 3)].rearrange("p (k t) -> p k t", k=KI)
    normed, at = core.area(at, KD, TC)
    squared = t3[:, 0:KD, :]
    ones = core.one[:].unsqueeze(2).to_broadcast([P, KI, TC])
    tail = core.weights[1]
    rstd, xdbl = tail[:, 7966:7966 + TC], None
    xdbl, at = core.area(at, TC)
    state, at = core.area(at, KI, DS)
    decay, at = core.area(at, 2, KI * DS)
    banks = core.banks
    da = [banks[:, 2 * s:2 * s + 2, :].rearrange("p a n -> p (a n)")[:, 0:US * (TC + 1)] for s in range(2)]
    da4 = [a.rearrange("p (s t) -> p s t", s=US) for a in da]
    ybank = [banks[:, 4, 0:TC], banks[:, 5, 0:TC]]
    lane_v2 = core.lane_v[:, 0:2 * TC].rearrange("p (m t) -> p m t", m=2)
    lane_s2 = core.lane_s[:, 0:2 * TC].rearrange("p (m t) -> p m t", m=2)
    w = core.weights[1]
    in_w, x_w, dt_w, out_w, vecs = [], [], [], [], []
    for side in range(2):
        o = [4096 * side + c for c in MW]
        in_w.append(w[:, o[0]:o[0] + 2048].rearrange("p (k n) -> p k n", k=KD))
        x_w.append(w[:, o[1]:o[1] + 192].rearrange("p (k n) -> p k n", k=KI))
        dt_w.append(w[0:DTR, o[2]:o[2] + DI])
        out_w.append(w[:, o[3]:o[3] + 1024].rearrange("p (k n) -> p k n", k=KI))
        vecs.append(w[:, o[4]:o[4] + NLW])
    lv = lambda side, name, j: vecs[side][:, LW[name][0] + j:LW[name][0] + j + 1]

    ln = Lanes(core, "mamba")
    S = lambda name: core.sem(f"mamba_{name}")
    set_up = S("set_up")
    side_ready = S("side_ready")
    a_exp = S("a_exp")
    squared_ready, rstd_ln, rstd_ready, normed_ready = S("squared"), S("rstd_ln"), S("rstd"), S("normed")
    carried = S("carried")
    silu_done = S("silu")
    bc_stored, bc_ready = S("bc_stored"), S("bc_ready")
    soft_abs, soft_exp, soft_ln = S("soft_abs"), S("soft_exp"), S("soft_ln")
    soft_one, soft_masked, soft_rest, soft_sum = S("soft_one"), S("soft_masked"), S("soft_rest"), S("soft_sum")
    dt_ready, u_ready = S("dt_ready"), S("u_ready")
    exp_done, fed_state, fed_ready = S("exp"), S("fed_state"), S("fed")
    scanned, unit_done, summed = S("scanned"), S("unit_done"), S("summed")
    y_full, y_skip, gated = S("y_full"), S("y_skip"), S("gated")
    scratch = core.nc.dram_tensor("mamba_bc", (2, 2 * DS, TC), F32, kind="Internal").ap()

    V_STEP, S_STEP = 5, 6
    v_after = lambda n, k: V_STEP * n + (4 + k)
    s_after = lambda n, k: S_STEP * n + (6 + k)
    unit = lambda n, i: n * UN + i
    at_start = lambda n: isinstance(n, int) and n < 0

    def at_step(l, half, j):
        n = (l * 2 + half) * BODY + j
        return n, j % 2, j // SET, half * 4 + j // NCH, j % NCH

    def following(l, half, j):
        if j < BODY - 1:
            return at_step(l, half, j + 1)[1:]
        return 0, 0, half * -4 + 4, 0

    def preceding(l, half, j):
        if j > 0:
            return at_step(l, half, j - 1)[1:]
        return 1, 1, half * -4 + 7, NCH - 1

    X = lambda b, c: core.X[:, :, b, c * TC:(c + 1) * TC]

    def prepare_pe(e, n, p, side, b, c):
        def mean():
            e.wait_ge(ln.s_free, s_after(n, 0))
            e.wait_ge(squared_ready, n + 2)
            for k in range(KD):
                mm = e.matmul(core.lane_s[:, 0:TC], core.mean_d[:], squared[:, k, :], start=(k == 0), stop=(k == KD - 1))
            mm.then_inc(ln.s_full, 1)

        def project(which, m0, free, full, count, lane):
            def go():
                e.wait_ge(free, count)
                e.wait_ge(normed_ready, n + 2)
                for m in range(2):
                    for k in range(KD):
                        f = which * DI + (m0 + m) * P
                        mm = e.matmul(lane[:, m, :], in_w[side][:, k, f:f + P], normed[:, k, :], start=(k == 0), stop=(k == KD - 1))
                mm.then_inc(full, 1)
            return go

        def convolve(m0):
            def go():
                if m0 == 0:
                    e.wait_ge(ln.v_free, v_after(n, 3))
                e.wait_ge(ln.s_free, s_after(n, 3 + m0 // 2))
                for m in range(2):
                    for j in range(TAPS):
                        mm = e.matmul(lane_s2[:, m, :], diag[:, side, m0 + m, j, :], raw[:, m0 + m, j:j + TC],
                                      start=(j == 0), stop=(j == TAPS - 1))
                mm.then_inc(ln.s_full, 1)
            return go

        def project_x():
            e.wait_ge(silu_done, n + 2)
            e.wait_ge(ln.s_free, s_after(n, 5))
            for k in range(KI):
                mm = e.matmul(core.lane_s[0:48, 0:TC], x_w[side][:, k, :], x[:, p, k, :], start=(k == 0), stop=(k == KI - 1))
            mm.then_inc(ln.s_full, 1)

        def project_dt(m0):
            def go():
                if m0 == 0:
                    e.wait_ge(ln.s_free, s_after(n, 6))
                e.wait_ge(ln.v_free, v_after(n, 3 + m0 // 2))
                for m in range(2):
                    mm = e.matmul(lane_v2[:, m, :], dt_w[side][:, (m0 + m) * P:(m0 + m + 1) * P], xdbl[0:DTR, :], start=True, stop=True)
                mm.then_inc(ln.v_full, 1)
            return go

        return {
            1: [mean],
            3: [project(0, 0, ln.v_free, ln.v_full, v_after(n, 1), lane_v2), project(1, 0, ln.s_free, ln.s_full, s_after(n, 1), lane_s2)],
            4: [project(0, 2, ln.v_free, ln.v_full, v_after(n, 2), lane_v2), project(1, 2, ln.s_free, ln.s_full, s_after(n, 2), lane_s2)],
            6: [convolve(0)], 7: [convolve(2)], 9: [project_x], 10: [project_dt(0)], 11: [project_dt(2)],
        }

    def prepare_act(e, n, p, side, b, c):
        def square():
            e.wait_ge(soft_sum, n + 1)
            e.activation(squared, X(b, c), ACT.Square).then_inc(squared_ready, 1)

        def inverse_root():
            e.wait_ge(ln.s_full, s_after(n, 1))
            e.activation(rstd, core.lane_s[:, 0:TC], ACT.Ln, bias=core.eps[:]).then_inc(ln.s_free, 1)
            e.wait_ge(ln.s_free, s_after(n, 1))
            e.activation(rstd, rstd, ACT.Exp, scale=-0.5).then_inc(rstd_ready, 1)

        def copy_z(m0):
            def go():
                if m0 == 0:
                    e.wait_ge(gated, KI * n + KI)
                e.wait_ge(ln.s_full, s_after(n, 2 + m0 // 2))
                e.activation(z[:, p, m0:m0 + 2, :], lane_s2, ACT.Copy).then_inc(ln.s_free, 1)
            return go

        def copy_x(m0):
            def go():
                e.wait_ge(ln.s_full, s_after(n, 4 + m0 // 2))
                for m in range(2):
                    last = e.activation(x[:, p, m0 + m, :], lane_s2[:, m, :], ACT.Identity, bias=lv(side, "conv_b", m0 + m))
                last.then_inc(ln.s_free, 1)
            return go

        def silu():
            e.wait_ge(ln.s_free, s_after(n, 5))
            e.activation(z[:, p], z[:, p], ACT.Silu)
            e.activation(x[:, p], x[:, p], ACT.Silu).then_inc(silu_done, 1)

        def copy_xdbl():
            e.wait_ge(ln.s_full, s_after(n, 6))
            e.wait_ge(bc_stored, 16 * (n + 1))
            e.activation(xdbl[0:48, :], core.lane_s[0:48, 0:TC], ACT.Copy).then_inc(ln.s_free, 1)

        def softplus():
            e.wait_ge(ln.v_free, v_after(n, 5))
            e.activation(t1, dt[:, p, :, 1:], ACT.Abs).then_inc(soft_abs, 1)
            e.wait_ge(soft_abs, n + 2)
            e.activation(t1, t1, ACT.Exp, scale=-1.0).then_inc(soft_exp, 1)
            e.wait_ge(soft_exp, n + 2)
            e.wait_ge(dt_ready, n + 1)
            e.activation(t2, t1, ACT.Ln, bias=1.0).then_inc(soft_ln, 1)

        return {0: [square], 2: [inverse_root], 3: [copy_z(0)], 4: [copy_z(2)], 6: [copy_x(0)], 7: [copy_x(2), silu],
                9: [copy_xdbl], 12: [softplus]}

    def prepare_dve(e, n, p, side, b, c):
        def scale():
            e.wait_ge(rstd_ready, n + 2)
            for k in range(KD):
                last = e.scalar_tensor_tensor(out=normed[:, k, :], in0=core.X[:, k, b, c * TC:(c + 1) * TC],
                                              scalar=lv(side, "norm", k), in1=rstd, op0=ALU.mult, op1=ALU.mult)
            last.then_inc(normed_ready, 1)

        def carry():
            if not at_start(n):
                e.wait_ge(ln.s_free, s_after(n - 1, 5))
            if c == 0:
                e.memset(raw[:, :, 0:3], 0.0).then_inc(carried, 1)
            else:
                e.tensor_copy(raw[:, :, 0:3], raw[:, :, TC:TC + 3]).then_inc(carried, 1)
            e.wait_ge(carried, n + 2)

        def copy_raw(m0):
            def go():
                e.wait_ge(ln.v_full, v_after(n, 2 + m0 // 2))
                e.tensor_copy(raw[:, m0:m0 + 2, 3:], lane_v2).then_inc(ln.v_free, 1)
            return go

        def bias_dt(m0):
            def go():
                e.wait_ge(ln.v_full, v_after(n, 4 + m0 // 2))
                for m in range(2):
                    last = e.tensor_scalar(dt[:, p, m0 + m, 1:], lane_v2[:, m, :], lv(side, "dt_b", m0 + m), None, ALU.add)
                last.then_inc(ln.v_free, 1)
            return go

        return {2: [scale], 3: [carry, copy_raw(0)], 4: [copy_raw(2)], 10: [bias_dt(0)], 11: [bias_dt(2)],
                14: [lambda: log_where_above_1(e, n)]}

    def finish_dt(e, n, p):
        e.wait_ge(soft_sum, n + 2)
        e.scalar_tensor_tensor(out=dt[:, p, :, 1:], in0=dt[:, p, :, 1:], scalar=0.0, in1=t2, op0=ALU.max, op1=ALU.add).then_inc(dt_ready, 1)
        e.wait_ge(dt_ready, n + 2)
        e.wait_ge(silu_done, n + 2)
        e.tensor_tensor(u[:, p], dt[:, p, :, 1:], x[:, p], ALU.mult).then_inc(u_ready, 1)

    def log_where_above_1(e, n):
        e.wait_ge(soft_one, 2 * n + 4)
        e.wait_ge(soft_ln, n + 2)
        e.scalar_tensor_tensor(out=t2, in0=t3, scalar=0.0, in1=t2, op0=ALU.is_gt, op1=ALU.mult).then_inc(soft_masked, 1)

    def prepare_pool(e, n):
        def one():
            e.wait_ge(soft_exp, n + 2)
            e.tensor_tensor(t3, t1, ones, ALU.add).then_inc(soft_one, 1)
            e.wait_ge(soft_one, 2 * n + 3)
            e.tensor_tensor(t3, t3, ones, ALU.subtract).then_inc(soft_one, 1)

        def rest():
            e.wait_ge(soft_masked, n + 2)
            e.tensor_tensor(t3, t1, t3, ALU.subtract).then_inc(soft_rest, 1)
            e.wait_ge(soft_rest, n + 2)
            e.tensor_tensor(t2, t2, t3, ALU.add).then_inc(soft_sum, 1)

        return {13: [one], 14: [rest]}

    def prepare_sp(e, n, p):
        e.wait_ge(ln.s_free, s_after(n, 6))
        e.wait_ge(bc_ready, 16 * (n + 1))
        e.dma_start(scratch[p], xdbl[DTR:DTR + 2 * DS, :]).then_inc(bc_stored, 16)
        e.wait_ge(bc_stored, 16 * (n + 2))
        if not at_start(n):
            e.wait_ge(unit_done, (n + 1) * CREDIT)
        e.dma_start(bc[:, p], scratch[p].partition_broadcast(P)).then_inc(bc_ready, 16)

    def side_act(e, m, side, loads):
        e.wait_ge(core.side_loaded[side], loads)
        e.wait_ge(side_ready, 2 * m)
        e.activation(decay[:, side, :], vecs[side][:, LW["A_log"][0]:LW["A_log"][0] + KI * DS], ACT.Exp).then_inc(a_exp, 1)

    def side_dve(e, m, side, loads):
        e.wait_ge(core.side_loaded[side], loads)
        for k in range(KI):
            for j in range(TAPS):
                last = e.tensor_scalar(diag[:, side, k, j, :], core.ident[:], lv(side, "conv_w", TAPS * k + j), None, ALU.mult)
        last.then_inc(side_ready, 1)
        e.wait_ge(a_exp, m + 1)
        e.tensor_scalar(decay[:, side, :], decay[:, side, :], -1.0, A_MAX, ALU.mult, ALU.min).then_inc(side_ready, 1)

    def project_out(e, n, p, side):
        e.wait_ge(gated, KI * n + KI)
        e.wait_ge(ln.v_free, v_after(n, 0))
        for m in range(KD):
            for k in range(KI):
                mm = e.matmul(lane_v2[:, m, :], out_w[side][:, k, m * P:(m + 1) * P], x[:, p, k, :], start=(k == 0), stop=(k == KI - 1))
        mm.then_inc(ln.v_full, 1)

    def residual(e, n, b, c):
        e.wait_ge(ln.v_full, v_after(n, 1))
        e.tensor_tensor(X(b, c), X(b, c), lane_v2, ALU.add).then_inc(ln.v_free, 1)

    def all_pieces(pieces):
        for i in sorted(pieces):
            for piece in pieces[i]:
                piece()

    LAST = STEPS - 1
    with core.nc.Block() as block:
        @block.sync
        def _(e):
            prepare_sp(e, -1, 0)
            with e.Fori(0, LAYERS) as l:
                with e.Fori(0, 2) as half:
                    for j in range(BODY):
                        n = at_step(l, half, j)[0]
                        p = following(l, half, j)[0]
                        if j % SET == 1:
                            e.wait_ge(ln.v_free, v_after(n - 1, 1))
                        prepare_sp(e, n, p)
                        if j == 1:
                            load_layer(e, core, 1, l, core.side_loaded[1])
                        if j == SET + 1:
                            load_layer(e, core, 0, (l + half) % LAYERS, core.side_loaded[0])
            e.wait_ge(bc_ready, 16 * (STEPS + 1))
            for side in range(2):
                e.wait_ge(core.side_loaded[side], (2 * LAYERS + 1) * 16 * W_LOADS)

        @block.tensor
        def _(e):
            e.wait_ge(side_ready, 2)
            all_pieces(prepare_pe(e, -1, 0, 0, 0, 0))
            with e.Fori(0, LAYERS) as l:
                with e.Fori(0, 2) as half:
                    for j in range(BODY):
                        n, p, side, b, c = at_step(l, half, j)
                        pieces = prepare_pe(e, n, *following(l, half, j))
                        for i in range(UN):
                            if i == 1:
                                pp, ps, _, _ = preceding(l, half, j)
                                project_out(e, n, pp, ps)
                                if j % SET == SET - 1:
                                    e.wait_ge(side_ready, 2 * ((l * 2 + half) * 2 + j // SET + 2))
                            for piece in pieces.get(i, []):
                                piece()
                            k, q = i // 4, i % 4
                            if q == 0:
                                e.wait_ge(gated, KI * n + (KI + k - 1))
                            e.wait_ge(unit_done, CREDIT + unit(n, i) + 1)
                            for s in range(US):
                                mm = e.matmul(ybank[k % 2], core.ident[:], hc[:, q, s, :], start=(q == 0 and s == 0),
                                              stop=(q == 3 and s == US - 1))
                            mm.then_inc(summed, 1)
            project_out(e, STEPS, 1, 1)

        @block.vector
        def _(e):
            e.memset(state, 0.0).then_inc(set_up, 1)
            e.memset(x[:, 1], 0.0).then_inc(set_up, 1)
            for p in range(2):
                e.memset(dt[:, p, :, 0:1], FAR).then_inc(set_up, 1)
            scrap = t2[:, 0, :]
            for i in range(CREDIT):
                e.memset(scrap[:, 4 * i:4 * i + 1], 0.0).then_inc(unit_done, 1)
                e.memset(scrap[:, 4 * i + 1:4 * i + 2], 0.0).then_inc(summed, 1)
                if i < KI:
                    e.memset(scrap[:, 4 * i + 2:4 * i + 3], 0.0).then_inc(gated, 1)
            side_dve(e, 0, 0, 16 * W_LOADS)
            all_pieces(prepare_dve(e, -1, 0, 0, 0, 0))
            finish_dt(e, -1, 0)
            with e.Fori(0, LAYERS) as l:
                with e.Fori(0, 2) as half:
                    for j in range(BODY):
                        n, p, side, b, c = at_step(l, half, j)
                        fp, fside, fb, fc = following(l, half, j)
                        pieces = prepare_dve(e, n, fp, fside, fb, fc)

                        def gate(k):
                            e.wait_ge(summed, CREDIT + unit(n, 4 * k + 4))
                            e.scalar_tensor_tensor(out=x[:, p, k, :], in0=x[:, p, k, :], scalar=lv(side, "D", k), in1=ybank[k % 2],
                                                   op0=ALU.mult, op1=ALU.add).then_inc(y_skip, 1)
                            e.wait_ge(y_skip, KI * n + (k + 1))
                            e.tensor_tensor(x[:, p, k, :], x[:, p, k, :], z[:, p, k, :], ALU.mult).then_inc(gated, 1)

                        for i in range(UN):
                            k, q = i // 4, i % 4
                            if i == 1:
                                _, _, pb, pc = preceding(l, half, j)
                                residual(e, n, pb, pc)
                                if j % SET == SET - 1:
                                    m = (l * 2 + half) * 2 + j // SET + 1
                                    side_dve(e, m, fside, (l * 2 + half + 2) * (16 * W_LOADS))
                            for piece in pieces.get(i, []):
                                piece()
                            e.wait_ge(exp_done, unit(n, i) + 1)
                            e.wait_ge(fed_ready, unit(n, i) + 1)
                            e.tensor_tensor_scan(da[i % 2], da[i % 2], fed[:, q].rearrange("p s t -> p (s t)"), 0.0,
                                                 ALU.mult, ALU.add).then_inc(scanned, 1)
                            e.wait_ge(scanned, unit(n, i) + 1)
                            keep = state[:, k, q * US:(q + 1) * US]
                            if c < NCH - 1:
                                e.tensor_copy(keep, da4[i % 2][:, :, TC])
                            else:
                                e.memset(keep, 0.0)
                            e.wait_ge(summed, CREDIT + unit(n, i) - 3)
                            e.tensor_tensor(hc[:, q], da4[i % 2][:, :, 1:], bc[:, p, DS + q * US:DS + (q + 1) * US, :],
                                            ALU.mult).then_inc(unit_done, 1)
                            if i in (5, 9, 13):
                                gate(i // 4 - 1)
                        finish_dt(e, n, fp)
                        gate(3)
            residual(e, STEPS, B - 1, NCH - 1)

        @block.scalar
        def _(e):
            side_act(e, 0, 0, 16 * W_LOADS)
            e.wait_ge(set_up, 4)
            all_pieces(prepare_act(e, -1, 0, 0, 0, 0))
            with e.Fori(0, LAYERS) as l:
                with e.Fori(0, 2) as half:
                    for j in range(BODY):
                        n, p, side, b, c = at_step(l, half, j)
                        fp, fside, fb, fc = following(l, half, j)
                        pieces = prepare_act(e, n, fp, fside, fb, fc)
                        if j % SET == 0:
                            e.wait_ge(side_ready, 2 * ((l * 2 + half) * 2 + j // SET + 1))
                        for i in range(UN):
                            k, q = i // 4, i % 4
                            if i == 0:
                                e.wait_ge(dt_ready, n + 1)
                            e.wait_ge(unit_done, CREDIT + unit(n, i) - 1)
                            for s in range(US):
                                f = k * DS + q * US + s
                                last = e.activation(da4[i % 2][:, s, :], dt[:, p, k, :], ACT.Exp, scale=decay[:, side, f:f + 1])
                            last.then_inc(exp_done, 1)
                            if i == 1 and j % SET == SET - 1:
                                m = (l * 2 + half) * 2 + j // SET + 1
                                side_act(e, m, fside, (l * 2 + half + 2) * (16 * W_LOADS))
                            for piece in pieces.get(i, []):
                                piece()

        @block.gpsimd
        def _(e):
            all_pieces(prepare_pool(e, -1))
            with e.Fori(0, LAYERS) as l:
                with e.Fori(0, 2) as half:
                    for j in range(BODY):
                        n, p, side, b, c = at_step(l, half, j)
                        pieces = prepare_pool(e, n)
                        e.wait_ge(bc_ready, 16 * (n + 1))
                        e.wait_ge(u_ready, n + 1)
                        for i in range(UN):
                            k, q = i // 4, i % 4
                            e.wait_ge(unit_done, CREDIT + unit(n, i) - 3)
                            kept = state[:, k, q * US:(q + 1) * US]
                            e.tensor_tensor(fed[:, q, :, 0], kept, core.one[:, 0:US], ALU.mult)
                            e.tensor_tensor(fed[:, q, :, 1:], u[:, p, k, :].unsqueeze(1).to_broadcast([P, US, TC]),
                                            bc[:, p, q * US:(q + 1) * US, :], ALU.mult).then_inc(fed_ready, 1)
                            for piece in pieces.get(i, []):
                                piece()


def final_norm(core):
    squared, at = core.area(0, KD, T)
    std, at = core.area(at, T)
    s_full, s_free = core.sem("final_s_full"), core.sem("final_s_free")
    squared_ready, inverted = core.sem("final_squared"), core.sem("final_inverted")
    scaled = core.sem("final_scaled")
    with core.nc.Block() as block:
        @block.sync
        def _(e):
            load_second(e, core)

        @block.tensor
        def _(e):
            with e.Fori(0, B) as b:
                e.wait_ge(squared_ready, b + 1)
                e.wait_ge(s_free, b)
                for k in range(KD):
                    mm = e.matmul(core.lane_s, core.mean_d[:], squared[:, k, :], start=(k == 0), stop=(k == KD - 1))
                mm.then_inc(s_full, 1)

        @block.scalar
        def _(e):
            with e.Fori(0, B) as b:
                e.wait_ge(s_full, b)
                e.activation(squared, core.X[:, :, b, PRE:S1], ACT.Square).then_inc(squared_ready, 1)
                e.wait_ge(s_full, b + 1)
                e.wait_ge(scaled, b)
                e.activation(std, core.lane_s, ACT.Sqrt, bias=core.eps[:]).then_inc(s_free, 1)

        @block.vector
        def _(e):
            with e.Fori(0, B) as b:
                e.wait_ge(s_free, b + 1)
                e.reciprocal(std, std).then_inc(inverted, 1)
                e.wait_ge(inverted, b + 1)
                for k in range(KD):
                    x = core.X[:, k, b, PRE:S1]
                    last = e.scalar_tensor_tensor(out=x, in0=x, scalar=core.v("final", k), in1=std, op0=ALU.mult, op1=ALU.mult)
                last.then_inc(scaled, 1)


CONSTS = 6
LOADS = 16 * 5


def start(core):
    d = core.dram
    c_ready = core.const_ready
    with core.nc.Block() as block:
        @block.sync
        def _(e):
            e.dma_start(core.vec[:], d["vec"]).then_inc(core.loaded, 16)
            for k in range(KD):
                e.dma_start(core.X[:, k, :, PRE:S1], d["xT"][k * P:(k + 1) * P]).then_inc(core.loaded, 16)
            load_weights(e, core, 0, [(0, d["L0_xattn_Wq1"]), (2048, d["L0_xattn_Wk1"]), (4096, d["L0_xattn_Wv1"]),
                                      (6144, d["L0_xattn_Wo1"])])
            e.dma_start(core.C[:, 0, :], d["ctxT"][0:P]).then_inc(core.loaded, 16)
            e.dma_start(core.C[0:DC - P, 1, :], d["ctxT"][P:DC]).then_inc(core.loaded, 16)

        @block.gpsimd
        def _(e):
            e.memset(core.mean_d[:], 1.0 / D).then_inc(c_ready, 1)
            e.memset(core.mean_c[:], 1.0 / DC).then_inc(c_ready, 1)
            e.memset(core.eps[:], EPS).then_inc(c_ready, 1)
            e.memset(core.ident[:], 0.0).then_inc(c_ready, 1)
            e.memset(core.one[:], 1.0).then_inc(c_ready, 1)
            e.wait_ge(c_ready, 5)
            e.affine_select(out=core.ident[:], in_=core.ident[:], compare_op=ALU.not_equal, fill=1.0, base=0,
                            pattern=[[-1, P]], channel_multiplier=1).then_inc(c_ready, 1)


def finish(core, out):
    stored = core.sem("stored")
    with core.nc.Block() as block:
        @block.sync
        def _(e):
            for k in range(KD):
                e.dma_start(out[k * P:(k + 1) * P], core.X[:, k, :, PRE:S1]).then_inc(stored, 16)
            e.wait_ge(stored, 16 * KD)


STAGES = [self_attention, cross_attention_0, feed_forward_0, prepend, mamba, final_norm, cross_attention_2, feed_forward_2,
          last_attention]


def build(nc, dram, out):
    with ExitStack() as ctx:
        core = Core(nc, ctx, dram)
        start(core)
        for stage in STAGES:
            stage(core)
        finish(core, out)


def layouts(i):
    import numpy as np

    cols = lambda a, w=P: np.asarray(a).reshape(-1, w).T

    def tall(a):
        return np.concatenate([np.asarray(a), np.zeros(2 * P - DC, np.float32)]).reshape(2, P).T

    g = lambda n: np.asarray(i[n])

    def per_layer(a):
        return a.reshape(LAYERS, -1, P, a.shape[-1]).transpose(0, 2, 1, 3).reshape(LAYERS, P, -1)

    layer_parts = {
        "norm": per_layer(g("L1_xattn_norm_w")[..., None]), "conv_b": per_layer(g("L1_xattn_conv_b")[..., None]),
        "conv_w": per_layer(g("L1_xattn_conv_w")), "dt_b": per_layer(g("L1_xattn_dt_proj_b")[..., None]),
        "D": per_layer(g("L1_xattn_D_param")[..., None]), "A_log": per_layer(g("L1_xattn_A_log")),
    }
    parts = {
        "bo1": cols(g("L0_xattn_bo1")), "bo2": cols(g("L0_xattn_bo2")), "bp": cols(g("L0_xattn_bp")),
        "b2_0": cols(g("L0_xattn_b2")), "g1": cols(g("L0_xattn_g1")), "be1": cols(g("L0_xattn_be1")),
        "g2": cols(g("L0_xattn_g2")), "be2": cols(g("L0_xattn_be2")), "g3": cols(g("L0_xattn_g3")),
        "be3": cols(g("L0_xattn_be3")),
        "final": cols(g("L1_xattn_final_norm_w")), "l1w": cols(g("L2_xattn_ln1_w")), "l1b": cols(g("L2_xattn_ln1_b")),
        "l2w": tall(g("L2_xattn_ln2_w")), "l2b": tall(g("L2_xattn_ln2_b")), "l3w": cols(g("L2_xattn_ln3_w")),
        "l3b": cols(g("L2_xattn_ln3_b")), "bproj": cols(g("L2_xattn_bproj")), "b1": cols(g("L2_xattn_b1")),
        "b2_2": cols(g("L2_xattn_b2")), "bq": cols(g("L3_xattn_bq")), "bk": cols(g("L3_xattn_bk")),
        "bv": cols(g("L3_xattn_bv")), "bd": cols(g("L3_xattn_bd")), "gq": cols(g("L3_xattn_g_q")),
        "beq": cols(g("L3_xattn_be_q")), "gkv": tall(g("L3_xattn_g_kv")), "bekv": tall(g("L3_xattn_be_kv")),
    }
    a = {
        "xT": g("x").transpose(2, 0, 1), "ctxT": g("ctx_768").transpose(2, 0, 1).reshape(DC, B * M),
        "layer_vec": np.concatenate([layer_parts[n] for n in LW], axis=2),
        "vec": np.concatenate([parts[n] for n, _ in VEC_SIZES], axis=1),
        "in_w": g("L1_xattn_in_proj_w").transpose(0, 2, 1), "x_w": g("L1_xattn_x_proj_w").transpose(0, 2, 1),
        "dt_w": g("L1_xattn_dt_proj_w").transpose(0, 2, 1), "out_w": g("L1_xattn_out_proj_w").transpose(0, 2, 1),
        "L3_Wq": g("L3_xattn_Wq").T, "L3_Wk": g("L3_xattn_Wk").T, "L3_Wv": g("L3_xattn_Wv").T, "L3_Wd": g("L3_xattn_Wd").T,
    }
    for n in ["L0_xattn_" + w for w in ("Wq1", "Wk1", "Wv1", "Wo1", "Wq2", "Wk2", "Wv2", "Wo2", "Wp", "W2")] + \
            ["L1_xattn_pre_w1", "L1_xattn_pre_w2"] + ["L2_xattn_" + w for w in ("Wq", "Wkv", "Wproj", "W1", "W2")]:
        a[n] = g(n)
    return {n: np.ascontiguousarray(x) for n, x in a.items()}


def kernel(**inputs):
    import concourse.bacc as bacc
    from concourse.bass_utils import run_bass_kernel_spmd

    nc = bacc.Bacc("TRN2", target_bir_lowering=False, num_devices=1)
    arrays = layouts(inputs)
    dram = {n: nc.dram_tensor(f"in_{n}", a.shape, F32, kind="ExternalInput").ap() for n, a in arrays.items()}
    out = nc.dram_tensor("out_T", (D, B, T), F32, kind="ExternalOutput").ap()
    build(nc, dram, out)
    r = run_bass_kernel_spmd(nc, [{f"in_{n}": a for n, a in arrays.items()}], core_ids=[0])
    return r.results[0]["out_T"].transpose(1, 2, 0)
```

```python
from contextlib import ExitStack

import concourse.bass as bass
from concourse import mybir

F32 = mybir.dt.float32
ALU = mybir.AluOpType
ACT = mybir.ActivationFunctionType
AX = mybir.AxisListType

P = 128
B, T, D, DC = 8, 512, 256, 192
PRE, S1 = 64, 576
KD = D // P
M = 64
H0, DH0 = 16, 64
INNER = H0 * DH0
HID = 4 * D
LAYERS, DI, DS, DTR, TAPS = 4, 512, 16, 16, 4
KI = DI // P
EPS = 1e-5
TC = 192
NCH = S1 // TC
CROWS = (P, DC - P)

VEC_SIZES = [
    ("bo1", 2), ("bo2", 2), ("bp", 16), ("b2_0", 2), ("g1", 2), ("be1", 2), ("g2", 2), ("be2", 2), ("g3", 2), ("be3", 2),
    ("final", 2),
    ("l1w", 2), ("l1b", 2), ("l2w", 2), ("l2b", 2), ("l3w", 2), ("l3b", 2), ("bproj", 2), ("b1", 8), ("b2_2", 2),
    ("bq", 2), ("bk", 2), ("bv", 2), ("bd", 2), ("gq", 2), ("beq", 2), ("gkv", 2), ("bekv", 2),
]
VEC = {}
_at = 0
for _n, _c in VEC_SIZES:
    VEC[_n] = (_at, _c)
    _at += _c
NVEC = _at


class Count:

    def __init__(self, n=0):
        self.before, self.n = 0, n

    def __call__(self, ahead=0):
        return self.before + (self.n + ahead)

    def add(self, k=1):
        self.n += k

    def round(self, i, share, start=0):
        self.before, self.n = i * share + start, 0


class Core:

    def __init__(self, nc, ctx, dram):
        self.nc, self.ctx, self.dram = nc, ctx, dram
        sb = lambda name, shape: ctx.enter_context(nc.sbuf_tensor(name, shape, F32))
        self.X = sb("X", [P, KD, B, S1])
        self.C = sb("C", [P, 2, B * M])
        self.vec = sb("vec", [P, NVEC])
        self.ident = sb("ident", [P, P])
        self.mean_d = sb("mean_d", [P, P])
        self.mean_c = sb("mean_c", [P, P])
        self.weights = [sb("weights0", [P, 8192]), sb("weights1", [P, 8192])]
        self.work = sb("work", [P, 25728])
        self.banks = ctx.enter_context(nc.psum_tensor("banks", [P, 8, 512], F32))
        self.lane_v, self.lane_s = self.banks[:, 6, :], self.banks[:, 7, :]
        self.eps = sb("eps", [P, 1])
        self.one = sb("one", [P, KI])
        self.const_ready = self.sem("const_ready")
        self.loaded = self.sem("loaded")
        self.w_loaded = [self.sem("w0_loaded"), self.sem("w1_loaded")]
        self.context_lanes, self.context_norm = Lanes(self, "context"), Norm(self, "context")
        self.w_count = [0, 0]

    def sem(self, name):
        return self.ctx.enter_context(self.nc.semaphore(name))

    def v(self, name, j=0, n=1):
        at = VEC[name][0] + j
        return self.vec[:, at:at + n]

    def area(self, at, *shape):
        n = 1
        for s in shape:
            n *= s
        names = "abcd"[:len(shape)]
        view = self.work[:, at:at + n]
        if len(shape) > 1:
            view = view.rearrange(f"p ({' '.join(names)}) -> p {' '.join(names)}", **dict(zip(names[1:], shape[1:])))
        return view, at + n


def wview(core, side, at, rows, n):
    return core.weights[side][:, at:at + rows * n].rearrange("p (k n) -> p k n", k=rows)


class Lanes:

    def __init__(self, core, stage):
        self.v_full, self.v_free = core.sem(f"{stage}_v_full"), core.sem(f"{stage}_v_free")
        self.s_full, self.s_free = core.sem(f"{stage}_s_full"), core.sem(f"{stage}_s_free")


class Norm:

    def __init__(self, core, stage):
        self.squared = core.sem(f"{stage}_squared")
        self.rstd = core.sem(f"{stage}_rstd")
        self.scaled = core.sem(f"{stage}_scaled")
        self.ready = core.sem(f"{stage}_normed")


def load_weights(e, core, side, parts):
    for at, src in parts:
        rows, cols = src.shape
        full = rows // P
        for k in range(0, full, 4):
            m = min(4, full - k)
            e.dma_start(wview(core, side, at + k * cols, m, cols), src[k * P:(k + m) * P, :].rearrange("(k p) n -> p k n", p=P)) \
                .then_inc(core.w_loaded[side], 16)
            core.w_count[side] += 16
        if rows % P:
            e.dma_start(core.weights[side][0:rows % P, at + full * cols:at + (full + 1) * cols], src[full * P:rows, :]) \
                .then_inc(core.w_loaded[side], 16)
            core.w_count[side] += 16



def norm_pe(e, core, nm, ln, V, S, n, x, mean, squared, N):
    e.wait_ge(ln.v_free, V())
    for k, (r, ap) in enumerate(x):
        mm = e.matmul(core.lane_v[:, 0:N], mean[0:r, :], ap, start=(k == 0), stop=(k == len(x) - 1))
    mm.then_inc(ln.v_full, 1)
    V.add()
    e.wait_ge(ln.s_free, S())
    e.wait_ge(nm.squared, n + 1)
    for k, (r, _) in enumerate(x):
        mm = e.matmul(core.lane_s[:, 0:N], mean[0:r, :], squared[0:r, k, :], start=(k == 0), stop=(k == len(x) - 1))
    mm.then_inc(ln.s_full, 1)
    S.add()


def norm_dve(e, core, nm, ln, V, S, n, x, centred, std, out, g, N):
    e.wait_ge(ln.v_full, V(1))
    for k, (r, ap) in enumerate(x):
        last = e.tensor_tensor(centred[0:r, k, :], ap, core.lane_v[0:r, 0:N], ALU.subtract)
    last.then_inc(ln.v_free, 1)
    V.add()
    S.add()
    e.wait_ge(ln.s_free, S())
    e.reciprocal(std, std).then_inc(nm.rstd, 1)
    e.wait_ge(nm.rstd, n + 1)
    for k, (r, _) in enumerate(x):
        last = e.scalar_tensor_tensor(out=out[0:r, k, :], in0=centred[0:r, k, :], scalar=core.v(g, k)[0:r, :],
                                      in1=std[0:r, :], op0=ALU.mult, op1=ALU.mult)
    last.then_inc(nm.scaled, 1)


def norm_act(e, core, nm, ln, V, S, n, rows, centred, squared, std, out, be, N):
    V.add()
    e.wait_ge(ln.v_free, V())
    for k, r in enumerate(rows):
        last = e.activation(squared[0:r, k, :], centred[0:r, k, :], ACT.Square)
    last.then_inc(nm.squared, 1)
    e.wait_ge(ln.s_full, S(1))
    e.activation(std, core.lane_s[:, 0:N], ACT.Sqrt, bias=core.eps[:]).then_inc(ln.s_free, 1)
    S.add()
    e.wait_ge(nm.scaled, n + 1)
    for k, r in enumerate(rows):
        last = e.activation(out[0:r, k, :], out[0:r, k, :], ACT.Identity, bias=core.v(be, k)[0:r, :])
    last.then_inc(nm.ready, 1)


UNITS = 2


def self_attention(core):
    at = 0
    normed, at = core.area(at, KD, T)
    centred, at = core.area(at, KD, T)
    squared, at = core.area(at, KD, T)
    std, at = core.area(at, T)
    q, at = core.area(at, 8, T)
    k_, at = core.area(at, 8, T)
    v_, at = core.area(at, 4, INNER)
    probs, at = core.area(at, 4, 2, T)
    probsT, at = core.area(at, 2, 4, T)
    nmax, at = core.area(at, 4, 2)
    sums, at = core.area(at, 4, 2)
    rsum, at = core.area(at, 4, 2)
    wq, wk, wv, wo = (wview(core, 0, 2048 * j, 2 if j < 3 else 8, INNER if j < 3 else D) for j in range(4))
    ln, nm = Lanes(core, "self"), Norm(core, "self")
    s_full = core.sem("self_scores")
    nmax_ready = core.sem("self_nmax")
    exp_done = core.sem("self_exp")
    rsum_ready = core.sem("self_rsum")
    p_ready = core.sem("self_probs")
    t_full = core.sem("self_t_full")
    tv_free, ts_free = core.sem("self_tv_free"), core.sem("self_ts_free")
    V_SHARE, S_SHARE = 1 + 12 + 4 + 2, 1 + 12 + 4
    x_in = lambda b: [(P, core.X[:, k, b, PRE:S1]) for k in range(KD)]

    with core.nc.Block() as block:
        @block.sync
        def _(e):
            d = core.dram
            load_weights(e, core, 1, [(0, d["L0_xattn_Wq2"]), (2048, d["L0_xattn_Wk2"]), (4096, d["L0_xattn_Wv2"]),
                                      (6144, d["L0_xattn_Wo2"])])

        @block.tensor
        def _(e):
            V, S = Count(), Count()
            e.wait_ge(core.const_ready, CONSTS)
            e.wait_ge(core.loaded, LOADS)
            e.wait_ge(core.w_loaded[0], core.w_count[0])
            with e.Fori(0, B) as b:
                V.round(b, V_SHARE)
                S.round(b, S_SHARE)
                norm_pe(e, core, nm, ln, V, S, b, x_in(b), core.mean_d, squared, T)
                e.wait_ge(nm.ready, b + 1)
                for w in (wq, wk):
                    for m in range(8):
                        lane, free, full, c = ((core.lane_v, ln.v_free, ln.v_full, V), (core.lane_s, ln.s_free, ln.s_full, S))[m % 2]
                        e.wait_ge(free, c())
                        for k in range(KD):
                            mm = e.matmul(lane, w[:, k, m * P:(m + 1) * P], normed[:, k, :], start=(k == 0), stop=(k == KD - 1))
                        mm.then_inc(full, 1)
                        c.add()
                for t in range(4):
                    for half in range(2):
                        lane, free, full, c = ((core.lane_v, ln.v_free, ln.v_full, V), (core.lane_s, ln.s_free, ln.s_full, S))[half]
                        e.wait_ge(free, c())
                        for k in range(KD):
                            mm = e.matmul(lane, normed[:, k, t * P:(t + 1) * P], wv[:, k, half * 512:half * 512 + 512],
                                          start=(k == 0), stop=(k == KD - 1))
                        mm.then_inc(full, 1)
                        c.add()
                e.wait_ge(ln.v_free, V())
                e.wait_ge(ln.s_free, S())
                for h in range(H0 + 1):
                    if h < H0:
                        r = DH0 * (h % 2)
                        for u in range(UNITS):
                            n = b * (H0 * UNITS) + (h * UNITS + u)
                            if h > 0:
                                e.wait_ge(exp_done, n - 1)
                            for j in range(2):
                                t = 2 * u + j
                                mm = e.matmul(core.banks[:, t, :], q[r:r + DH0, h // 2, t * P:(t + 1) * P],
                                              k_[r:r + DH0, h // 2, :], start=True, stop=True)
                            mm.then_inc(s_full, 1)
                    if h > 0:
                        g = h - 1
                        for t in range(4):
                            e.wait_ge(p_ready, b * (H0 * UNITS) + (g * UNITS + t // 2 + 1))
                            e.wait_ge((tv_free, ts_free)[t % 2], b * (2 * H0) + (2 * g + t // 2))
                            for kt in range(4):
                                mm = e.transpose(core.banks[:, 4 + t % 2, kt * P:(kt + 1) * P],
                                                 probs[:, 2 * (g % 2) + t // 2, t % 2, kt * P:(kt + 1) * P], core.ident[:])
                            mm.then_inc(t_full, 1)
                        e.wait_ge(tv_free, b * (2 * H0) + 2 * (g + 1))
                        e.wait_ge(ts_free, b * (2 * H0) + 2 * (g + 1))
                        lane, free, full, c = ((core.lane_v, ln.v_free, ln.v_full, V), (core.lane_s, ln.s_free, ln.s_full, S))[g // 2 % 2]
                        if g % 2 == 0:
                            e.wait_ge(free, c())
                        r = DH0 * (g % 2)
                        for kt in range(4):
                            mm = e.matmul(lane[r:r + DH0, :], v_[:, kt, g * DH0:(g + 1) * DH0], probsT[:, g % 2, kt, :],
                                          start=(kt == 0), stop=(kt == 3))
                        if g % 2 == 1:
                            mm.then_inc(full, 1)
                            c.add()
                e.wait_ge(ln.v_free, V())
                e.wait_ge(ln.s_free, S())
                for m in range(KD):
                    e.wait_ge(ln.v_free, V())
                    for k in range(8):
                        mm = e.matmul(core.lane_v, wo[:, k, m * P:(m + 1) * P], q[:, k, :], start=(k == 0), stop=(k == 7))
                    mm.then_inc(ln.v_full, 1)
                    V.add()

        @block.vector
        def _(e):
            V, S = Count(), Count()
            e.wait_ge(core.loaded, LOADS)
            with e.Fori(0, B) as b:
                V.round(b, V_SHARE)
                S.round(b, S_SHARE)
                norm_dve(e, core, nm, ln, V, S, b, x_in(b), centred, std, normed, "g1", T)
                for w in range(2):
                    for m in range(0, 8, 2):
                        e.wait_ge(ln.v_full, V(1))
                        if w == 0:
                            e.tensor_scalar(q[:, m, :], core.lane_v, DH0 ** -0.5, None, ALU.mult).then_inc(ln.v_free, 1)
                        else:
                            e.tensor_copy(k_[:, m, :], core.lane_v).then_inc(ln.v_free, 1)
                        V.add()
                for t in range(4):
                    e.wait_ge(ln.v_full, V(1))
                    e.tensor_copy(v_[:, t, 0:512], core.lane_v).then_inc(ln.v_free, 1)
                    V.add()
                for h in range(H0 + 1):
                    if h < H0:
                        for u in range(UNITS):
                            n = b * (H0 * UNITS) + (h * UNITS + u)
                            e.wait_ge(s_full, n + 1)
                            e.tensor_reduce(nmax[:, 2 * (h % 2) + u, :], core.banks[:, 2 * u:2 * u + 2, :], AX.X, ALU.max,
                                            negate=True).then_inc(nmax_ready, 1)
                    if h > 0:
                        g = h - 1
                        for t in (0, 2):
                            e.wait_ge(t_full, b * (4 * H0) + (4 * g + t + 1))
                            e.tensor_copy(probsT[:, g % 2, :, t * P:(t + 1) * P],
                                          core.banks[:, 4, :].rearrange("p (k q) -> p k q", k=4)).then_inc(tv_free, 1)
                    if h < H0:
                        for u in range(UNITS):
                            n = b * (H0 * UNITS) + (h * UNITS + u)
                            slot = 2 * (h % 2) + u
                            e.wait_ge(exp_done, n + 1)
                            e.reciprocal(rsum[:, slot, :], sums[:, slot, :]).then_inc(rsum_ready, 1)
                            e.wait_ge(rsum_ready, n + 1)
                            for j in range(2):
                                last = e.tensor_scalar(probs[:, slot, j, :], probs[:, slot, j, :], rsum[:, slot, j:j + 1],
                                                       None, ALU.mult)
                            last.then_inc(p_ready, 1)
                    if h > 0 and g % 4 == 1:
                        e.wait_ge(ln.v_full, V(1))
                        e.tensor_copy(q[:, g // 2, :], core.lane_v).then_inc(ln.v_free, 1)
                        V.add()
                for m in range(KD):
                    e.wait_ge(ln.v_full, V(1))
                    x = core.X[:, m, b, PRE:S1]
                    e.scalar_tensor_tensor(out=x, in0=core.lane_v, scalar=core.v("bo1", m), in1=x,
                                           op0=ALU.add, op1=ALU.add).then_inc(ln.v_free, 1)
                    V.add()

        @block.scalar
        def _(e):
            V, S = Count(), Count()
            e.wait_ge(core.loaded, LOADS)
            e.wait_ge(core.const_ready, CONSTS)
            with e.Fori(0, B) as b:
                V.round(b, V_SHARE)
                S.round(b, S_SHARE)
                norm_act(e, core, nm, ln, V, S, b, [P] * KD, centred, squared, std, normed, "be1", T)
                for w in range(2):
                    for m in range(1, 8, 2):
                        e.wait_ge(ln.s_full, S(1))
                        e.activation((q, k_)[w][:, m, :], core.lane_s, ACT.Copy, scale=(DH0 ** -0.5, 1.0)[w]).then_inc(ln.s_free, 1)
                        S.add()
                for t in range(4):
                    e.wait_ge(ln.s_full, S(1))
                    e.activation(v_[:, t, 512:1024], core.lane_s, ACT.Copy).then_inc(ln.s_free, 1)
                    S.add()
                for h in range(H0 + 1):
                    for u in range(UNITS):
                        if h < H0:
                            n = b * (H0 * UNITS) + (h * UNITS + u)
                            slot = 2 * (h % 2) + u
                            e.wait_ge(nmax_ready, n + 1)
                            for j in range(2):
                                last = e.activation(probs[:, slot, j, :], core.banks[:, 2 * u + j, :], ACT.Exp,
                                                    bias=nmax[:, slot, j:j + 1], accum_out=sums[:, slot, j:j + 1])
                            last.then_inc(exp_done, 1)
                        if h > 0:
                            g, t = h - 1, 2 * u + 1
                            e.wait_ge(t_full, b * (4 * H0) + (4 * g + t + 1))
                            e.activation(probsT[:, g % 2, :, t * P:(t + 1) * P],
                                         core.banks[:, 5, :].rearrange("p (k q) -> p k q", k=4), ACT.Copy).then_inc(ts_free, 1)
                    if h > 0 and g % 4 == 3:
                        e.wait_ge(ln.s_full, S(1))
                        e.activation(q[:, g // 2, :], core.lane_s, ACT.Copy).then_inc(ln.s_free, 1)
                        S.add()

def lanes_of(core, ln, V, S):
    return ((core.lane_v, ln.v_free, ln.v_full, V), (core.lane_s, ln.s_free, ln.s_full, S))


def norm_context(core, nth, g, be, out, squared, std):
    ln, nm = core.context_lanes, core.context_norm
    x = [(r, core.C[0:r, k, :]) for k, r in enumerate(CROWS)]
    N = B * M
    counts = lambda: (Count(nth), Count(nth))
    with core.nc.Block() as block:
        @block.tensor
        def _(e):
            norm_pe(e, core, nm, ln, *counts(), nth, x, core.mean_c, squared, N)

        @block.vector
        def _(e):
            norm_dve(e, core, nm, ln, *counts(), nth, x, out, std, out, g, N)

        @block.scalar
        def _(e):
            norm_act(e, core, nm, ln, *counts(), nth, CROWS, out, squared, std, out, be, N)


def cross_attention(core, name, side, weights, heads, width, norm, bias, ctx_norm, prefetch):
    hpt, inner = P // width, heads * width
    tiles, chunks = inner // P, heads // 2
    per_tile = chunks // tiles
    at = 0
    normed, at = core.area(at, KD, T)
    centred, at = core.area(at, KD, T)
    squared, at = core.area(at, KD, T)
    std, at = core.area(at, T)
    q, at = core.area(at, tiles, T)
    probs, at = core.area(at, 2, heads * M)
    probsT, at = core.area(at, chunks, T)
    kblk, at = core.area(at, tiles, hpt * M)
    vblk, at = core.area(at, chunks, P)
    kmask, at = core.area(at, hpt, M)
    vmask, at = core.area(at, per_tile, P)
    ctx2, at = core.area(at, 2, 2, M)
    rowmax, at = core.area(at, 2, heads)
    rowsum, at = core.area(at, 2, heads)
    if ctx_norm:
        context, at = core.area(at, 2, B * M)
        norm_context(core, 0, ctx_norm[0], ctx_norm[1], context, squared, std)
    else:
        context = core.C
    wq, wk, wv, wo = (wview(core, side, c, r, n) for c, r, n in weights)
    ln, nm = Lanes(core, name), Norm(core, name)
    masks_ready, vmask_ready = core.sem(f"{name}_kmask"), core.sem(f"{name}_vmask")
    ctx_ready = core.sem(f"{name}_ctx_ready")
    s_full = core.sem(f"{name}_scores")
    max_done, shifted = core.sem(f"{name}_max"), core.sem(f"{name}_shifted")
    exp_done = core.sem(f"{name}_exp")
    sum_done, rsum_ready = core.sem(f"{name}_sum"), core.sem(f"{name}_rsum")
    p_ready = core.sem(f"{name}_probs")
    t_full = core.sem(f"{name}_t_full")
    tv_free, ts_free = core.sem(f"{name}_tv_free"), core.sem(f"{name}_ts_free")
    V_GROUPS = inner // 512 if inner > 512 else 1
    v_cols = inner // V_GROUPS
    V_SHARE, S_SHARE = 1 + 1 + V_GROUPS + tiles + 2, 1 + tiles
    QT = T // P
    x_in = lambda b: [(P, core.X[:, k, b, PRE:S1]) for k in range(KD)]

    with core.nc.Block() as block:
        @block.sync
        def _(e):
            prefetch(e)

        @block.gpsimd
        def _(e):
            e.memset(kmask, 1.0).then_inc(masks_ready, 1)
            e.wait_ge(masks_ready, 1)
            e.affine_select(out=kmask, in_=kmask, compare_op=ALU.is_ge, fill=0.0, base=0,
                            pattern=[[-width, hpt], [0, M]], channel_multiplier=1).then_inc(masks_ready, 1)
            e.wait_ge(masks_ready, 2)
            e.affine_select(out=kmask, in_=kmask, compare_op=ALU.is_ge, fill=0.0, base=width - 1,
                            pattern=[[width, hpt], [0, M]], channel_multiplier=-1).then_inc(masks_ready, 1)
            with e.Fori(0, B) as b:
                e.wait_ge(ln.v_free, b * V_SHARE)
                for j in range(2):
                    for k, r in enumerate(CROWS):
                        own = context[0:r, k, bass.ts(b, M)]
                        last = e.tensor_tensor(ctx2[0:r, k, j, :], own, core.one[0:r, 0:1].to_broadcast([r, M]), ALU.mult)
                last.then_inc(ctx_ready, 1)

        @block.tensor
        def _(e):
            V, S = Count(), Count()
            e.wait_ge(core.w_loaded[side], core.w_count[side])
            with e.Fori(0, B) as b:
                V.round(b, V_SHARE)
                S.round(b, S_SHARE)
                lanes = lanes_of(core, ln, V, S)
                norm_pe(e, core, nm, ln, V, S, b, x_in(b), core.mean_d, squared, T)
                e.wait_ge(ctx_ready, b + 1)
                e.wait_ge(ln.v_free, V())
                for m in range(tiles):
                    for k, r in enumerate(CROWS):
                        mm = e.matmul(core.lane_v[:, m * M:(m + 1) * M], wk[0:r, k, m * P:(m + 1) * P],
                                      ctx2[0:r, k, 0, :], start=(k == 0), stop=(k == 1))
                mm.then_inc(ln.v_full, 1)
                V.add()
                for g in range(V_GROUPS):
                    e.wait_ge(ln.v_free, V())
                    for k, r in enumerate(CROWS):
                        mm = e.matmul(core.lane_v[:, 0:v_cols], ctx2[0:r, k, :, :].rearrange("p a m -> p (a m)"),
                                      wv[0:r, k, g * v_cols:(g + 1) * v_cols], start=(k == 0), stop=(k == 1))
                    mm.then_inc(ln.v_full, 1)
                    V.add()
                e.wait_ge(nm.ready, b + 1)
                for m in range(tiles):
                    lane, free, full, c = lanes[m % 2]
                    e.wait_ge(free, c())
                    for k in range(KD):
                        mm = e.matmul(lane, wq[:, k, m * P:(m + 1) * P], normed[:, k, :], start=(k == 0), stop=(k == KD - 1))
                    mm.then_inc(full, 1)
                    c.add()
                e.wait_ge(ln.v_free, V())
                e.wait_ge(ln.s_free, S())
                for i in range(QT + 1):
                    if i < QT:
                        if i >= 2:
                            e.wait_ge(shifted, b * QT + (i - 1))
                        for m in range(tiles):
                            c0 = m * hpt * M
                            mm = e.matmul(core.banks[:, 2 * (i % 2) + c0 // 512, c0 % 512:c0 % 512 + hpt * M],
                                          q[:, m, i * P:(i + 1) * P], kblk[:, m, :], start=True, stop=True)
                        mm.then_inc(s_full, 1)
                    if i > 0:
                        t = i - 1
                        e.wait_ge(p_ready, b * QT + (t + 1))
                        e.wait_ge(tv_free, b * QT + t)
                        e.wait_ge(ts_free, b * QT + t)
                        for c in range(chunks):
                            mm = e.transpose(core.banks[:, 4 + c // 4, c % 4 * P:(c % 4 + 1) * P],
                                             probs[:, t % 2, c * P:(c + 1) * P], core.ident[:])
                        mm.then_inc(t_full, 1)
                e.wait_ge(tv_free, b * QT + QT)
                e.wait_ge(ts_free, b * QT + QT)
                for m in range(tiles):
                    lane, free, full, c = lanes[m % 2]
                    e.wait_ge(free, c())
                    for j in range(per_tile):
                        mm = e.matmul(lane, vblk[:, m * per_tile + j, :], probsT[:, m * per_tile + j, :],
                                      start=(j == 0), stop=(j == per_tile - 1))
                    mm.then_inc(full, 1)
                    c.add()
                e.wait_ge(ln.v_free, V())
                e.wait_ge(ln.s_free, S())
                for m in range(KD):
                    e.wait_ge(ln.v_free, V())
                    for k in range(tiles):
                        mm = e.matmul(core.lane_v, wo[:, k, m * P:(m + 1) * P], q[:, k, :], start=(k == 0), stop=(k == tiles - 1))
                    mm.then_inc(ln.v_full, 1)
                    V.add()

        @block.vector
        def _(e):
            V, S = Count(), Count()
            e.memset(vmask, 0.0).then_inc(vmask_ready, 1)
            e.wait_ge(vmask_ready, 1)
            for h in range(2):
                for c in range(per_tile):
                    f = (2 * c + h) * width
                    last = e.memset(vmask[h * M:(h + 1) * M, c, f:f + width], 1.0)
            last.then_inc(vmask_ready, 1)
            e.wait_ge(vmask_ready, 2)
            e.wait_ge(masks_ready, 3)
            with e.Fori(0, B) as b:
                V.round(b, V_SHARE)
                S.round(b, S_SHARE)
                norm_dve(e, core, nm, ln, V, S, b, x_in(b), centred, std, normed, norm[0], T)
                e.wait_ge(ln.v_full, V(1))
                e.tensor_tensor(kblk.rearrange("p t (h m) -> p t h m", h=hpt),
                                core.lane_v[:, 0:tiles * M].rearrange("p (t m) -> p t m", t=tiles).unsqueeze(2)
                                .to_broadcast([P, tiles, hpt, M]),
                                kmask.unsqueeze(1).to_broadcast([P, tiles, hpt, M]), ALU.mult).then_inc(ln.v_free, 1)
                V.add()
                for g in range(V_GROUPS):
                    gt = v_cols // P
                    shape = [P, gt, per_tile, P]
                    e.wait_ge(ln.v_full, V(1))
                    e.tensor_tensor(vblk[:, g * gt * per_tile:(g + 1) * gt * per_tile, :].rearrange("p (t c) f -> p t c f", t=gt),
                                    core.lane_v[:, 0:v_cols].rearrange("p (t f) -> p t f", t=gt).unsqueeze(2).to_broadcast(shape),
                                    vmask.unsqueeze(1).to_broadcast(shape), ALU.mult).then_inc(ln.v_free, 1)
                    V.add()
                for m in range(0, tiles, 2):
                    e.wait_ge(ln.v_full, V(1))
                    e.tensor_scalar(q[:, m, :], core.lane_v, width ** -0.5, None, ALU.mult).then_inc(ln.v_free, 1)
                    V.add()
                for i in range(QT + 2):
                    if i >= 2:
                        t = i - 2
                        e.wait_ge(t_full, b * QT + (t + 1))
                        e.tensor_copy(probsT[:, 0:4, t * P:(t + 1) * P],
                                      core.banks[:, 4, :].rearrange("p (c q) -> p c q", c=4)).then_inc(tv_free, 1)
                    if i < QT:
                        s = i % 2
                        scores = core.banks[:, 2 * s:2 * s + 2, :].rearrange("p a n -> p (a n)").rearrange("p (h m) -> p h m", h=heads)
                        e.wait_ge(s_full, b * QT + (i + 1))
                        e.tensor_reduce(rowmax[:, s, :], scores, AX.X, ALU.max).then_inc(max_done, 1)
                        e.wait_ge(max_done, b * QT + (i + 1))
                        e.tensor_tensor(probs[:, s, :].rearrange("p (h m) -> p h m", h=heads), scores,
                                        rowmax[:, s, :].unsqueeze(2).to_broadcast([P, heads, M]), ALU.subtract).then_inc(shifted, 1)
                    if 1 <= i <= QT:
                        t = i - 1
                        s = t % 2
                        view = probs[:, s, :].rearrange("p (h m) -> p h m", h=heads)
                        e.wait_ge(exp_done, b * QT + (t + 1))
                        e.tensor_reduce(rowsum[:, s, :], view, AX.X, ALU.add).then_inc(sum_done, 1)
                        e.wait_ge(sum_done, b * QT + (t + 1))
                        e.reciprocal(rowsum[:, s, :], rowsum[:, s, :]).then_inc(rsum_ready, 1)
                        e.wait_ge(rsum_ready, b * QT + (t + 1))
                        e.tensor_tensor(view, view, rowsum[:, s, :].unsqueeze(2).to_broadcast([P, heads, M]), ALU.mult) \
                            .then_inc(p_ready, 1)
                for m in range(0, tiles, 2):
                    e.wait_ge(ln.v_full, V(1))
                    e.tensor_copy(q[:, m, :], core.lane_v).then_inc(ln.v_free, 1)
                    V.add()
                for m in range(KD):
                    e.wait_ge(ln.v_full, V(1))
                    x = core.X[:, m, b, PRE:S1]
                    e.scalar_tensor_tensor(out=x, in0=core.lane_v, scalar=core.v(bias, m), in1=x,
                                           op0=ALU.add, op1=ALU.add).then_inc(ln.v_free, 1)
                    V.add()

        @block.scalar
        def _(e):
            V, S = Count(), Count()
            with e.Fori(0, B) as b:
                V.round(b, V_SHARE)
                S.round(b, S_SHARE)
                norm_act(e, core, nm, ln, V, S, b, [P] * KD, centred, squared, std, normed, norm[1], T)
                for m in range(1, tiles, 2):
                    e.wait_ge(ln.s_full, S(1))
                    e.activation(q[:, m, :], core.lane_s, ACT.Copy, scale=width ** -0.5).then_inc(ln.s_free, 1)
                    S.add()
                for i in range(QT + 2):
                    if i < QT:
                        e.wait_ge(shifted, b * QT + (i + 1))
                        e.activation(probs[:, i % 2, :], probs[:, i % 2, :], ACT.Exp).then_inc(exp_done, 1)
                    if i >= 2:
                        t = i - 2
                        e.wait_ge(t_full, b * QT + (t + 1))
                        e.activation(probsT[:, 4:8, t * P:(t + 1) * P],
                                     core.banks[:, 5, :].rearrange("p (c q) -> p c q", c=4), ACT.Copy).then_inc(ts_free, 1)
                for m in range(1, tiles, 2):
                    e.wait_ge(ln.s_full, S(1))
                    e.activation(q[:, m, :], core.lane_s, ACT.Copy).then_inc(ln.s_free, 1)
                    S.add()


def cross_attention_0(core):
    d = core.dram
    cross_attention(core, "cross0", 1, [(0, 2, INNER), (2048, 2, INNER), (4096, 2, INNER), (6144, 8, D)], H0, DH0,
                    ("g2", "be2"), "bo2", None,
                    lambda e: load_weights(e, core, 0, [(0, d["L0_xattn_Wp"]), (4096, d["L0_xattn_W2"])]))


def feed_forward(core, name, side, w1, w2, norm, b1, b2, gated, prefetch):
    at = 0
    normed, at = core.area(at, KD, T)
    centred, at = core.area(at, KD, T)
    squared, at = core.area(at, KD, T)
    std, at = core.area(at, T)
    hidden, at = core.area(at, 8, T)
    gate, at = core.area(at, 2, T)
    ln, nm = Lanes(core, name), Norm(core, name)
    gelu_done = core.sem(f"{name}_gelu")
    V_SHARE, S_SHARE = (1 + 8 + 2, 1 + 8) if gated else (1 + 4 + 2, 1 + 4)
    x_in = lambda b: [(P, core.X[:, k, b, PRE:S1]) for k in range(KD)]
    if gated:
        groups = [g for m in range(8) for g in ((1, 8 + m), (0, m))]
    else:
        groups = [(m % 2, m) for m in range(8)]

    with core.nc.Block() as block:
        @block.sync
        def _(e):
            prefetch(e)

        @block.tensor
        def _(e):
            V, S = Count(), Count()
            e.wait_ge(core.w_loaded[side], core.w_count[side])
            with e.Fori(0, B) as b:
                V.round(b, V_SHARE)
                S.round(b, S_SHARE)
                lanes = lanes_of(core, ln, V, S)
                norm_pe(e, core, nm, ln, V, S, b, x_in(b), core.mean_d, squared, T)
                e.wait_ge(nm.ready, b + 1)
                for which, m in groups:
                    lane, free, full, c = lanes[which]
                    e.wait_ge(free, c())
                    for k in range(KD):
                        mm = e.matmul(lane, w1[:, k, m * P:(m + 1) * P], normed[:, k, :], start=(k == 0), stop=(k == KD - 1))
                    mm.then_inc(full, 1)
                    c.add()
                e.wait_ge(ln.v_free, V())
                e.wait_ge(ln.s_free, S())
                if not gated:
                    e.wait_ge(gelu_done, 4 * b + 4)
                for m in range(KD):
                    e.wait_ge(ln.v_free, V())
                    for k in range(8):
                        mm = e.matmul(core.lane_v, w2[:, k, m * P:(m + 1) * P], hidden[:, k, :], start=(k == 0), stop=(k == 7))
                    mm.then_inc(ln.v_full, 1)
                    V.add()

        @block.vector
        def _(e):
            V, S = Count(), Count()
            with e.Fori(0, B) as b:
                V.round(b, V_SHARE)
                S.round(b, S_SHARE)
                norm_dve(e, core, nm, ln, V, S, b, x_in(b), centred, std, normed, norm[0], T)
                for which, m in groups:
                    if which == 1:
                        S.add()
                        continue
                    e.wait_ge(ln.v_full, V(1))
                    if gated:
                        e.wait_ge(ln.s_free, S())
                        e.scalar_tensor_tensor(out=hidden[:, m, :], in0=core.lane_v, scalar=core.v(b1, m), in1=gate[:, m % 2, :],
                                               op0=ALU.add, op1=ALU.mult).then_inc(ln.v_free, 1)
                    else:
                        e.tensor_scalar(hidden[:, m, :], core.lane_v, core.v(b1, m), None, ALU.add).then_inc(ln.v_free, 1)
                    V.add()
                for m in range(KD):
                    e.wait_ge(ln.v_full, V(1))
                    x = core.X[:, m, b, PRE:S1]
                    e.scalar_tensor_tensor(out=x, in0=core.lane_v, scalar=core.v(b2, m), in1=x,
                                           op0=ALU.add, op1=ALU.add).then_inc(ln.v_free, 1)
                    V.add()

        @block.scalar
        def _(e):
            V, S = Count(), Count()
            with e.Fori(0, B) as b:
                V.round(b, V_SHARE)
                S.round(b, S_SHARE)
                norm_act(e, core, nm, ln, V, S, b, [P] * KD, centred, squared, std, normed, norm[1], T)
                for which, m in groups:
                    if which == 1:
                        e.wait_ge(ln.s_full, S(1))
                        if gated:
                            if m - 8 >= 2:
                                e.wait_ge(ln.v_free, V(-1))
                            to = gate[:, m % 2, :]
                        else:
                            to = hidden[:, m, :]
                        e.activation(to, core.lane_s, ACT.Gelu, bias=core.v(b1, m)).then_inc(ln.s_free, 1)
                        S.add()
                    else:
                        V.add()
                        if not gated:
                            e.wait_ge(ln.v_free, V())
                            e.activation(hidden[:, m, :], hidden[:, m, :], ACT.Gelu).then_inc(gelu_done, 1)


def feed_forward_0(core):
    d = core.dram
    feed_forward(core, "ff0", 0, wview(core, 0, 0, 2, 2048), wview(core, 0, 4096, 8, D), ("g3", "be3"), "bp", "b2_0", True,
                 lambda e: load_mamba(e, core, 0))


def cross_attention_2(core):
    cross_attention(core, "cross2", 0, [(0, 2, D), (512, 2, D), (1024, 2, D), (1536, 2, D)], 16, 16,
                    ("l1w", "l1b"), "bproj", ("l2w", "l2b"), lambda e: load_last(e, core))


def feed_forward_2(core):
    feed_forward(core, "ff2", 0, wview(core, 0, 2048, 2, HID), wview(core, 0, 4096, 8, D), ("l3w", "l3b"), "b1", "b2_2", False,
                 lambda e: None)


def load_second(e, core):
    d = core.dram
    kv = d["L2_xattn_Wkv"]
    load_weights(e, core, 0, [(0, d["L2_xattn_Wq"]), (512, kv[:, 0:D]), (1024, kv[:, D:2 * D]), (1536, d["L2_xattn_Wproj"]),
                              (2048, d["L2_xattn_W1"]), (4096, d["L2_xattn_W2"])])


def load_last(e, core):
    d = core.dram
    load_weights(e, core, 1, [(0, d["L3_Wq"]), (512, d["L3_Wk"]), (1024, d["L3_Wv"]), (1536, d["L3_Wd"])])


def last_attention(core):
    at = 0
    normed, at = core.area(at, KD, T)
    centred, at = core.area(at, KD, T)
    squared, at = core.area(at, KD, T)
    std, at = core.area(at, T)
    context, at = core.area(at, 2, B * M)
    q, at = core.area(at, KD, T)
    kT, at = core.area(at, KD, M)
    v_, at = core.area(at, D)
    ctx1, at = core.area(at, 2, M)
    probs, at = core.area(at, 4, M)
    probsT, at = core.area(at, T)
    mixed, at = core.area(at, KD, T)
    rowmax, at = core.area(at, 4)
    rowsum, at = core.area(at, 4)
    name = "last"
    norm_context(core, 1, "gkv", "bekv", context, squared, std)
    wq, wk, wv, wd = (wview(core, 1, 512 * j, 2, D) for j in range(4))
    ln, nm = Lanes(core, name), Norm(core, name)
    ctx_ready = core.sem(f"{name}_ctx_ready")
    s_full = core.sem(f"{name}_scores")
    max_done, shifted = core.sem(f"{name}_max"), core.sem(f"{name}_shifted")
    exp_done = core.sem(f"{name}_exp")
    sum_done, rsum_ready, p_ready = core.sem(f"{name}_sum"), core.sem(f"{name}_rsum"), core.sem(f"{name}_probs")
    t_full, t_free = core.sem(f"{name}_t_full"), core.sem(f"{name}_t_free")
    V_SHARE, S_SHARE = 1 + 2 + 1 + 1 + 2, 1 + 1 + 1
    x_in = lambda b: [(P, core.X[:, k, b, PRE:S1]) for k in range(KD)]
    QT = T // P

    with core.nc.Block() as block:
        @block.gpsimd
        def _(e):
            with e.Fori(0, B) as b:
                e.wait_ge(ln.v_free, b * V_SHARE)
                for k, r in enumerate(CROWS):
                    own = context[0:r, k, bass.ts(b, M)]
                    last = e.tensor_tensor(ctx1[0:r, k, :], own, core.one[0:r, 0:1].to_broadcast([r, M]), ALU.mult)
                last.then_inc(ctx_ready, 1)

        @block.tensor
        def _(e):
            V, S = Count(), Count()
            e.wait_ge(core.w_loaded[1], core.w_count[1])
            with e.Fori(0, B) as b:
                V.round(b, V_SHARE)
                S.round(b, S_SHARE)
                lanes = lanes_of(core, ln, V, S)
                norm_pe(e, core, nm, ln, V, S, b, x_in(b), core.mean_d, squared, T)
                e.wait_ge(ctx_ready, b + 1)
                e.wait_ge(ln.v_free, V())
                for m in range(KD):
                    for k, r in enumerate(CROWS):
                        mm = e.matmul(core.lane_v[:, m * M:(m + 1) * M], wk[0:r, k, m * P:(m + 1) * P], ctx1[0:r, k, :],
                                      start=(k == 0), stop=(k == 1))
                mm.then_inc(ln.v_full, 1)
                V.add()
                e.wait_ge(ln.v_free, V())
                for k, r in enumerate(CROWS):
                    mm = e.matmul(core.lane_v[0:M, 0:D], ctx1[0:r, k, :], wv[0:r, k, :], start=(k == 0), stop=(k == 1))
                mm.then_inc(ln.v_full, 1)
                V.add()
                e.wait_ge(nm.ready, b + 1)
                for m in range(KD):
                    lane, free, full, c = lanes[m % 2]
                    e.wait_ge(free, c())
                    for k in range(KD):
                        mm = e.matmul(lane, wq[:, k, m * P:(m + 1) * P], normed[:, k, :], start=(k == 0), stop=(k == KD - 1))
                    mm.then_inc(full, 1)
                    c.add()
                e.wait_ge(ln.v_free, V())
                e.wait_ge(ln.s_free, S())
                for t in range(QT):
                    for k in range(KD):
                        mm = e.matmul(core.banks[:, 0, t * M:(t + 1) * M], q[:, k, t * P:(t + 1) * P], kT[:, k, :],
                                      start=(k == 0), stop=(k == KD - 1))
                mm.then_inc(s_full, 1)
                e.wait_ge(p_ready, b + 1)
                for t in range(QT):
                    mm = e.matmul(core.banks[0:M, 4, t * P:(t + 1) * P], probs[:, t, :], core.ident[:], start=True, stop=True)
                mm.then_inc(t_full, 1)
                e.wait_ge(t_free, b + 1)
                for m in range(KD):
                    lane, free, full, c = lanes[m % 2]
                    e.wait_ge(free, c())
                    e.matmul(lane, v_[0:M, m * P:(m + 1) * P], probsT[0:M, :], start=True, stop=True).then_inc(full, 1)
                    c.add()
                e.wait_ge(ln.v_free, V())
                e.wait_ge(ln.s_free, S())
                for m in range(KD):
                    e.wait_ge(ln.v_free, V())
                    for k in range(KD):
                        mm = e.matmul(core.lane_v, wd[:, k, m * P:(m + 1) * P], mixed[:, k, :], start=(k == 0), stop=(k == KD - 1))
                    mm.then_inc(ln.v_full, 1)
                    V.add()

        @block.vector
        def _(e):
            V, S = Count(), Count()
            with e.Fori(0, B) as b:
                V.round(b, V_SHARE)
                S.round(b, S_SHARE)
                norm_dve(e, core, nm, ln, V, S, b, x_in(b), centred, std, normed, "gq", T)
                e.wait_ge(ln.v_full, V(1))
                for m in range(KD):
                    last = e.tensor_scalar(kT[:, m, :], core.lane_v[:, m * M:(m + 1) * M], core.v("bk", m), None, ALU.add)
                last.then_inc(ln.v_free, 1)
                V.add()
                e.wait_ge(ln.v_full, V(1))
                e.tensor_copy(v_[0:M, :], core.lane_v[0:M, 0:D]).then_inc(ln.v_free, 1)
                V.add()
                e.wait_ge(ln.v_full, V(1))
                e.tensor_scalar(q[:, 0, :], core.lane_v, core.v("bq", 0), None, ALU.add).then_inc(ln.v_free, 1)
                V.add()
                scores = core.banks[:, 0, 0:QT * M].rearrange("p (t m) -> p t m", t=QT)
                e.wait_ge(s_full, b + 1)
                e.tensor_reduce(rowmax, scores, AX.X, ALU.max).then_inc(max_done, 1)
                e.wait_ge(max_done, b + 1)
                e.tensor_tensor(probs, scores, rowmax.unsqueeze(2).to_broadcast([P, QT, M]), ALU.subtract).then_inc(shifted, 1)
                e.wait_ge(exp_done, b + 1)
                e.tensor_reduce(rowsum, probs, AX.X, ALU.add).then_inc(sum_done, 1)
                e.wait_ge(sum_done, b + 1)
                e.reciprocal(rowsum, rowsum).then_inc(rsum_ready, 1)
                e.wait_ge(rsum_ready, b + 1)
                e.tensor_tensor(probs, probs, rowsum.unsqueeze(2).to_broadcast([P, QT, M]), ALU.mult).then_inc(p_ready, 1)
                e.wait_ge(t_full, b + 1)
                e.tensor_copy(probsT[0:M, :], core.banks[0:M, 4, :]).then_inc(t_free, 1)
                e.wait_ge(ln.v_full, V(1))
                e.tensor_scalar(mixed[:, 0, :], core.lane_v, core.v("bv", 0), None, ALU.add).then_inc(ln.v_free, 1)
                V.add()
                for m in range(KD):
                    e.wait_ge(ln.v_full, V(1))
                    x = core.X[:, m, b, PRE:S1]
                    e.scalar_tensor_tensor(out=x, in0=core.lane_v, scalar=core.v("bd", m), in1=x,
                                           op0=ALU.add, op1=ALU.add).then_inc(ln.v_free, 1)
                    V.add()

        @block.scalar
        def _(e):
            V, S = Count(), Count()
            with e.Fori(0, B) as b:
                V.round(b, V_SHARE)
                S.round(b, S_SHARE)
                norm_act(e, core, nm, ln, V, S, b, [P] * KD, centred, squared, std, normed, "beq", T)
                e.wait_ge(ln.s_full, S(1))
                e.activation(q[:, 1, :], core.lane_s, ACT.Identity, bias=core.v("bq", 1)).then_inc(ln.s_free, 1)
                S.add()
                e.wait_ge(shifted, b + 1)
                e.activation(probs, probs, ACT.Exp).then_inc(exp_done, 1)
                e.wait_ge(ln.s_full, S(1))
                e.activation(mixed[:, 1, :], core.lane_s, ACT.Identity, bias=core.v("bv", 1)).then_inc(ln.s_free, 1)
                S.add()


CHUNKS = B * NCH
STEPS = LAYERS * CHUNKS
BODY = 12
SET = BODY // 2
UN, US = 16, 4
CREDIT = UN
LW = {"norm": (0, 2), "conv_b": (2, 4), "conv_w": (6, 16), "dt_b": (22, 4), "D": (26, 4), "A_log": (30, 64)}
NLW = 94
W_LOADS = 5
FAR = 1e25
A_MAX = -1e-22
MW = (0, 2048, 2240, 2752, 3776)


def load_layer(e, core, side, layer, sem):
    d, w = core.dram, core.weights[1]
    o = [4096 * side + c for c in MW]
    view = lambda c, k, n: w[:, c:c + k * n].rearrange("p (k n) -> p k n", k=k)
    one = lambda a: a[bass.ds(layer, 1)].rearrange("l r n -> (l r) n")
    tiles = lambda a: one(a).rearrange("(k p) n -> p k n", p=P)
    e.dma_start(view(o[0], KD, 2 * DI), tiles(d["in_w"])).then_inc(sem, 16)
    e.dma_start(view(o[1], KI, 48), tiles(d["x_w"])).then_inc(sem, 16)
    e.dma_start(w[0:DTR, o[2]:o[2] + DI], one(d["dt_w"])).then_inc(sem, 16)
    e.dma_start(view(o[3], KI, D), tiles(d["out_w"])).then_inc(sem, 16)
    e.dma_start(w[:, o[4]:o[4] + NLW], one(d["layer_vec"])).then_inc(sem, 16)


def load_mamba(e, core, _):
    core.side_loaded = [core.sem("side0_loaded"), core.sem("side1_loaded")]
    for side in range(2):
        load_layer(e, core, side, 0, core.side_loaded[side])


def prepend(core):
    w1, w2 = wview(core, 0, 6144, 2, D), wview(core, 0, 6656, 2, D)
    hidden, _ = core.area(0, KD, B * M)
    ln = Lanes(core, "pre")
    with core.nc.Block() as block:
        @block.sync
        def _(e):
            load_weights(e, core, 0, [(6144, core.dram["L1_xattn_pre_w1"]), (6656, core.dram["L1_xattn_pre_w2"])])

        @block.tensor
        def _(e):
            e.wait_ge(core.w_loaded[0], core.w_count[0])
            for m in range(KD):
                e.wait_ge(ln.s_free, m)
                for k, r in enumerate(CROWS):
                    mm = e.matmul(core.lane_s, w1[0:r, k, m * P:(m + 1) * P], core.C[0:r, k, :], start=(k == 0), stop=(k == 1))
                mm.then_inc(ln.s_full, 1)
            e.wait_ge(ln.s_free, KD)
            for m in range(KD):
                e.wait_ge(ln.v_free, m)
                for k in range(KD):
                    mm = e.matmul(core.lane_v, w2[:, k, m * P:(m + 1) * P], hidden[:, k, :], start=(k == 0), stop=(k == KD - 1))
                mm.then_inc(ln.v_full, 1)

        @block.scalar
        def _(e):
            for m in range(KD):
                e.wait_ge(ln.s_full, m + 1)
                e.activation(hidden[:, m, :], core.lane_s, ACT.Silu).then_inc(ln.s_free, 1)

        @block.vector
        def _(e):
            for m in range(KD):
                e.wait_ge(ln.v_full, m + 1)
                e.tensor_copy(core.X[:, m, :, 0:PRE], core.lane_v.rearrange("p (b t) -> p b t", b=B)).then_inc(ln.v_free, 1)


def mamba(core):
    at = 0
    bc, at = core.area(at, 2, 2 * DS, TC)
    x, at = core.area(at, 2, KI, TC)
    z, at = core.area(at, 2, KI, TC)
    u, at = core.area(at, 2, KI, TC)
    dt, at = core.area(at, 2, KI, TC + 1)
    t1, at = core.area(at, KI, TC)
    t2, at = core.area(at, KI, TC)
    t3, at = core.area(at, KI, TC)
    fed, at = core.area(at, 4, US, TC + 1)
    normed, at = core.area(at, KD, TC)
    squared, at = core.area(at, KD, TC)
    rstd, at = core.area(at, TC)
    xdbl, at = core.area(at, TC)
    state, at = core.area(at, KI, DS)
    decay, at = core.area(at, 2, KI * DS)
    zero, at = core.area(at, 1)
    log_1, at = core.area(at, 1)
    spread = core.weights[0]
    diag = spread[:, 0:4096].rearrange("p (s k j n) -> p s k j n", s=2, k=KI, j=TAPS)
    hc = spread[:, 4096:7168].rearrange("p (q s t) -> p q s t", q=4, s=US)
    raw = spread[:, 7168:7168 + KI * (TC + 3)].rearrange("p (k t) -> p k t", k=KI)
    banks = core.banks
    da = [banks[:, 2 * s:2 * s + 2, :].rearrange("p a n -> p (a n)")[:, 0:US * (TC + 1)] for s in range(2)]
    da4 = [a.rearrange("p (s t) -> p s t", s=US) for a in da]
    ybank = [banks[:, 4, 0:TC], banks[:, 5, 0:TC]]
    lane_v2 = core.lane_v[:, 0:2 * TC].rearrange("p (m t) -> p m t", m=2)
    lane_s2 = core.lane_s[:, 0:2 * TC].rearrange("p (m t) -> p m t", m=2)
    w = core.weights[1]
    in_w, x_w, dt_w, out_w, vecs = [], [], [], [], []
    for side in range(2):
        o = [4096 * side + c for c in MW]
        in_w.append(w[:, o[0]:o[0] + 2048].rearrange("p (k n) -> p k n", k=KD))
        x_w.append(w[:, o[1]:o[1] + 192].rearrange("p (k n) -> p k n", k=KI))
        dt_w.append(w[0:DTR, o[2]:o[2] + DI])
        out_w.append(w[:, o[3]:o[3] + 1024].rearrange("p (k n) -> p k n", k=KI))
        vecs.append(w[:, o[4]:o[4] + NLW])
    lv = lambda side, name, j: vecs[side][:, LW[name][0] + j:LW[name][0] + j + 1]

    ln = Lanes(core, "mamba")
    S = lambda name: core.sem(f"mamba_{name}")
    set_up = S("set_up")
    side_ready = S("side_ready")
    a_exp = S("a_exp")
    squared_ready, rstd_ln, rstd_ready, normed_ready = S("squared"), S("rstd_ln"), S("rstd"), S("normed")
    carried = S("carried")
    silu_done = S("silu")
    bc_stored, bc_ready = S("bc_stored"), S("bc_ready")
    soft_abs, soft_exp, soft_ln = S("soft_abs"), S("soft_exp"), S("soft_ln")
    soft_one, soft_rest, soft_sum = S("soft_one"), S("soft_rest"), S("soft_sum")
    dt_ready, u_ready = S("dt_ready"), S("u_ready")
    exp_done, fed_ready, scanned, unit_done, summed = S("exp"), S("fed"), S("scanned"), S("unit_done"), S("summed")
    y_skip, gated = S("y_skip"), S("gated")
    scratch = core.nc.dram_tensor("mamba_bc", (2, 2 * DS, TC), F32, kind="Internal").ap()

    FIRST = -2

    def v_after(n, k):
        return k - 4 if isinstance(n, int) and n == FIRST else 6 * n + (7 + k)

    s_after = lambda n, k: 5 * n + (6 + k)
    unit = lambda n, i: n * UN + i

    def at_step(l, half, j):
        n = (l * 2 + half) * BODY + j
        return n, j % 2, j // SET, half * 4 + j // NCH, j % NCH

    def following(l, half, j, d):
        j += d
        if j < BODY:
            return at_step(l, half, j)[1:]
        j -= BODY
        return j % 2, 0, half * -4 + (4 + j // NCH), j % NCH

    def preceding(l, half, j):
        if j > 0:
            return at_step(l, half, j - 1)[1:]
        return 1, 1, half * -4 + 7, NCH - 1

    X = lambda b, c: core.X[:, :, b, c * TC:(c + 1) * TC]

    def late_pe(e, n, p, side, b, c):
        def convolve(m0):
            def go():
                e.wait_ge(ln.s_free, s_after(n, m0 // 2))
                if m0 == 0:
                    e.wait_ge(ln.v_free, v_after(n - 1, 6))
                for m in range(2):
                    for j in range(TAPS):
                        mm = e.matmul(lane_s2[:, m, :], diag[:, side, m0 + m, j, :], raw[:, m0 + m, j:j + TC],
                                      start=(j == 0), stop=(j == TAPS - 1))
                mm.then_inc(ln.s_full, 1)
            return go

        def project_z(m0):
            def go():
                e.wait_ge(ln.v_free, v_after(n, 1 + m0 // 2))
                for m in range(2):
                    for k in range(KD):
                        f = DI + (m0 + m) * P
                        mm = e.matmul(lane_v2[:, m, :], in_w[side][:, k, f:f + P], normed[:, k, :], start=(k == 0), stop=(k == KD - 1))
                mm.then_inc(ln.v_full, 1)
            return go

        def project_x():
            e.wait_ge(silu_done, n + 2)
            e.wait_ge(ln.s_free, s_after(n, 2))
            for k in range(KI):
                mm = e.matmul(core.lane_s[0:48, 0:TC], x_w[side][:, k, :], x[:, p, k, :], start=(k == 0), stop=(k == KI - 1))
            mm.then_inc(ln.s_full, 1)

        def project_dt():
            e.wait_ge(ln.s_free, s_after(n, 3))
            e.wait_ge(ln.v_free, v_after(n, 3))
            for m in range(KI):
                mm = e.matmul((lane_v2, lane_s2)[m // 2][:, m % 2, :], dt_w[side][:, m * P:(m + 1) * P], xdbl[0:DTR, :],
                              start=True, stop=True)
                if m % 2 == 1:
                    mm.then_inc((ln.v_full, ln.s_full)[m // 2], 1)

        return {0: [convolve(0)], 3: [convolve(2), project_z(0)], 4: [project_z(2)], 6: [project_x], 8: [project_dt]}

    def early_pe(e, n, p, side, b, c):
        def mean():
            e.wait_ge(ln.v_free, v_after(n, 4))
            e.wait_ge(squared_ready, n + 3)
            for k in range(KD):
                mm = e.matmul(core.lane_v[:, 0:TC], core.mean_d[:], squared[:, k, :], start=(k == 0), stop=(k == KD - 1))
            mm.then_inc(ln.v_full, 1)

        def project_in():
            e.wait_ge(normed_ready, n + 3)
            for m in range(KI):
                if m == 0:
                    e.wait_ge(ln.v_free, v_after(n, 5))
                if m == 2:
                    e.wait_ge(ln.s_free, s_after(n, 4))
                for k in range(KD):
                    mm = e.matmul((lane_v2, lane_s2)[m // 2][:, m % 2, :], in_w[side][:, k, m * P:(m + 1) * P], normed[:, k, :],
                                  start=(k == 0), stop=(k == KD - 1))
                if m % 2 == 1:
                    mm.then_inc((ln.v_full, ln.s_full)[m // 2], 1)

        return {9: [mean], 13: [project_in]}

    def late_act(e, n, p, side, b, c):
        def copy_x(m0):
            def go():
                if m0 == 0:
                    e.wait_ge(ln.v_full, v_after(n, 1))
                e.wait_ge(ln.s_full, s_after(n, 1 + m0 // 2))
                for m in range(2):
                    last = e.activation(x[:, p, m0 + m, :], lane_s2[:, m, :], ACT.Identity, bias=lv(side, "conv_b", m0 + m))
                last.then_inc(ln.s_free, 1)
            return go

        def silu():
            e.wait_ge(ln.s_free, s_after(n, 2))
            e.activation(x[:, p], x[:, p], ACT.Silu).then_inc(silu_done, 1)
            e.wait_ge(ln.v_free, v_after(n, 3))
            e.activation(z[:, p], z[:, p], ACT.Silu)

        def copy_xdbl():
            e.wait_ge(ln.s_full, s_after(n, 3))
            e.wait_ge(bc_stored, 16 * (n + 1))
            e.activation(xdbl[0:48, :], core.lane_s[0:48, 0:TC], ACT.Copy).then_inc(ln.s_free, 1)

        def bias_dt():
            e.wait_ge(ln.s_full, s_after(n, 4))
            for m in range(2):
                last = e.activation(dt[:, p, 2 + m, 1:], lane_s2[:, m, :], ACT.Identity, bias=lv(side, "dt_b", 2 + m))
            last.then_inc(ln.s_free, 1)

        def softplus():
            e.wait_ge(ln.v_free, v_after(n, 4))
            e.wait_ge(ln.s_free, s_after(n, 4))
            e.wait_ge(soft_rest, n + 1)
            e.activation(t1, dt[:, p, :, 1:], ACT.Abs).then_inc(soft_abs, 1)
            e.wait_ge(soft_abs, n + 2)
            e.activation(t1, t1, ACT.Exp, scale=-1.0).then_inc(soft_exp, 1)
            e.wait_ge(soft_exp, n + 2)
            e.wait_ge(dt_ready, n + 1)
            e.activation(t2, t1, ACT.Ln, bias=1.0).then_inc(soft_ln, 1)

        return {3: [copy_x(0)], 5: [copy_x(2)], 6: [silu], 8: [copy_xdbl], 10: [bias_dt], 11: [softplus]}

    def early_act(e, n, p, side, b, c):
        def square():
            if not (isinstance(n, int) and n == FIRST):
                e.wait_ge(ln.v_full, v_after(n - 1, 5))
            e.activation(squared, X(b, c), ACT.Square).then_inc(squared_ready, 1)

        def inverse_root():
            e.wait_ge(ln.v_full, v_after(n, 5))
            e.activation(rstd, core.lane_v[:, 0:TC], ACT.Ln, bias=core.eps[:]).then_inc(ln.v_free, 1)
            e.wait_ge(ln.v_free, v_after(n, 5))
            e.activation(rstd, rstd, ACT.Exp, scale=-0.5).then_inc(rstd_ready, 1)

        def copy_raw():
            e.wait_ge(ln.s_full, s_after(n, 5))
            e.wait_ge(carried, n + 3)
            e.activation(raw[:, 2:4, 3:], lane_s2, ACT.Copy).then_inc(ln.s_free, 1)

        return {7: [square], 11: [inverse_root], 15: [copy_raw]}

    def late_dve(e, n, p, side, b, c):
        def copy_z(m0):
            def go():
                e.wait_ge(ln.v_full, v_after(n, 2 + m0 // 2))
                e.tensor_copy(z[:, p, m0:m0 + 2, :], lane_v2).then_inc(ln.v_free, 1)
            return go

        def bias_dt():
            e.wait_ge(ln.v_full, v_after(n, 4))
            for m in range(2):
                last = e.tensor_scalar(dt[:, p, m, 1:], lane_v2[:, m, :], lv(side, "dt_b", m), None, ALU.add)
            last.then_inc(ln.v_free, 1)

        def one():
            e.wait_ge(soft_exp, n + 2)
            e.tensor_scalar(t3, t1, 1.0, 1.0, ALU.add, ALU.subtract).then_inc(soft_one, 1)

        def total():
            e.wait_ge(soft_rest, n + 2)
            e.wait_ge(soft_ln, n + 2)
            e.scalar_tensor_tensor(out=t2, in0=t2, scalar=log_1, in1=t3, op0=ALU.subtract, op1=ALU.add).then_inc(soft_sum, 1)

        def finish_dt():
            e.wait_ge(soft_sum, n + 2)
            e.wait_ge(ln.s_free, s_after(n, 4))
            e.scalar_tensor_tensor(out=dt[:, p, :, 1:], in0=dt[:, p, :, 1:], scalar=0.0, in1=t2, op0=ALU.max, op1=ALU.add) \
                .then_inc(dt_ready, 1)
            e.wait_ge(dt_ready, n + 2)
            e.wait_ge(silu_done, n + 2)
            e.tensor_tensor(u[:, p], dt[:, p, :, 1:], x[:, p], ALU.mult).then_inc(u_ready, 1)

        return {4: [copy_z(0)], 5: [copy_z(2)], 9: [bias_dt], 11: [one], 13: [total], 14: [finish_dt]}

    def early_dve(e, n, p, side, b, c):
        def scale():
            e.wait_ge(rstd_ready, n + 3)
            for k in range(KD):
                last = e.scalar_tensor_tensor(out=normed[:, k, :], in0=core.X[:, k, b, c * TC:(c + 1) * TC],
                                              scalar=lv(side, "norm", k), in1=rstd, op0=ALU.mult, op1=ALU.mult)
            last.then_inc(normed_ready, 1)

        def carry():
            if not (isinstance(n, int) and n == FIRST):
                e.wait_ge(ln.s_full, s_after(n, 2))
            if c == 0:
                e.memset(raw[:, :, 0:3], 0.0).then_inc(carried, 1)
            else:
                e.tensor_copy(raw[:, :, 0:3], raw[:, :, TC:TC + 3]).then_inc(carried, 1)
            e.wait_ge(carried, n + 3)
            e.wait_ge(ln.v_full, v_after(n, 6))
            e.tensor_copy(raw[:, 0:2, 3:], lane_v2).then_inc(ln.v_free, 1)

        return {12: [scale], 15: [carry]}

    def late_pool(e, n):
        def rest():
            e.wait_ge(soft_one, n + 2)
            e.tensor_tensor(t3, t1, t3, ALU.subtract).then_inc(soft_rest, 1)

        return {14: [rest]}

    def late_sp(e, n, p):
        e.wait_ge(ln.s_free, s_after(n, 3))
        e.wait_ge(bc_ready, 16 * (n + 1))
        e.dma_start(scratch[p], xdbl[DTR:DTR + 2 * DS, :]).then_inc(bc_stored, 16)
        e.wait_ge(bc_stored, 16 * (n + 2))
        if not (isinstance(n, int) and n < 0):
            e.wait_ge(unit_done, (n + 1) * CREDIT)
        e.dma_start(bc[:, p], scratch[p].partition_broadcast(P)).then_inc(bc_ready, 16)

    def side_act(e, m, side, loads):
        e.wait_ge(core.side_loaded[side], loads)
        e.wait_ge(side_ready, 2 * m)
        e.activation(decay[:, side, :], vecs[side][:, LW["A_log"][0]:LW["A_log"][0] + KI * DS], ACT.Exp).then_inc(a_exp, 1)

    def side_dve(e, m, side, loads):
        e.wait_ge(core.side_loaded[side], loads)
        for k in range(KI):
            for j in range(TAPS):
                last = e.tensor_scalar(diag[:, side, k, j, :], core.ident[:], lv(side, "conv_w", TAPS * k + j), None, ALU.mult)
        last.then_inc(side_ready, 1)
        e.wait_ge(a_exp, m + 1)
        e.tensor_scalar(decay[:, side, :], decay[:, side, :], -1.0, A_MAX, ALU.mult, ALU.min).then_inc(side_ready, 1)

    def project_out(e, n, p, side):
        e.wait_ge(gated, KI * n + KI)
        e.wait_ge(ln.v_free, v_after(n, 0))
        for m in range(KD):
            for k in range(KI):
                mm = e.matmul(lane_v2[:, m, :], out_w[side][:, k, m * P:(m + 1) * P], x[:, p, k, :], start=(k == 0), stop=(k == KI - 1))
        mm.then_inc(ln.v_full, 1)

    def gate(e, n, k, p, side):
        e.wait_ge(summed, n * UN + (CREDIT + UN // KI * (k + 1)))
        e.scalar_tensor_tensor(out=x[:, p, k, :], in0=x[:, p, k, :], scalar=lv(side, "D", k), in1=ybank[k % 2],
                               op0=ALU.mult, op1=ALU.add).then_inc(y_skip, 1)
        e.wait_ge(y_skip, KI * n + (k + 2))
        e.tensor_tensor(x[:, p, k, :], x[:, p, k, :], z[:, p, k, :], ALU.mult).then_inc(gated, 1)

    def residual(e, n, b, c):
        e.wait_ge(ln.v_full, v_after(n, 1))
        e.tensor_tensor(X(b, c), X(b, c), lane_v2, ALU.add).then_inc(ln.v_free, 1)

    def in_order(*parts):
        return {i: [piece for part in parts for piece in part.get(i, [])] for i in range(UN)}

    def before_first(late, early):
        for parts in (early(FIRST, 0, 0, 0, 0),), (late(-1, 0, 0, 0, 0), early(-1, 1, 0, 0, 1)):
            for pieces in in_order(*parts).values():
                for piece in pieces:
                    piece()

    def pieces_of(late, early, e, l, half, j):
        n = at_step(l, half, j)[0]
        return in_order(late(e, n, *following(l, half, j, 1)), early(e, n, *following(l, half, j, 2)))

    LOAD = 16 * W_LOADS
    SETTING = 8
    with core.nc.Block() as block:
        @block.sync
        def _(e):
            late_sp(e, -1, 0)
            with e.Fori(0, LAYERS) as l:
                with e.Fori(0, 2) as half:
                    for j in range(BODY):
                        n = at_step(l, half, j)[0]
                        p = following(l, half, j, 1)[0]
                        if j % SET == 1:
                            e.wait_ge(ln.v_free, v_after(n - 1, 1))
                        late_sp(e, n, p)
                        if j == 1:
                            load_layer(e, core, 1, l, core.side_loaded[1])
                        if j == SET + 1:
                            load_layer(e, core, 0, (l + half) % LAYERS, core.side_loaded[0])
            e.wait_ge(bc_ready, 16 * (STEPS + 1))
            for side in range(2):
                e.wait_ge(core.side_loaded[side], (2 * LAYERS + 1) * LOAD)

        @block.tensor
        def _(e):
            e.wait_ge(side_ready, 2)
            e.wait_ge(core.side_loaded[1], LOAD)
            e.wait_ge(set_up, 5)
            e.matmul(ybank[1], core.ident[:], x[:, 1, 0, :], start=True, stop=True).then_inc(summed, 1)
            before_first(lambda *a: late_pe(e, *a), lambda *a: early_pe(e, *a))
            with e.Fori(0, LAYERS) as l:
                with e.Fori(0, 2) as half:
                    for j in range(BODY):
                        n, p, side, b, c = at_step(l, half, j)
                        pieces = pieces_of(late_pe, early_pe, e, l, half, j)
                        for i in range(UN):
                            if i == 1:
                                pp, ps, _, _ = preceding(l, half, j)
                                project_out(e, n, pp, ps)
                            if i == SETTING + 1 and j % SET == SET - 2:
                                e.wait_ge(side_ready, 2 * ((l * 2 + half) * 2 + (j // SET + 2)))
                            for piece in pieces[i]:
                                piece()
                            k, q = i // 4, i % 4
                            if q == 0:
                                e.wait_ge(gated, KI * n + (KI + k - 1))
                            e.wait_ge(unit_done, n * UN + (CREDIT + i + 1))
                            for s in range(US):
                                mm = e.matmul(ybank[k % 2], core.ident[:], hc[:, q, s, :], start=(q == 0 and s == 0),
                                              stop=(q == 3 and s == US - 1))
                            mm.then_inc(summed, 1)
            project_out(e, STEPS, 1, 1)

        @block.vector
        def _(e):
            e.memset(state, 0.0).then_inc(set_up, 1)
            e.memset(x[:, 1], 0.0).then_inc(set_up, 1)
            e.memset(z[:, 1], 0.0).then_inc(set_up, 1)
            e.memset(zero, 0.0).then_inc(set_up, 1)
            e.memset(dt[:, :, :, 0:1], FAR).then_inc(set_up, 1)
            scrap = t2[:, 0, :]
            for i in range(CREDIT):
                e.memset(scrap[:, 4 * i:4 * i + 1], 0.0).then_inc(unit_done, 1)
                if i > 0:
                    e.memset(scrap[:, 4 * i + 1:4 * i + 2], 0.0).then_inc(summed, 1)
                if 0 < i < KI:
                    e.memset(scrap[:, 4 * i + 2:4 * i + 3], 0.0).then_inc(gated, 1)
            e.wait_ge(core.side_loaded[1], LOAD)
            side_dve(e, 0, 0, LOAD)
            before_first(lambda *a: late_dve(e, *a), lambda *a: early_dve(e, *a))
            with e.Fori(0, LAYERS) as l:
                with e.Fori(0, 2) as half:
                    for j in range(BODY):
                        n, p, side, b, c = at_step(l, half, j)
                        pp, ps, pb, pc = preceding(l, half, j)
                        pieces = pieces_of(late_dve, early_dve, e, l, half, j)
                        for i in range(UN):
                            k, q = i // 4, i % 4
                            if i == 3:
                                residual(e, n, pb, pc)
                            if i == SETTING and j % SET == SET - 2:
                                m = (l * 2 + half) * 2 + (j // SET + 1)
                                side_dve(e, m, following(l, half, j, 2)[1], (l * 2 + half + 2) * LOAD)
                            for piece in pieces[i]:
                                piece()
                            e.wait_ge(exp_done, unit(n, i) + 1)
                            e.wait_ge(fed_ready, unit(n, i) + 1)
                            e.tensor_tensor_scan(da[i % 2], da[i % 2], fed[:, q].rearrange("p s t -> p (s t)"), 0.0,
                                                 ALU.mult, ALU.add).then_inc(scanned, 1)
                            e.wait_ge(scanned, unit(n, i) + 1)
                            keep = state[:, k, q * US:(q + 1) * US]
                            if c < NCH - 1:
                                e.tensor_copy(keep, da4[i % 2][:, :, TC])
                            else:
                                e.memset(keep, 0.0)
                            e.wait_ge(summed, n * UN + (CREDIT + i - 3))
                            e.tensor_tensor(hc[:, q], da4[i % 2][:, :, 1:], bc[:, p, DS + q * US:DS + (q + 1) * US, :],
                                            ALU.mult).then_inc(unit_done, 1)
                            if i == 0:
                                gate(e, n - 1, KI - 1, pp, ps)
                            if i in (5, 9, 13):
                                gate(e, n, i // 4 - 1, p, side)
            gate(e, STEPS - 1, KI - 1, 1, 1)
            residual(e, STEPS, B - 1, NCH - 1)

        @block.scalar
        def _(e):
            e.wait_ge(set_up, 5)
            e.activation(log_1, zero, ACT.Ln, bias=1.0)
            side_act(e, 0, 0, LOAD)
            before_first(lambda *a: late_act(e, *a), lambda *a: early_act(e, *a))
            with e.Fori(0, LAYERS) as l:
                with e.Fori(0, 2) as half:
                    for j in range(BODY):
                        n, p, side, b, c = at_step(l, half, j)
                        pieces = pieces_of(late_act, early_act, e, l, half, j)
                        if j % SET == 0:
                            e.wait_ge(side_ready, 2 * ((l * 2 + half) * 2 + (j // SET + 1)))
                        for i in range(UN):
                            k, q = i // 4, i % 4
                            if i == 0:
                                e.wait_ge(dt_ready, n + 1)
                            e.wait_ge(unit_done, n * UN + (CREDIT + i - 1))
                            for s in range(US):
                                f = k * DS + q * US + s
                                last = e.activation(da4[i % 2][:, s, :], dt[:, p, k, :], ACT.Exp, scale=decay[:, side, f:f + 1])
                            last.then_inc(exp_done, 1)
                            if i == SETTING and j % SET == SET - 2:
                                m = (l * 2 + half) * 2 + (j // SET + 1)
                                side_act(e, m, following(l, half, j, 2)[1], (l * 2 + half + 2) * LOAD)
                            for piece in pieces[i]:
                                piece()

        @block.gpsimd
        def _(e):
            for piece in late_pool(e, -1)[14]:
                piece()
            with e.Fori(0, LAYERS) as l:
                with e.Fori(0, 2) as half:
                    for j in range(BODY):
                        n, p, side, b, c = at_step(l, half, j)
                        pieces = late_pool(e, n)
                        e.wait_ge(bc_ready, 16 * (n + 1))
                        e.wait_ge(u_ready, n + 1)
                        for i in range(UN):
                            k, q = i // 4, i % 4
                            e.wait_ge(unit_done, n * UN + (CREDIT + i - 3))
                            kept = state[:, k, q * US:(q + 1) * US]
                            e.tensor_tensor(fed[:, q, :, 0], kept, core.one[:, 0:US], ALU.mult)
                            e.tensor_tensor(fed[:, q, :, 1:], u[:, p, k, :].unsqueeze(1).to_broadcast([P, US, TC]),
                                            bc[:, p, q * US:(q + 1) * US, :], ALU.mult).then_inc(fed_ready, 1)
                            for piece in pieces.get(i, []):
                                piece()


def final_norm(core):
    squared, at = core.area(0, KD, T)
    std, at = core.area(at, T)
    s_full, s_free = core.sem("final_s_full"), core.sem("final_s_free")
    squared_ready, inverted = core.sem("final_squared"), core.sem("final_inverted")
    scaled = core.sem("final_scaled")
    with core.nc.Block() as block:
        @block.sync
        def _(e):
            load_second(e, core)

        @block.tensor
        def _(e):
            with e.Fori(0, B) as b:
                e.wait_ge(squared_ready, b + 1)
                e.wait_ge(s_free, b)
                for k in range(KD):
                    mm = e.matmul(core.lane_s, core.mean_d[:], squared[:, k, :], start=(k == 0), stop=(k == KD - 1))
                mm.then_inc(s_full, 1)

        @block.scalar
        def _(e):
            with e.Fori(0, B) as b:
                e.wait_ge(s_full, b)
                e.activation(squared, core.X[:, :, b, PRE:S1], ACT.Square).then_inc(squared_ready, 1)
                e.wait_ge(s_full, b + 1)
                e.wait_ge(scaled, b)
                e.activation(std, core.lane_s, ACT.Sqrt, bias=core.eps[:]).then_inc(s_free, 1)

        @block.vector
        def _(e):
            with e.Fori(0, B) as b:
                e.wait_ge(s_free, b + 1)
                e.reciprocal(std, std).then_inc(inverted, 1)
                e.wait_ge(inverted, b + 1)
                for k in range(KD):
                    x = core.X[:, k, b, PRE:S1]
                    last = e.scalar_tensor_tensor(out=x, in0=x, scalar=core.v("final", k), in1=std, op0=ALU.mult, op1=ALU.mult)
                last.then_inc(scaled, 1)


CONSTS = 6
LOADS = 16 * 5


def start(core):
    d = core.dram
    c_ready = core.const_ready
    with core.nc.Block() as block:
        @block.sync
        def _(e):
            e.dma_start(core.vec[:], d["vec"]).then_inc(core.loaded, 16)
            for k in range(KD):
                e.dma_start(core.X[:, k, :, PRE:S1], d["xT"][k * P:(k + 1) * P]).then_inc(core.loaded, 16)
            load_weights(e, core, 0, [(0, d["L0_xattn_Wq1"]), (2048, d["L0_xattn_Wk1"]), (4096, d["L0_xattn_Wv1"]),
                                      (6144, d["L0_xattn_Wo1"])])
            e.dma_start(core.C[:, 0, :], d["ctxT"][0:P]).then_inc(core.loaded, 16)
            e.dma_start(core.C[0:DC - P, 1, :], d["ctxT"][P:DC]).then_inc(core.loaded, 16)

        @block.gpsimd
        def _(e):
            e.memset(core.mean_d[:], 1.0 / D).then_inc(c_ready, 1)
            e.memset(core.mean_c[:], 1.0 / DC).then_inc(c_ready, 1)
            e.memset(core.eps[:], EPS).then_inc(c_ready, 1)
            e.memset(core.ident[:], 0.0).then_inc(c_ready, 1)
            e.memset(core.one[:], 1.0).then_inc(c_ready, 1)
            e.wait_ge(c_ready, 5)
            e.affine_select(out=core.ident[:], in_=core.ident[:], compare_op=ALU.not_equal, fill=1.0, base=0,
                            pattern=[[-1, P]], channel_multiplier=1).then_inc(c_ready, 1)


def finish(core, out):
    stored = core.sem("stored")
    with core.nc.Block() as block:
        @block.sync
        def _(e):
            for k in range(KD):
                e.dma_start(out[k * P:(k + 1) * P], core.X[:, k, :, PRE:S1]).then_inc(stored, 16)
            e.wait_ge(stored, 16 * KD)


STAGES = [self_attention, cross_attention_0, feed_forward_0, prepend, mamba, final_norm, cross_attention_2, feed_forward_2,
          last_attention]


def build(nc, dram, out):
    with ExitStack() as ctx:
        core = Core(nc, ctx, dram)
        start(core)
        for stage in STAGES:
            stage(core)
        finish(core, out)


def layouts(i):
    import numpy as np

    cols = lambda a, w=P: np.asarray(a).reshape(-1, w).T

    def tall(a):
        return np.concatenate([np.asarray(a), np.zeros(2 * P - DC, np.float32)]).reshape(2, P).T

    g = lambda n: np.asarray(i[n])

    def per_layer(a):
        return a.reshape(LAYERS, -1, P, a.shape[-1]).transpose(0, 2, 1, 3).reshape(LAYERS, P, -1)

    layer_parts = {
        "norm": per_layer(g("L1_xattn_norm_w")[..., None]), "conv_b": per_layer(g("L1_xattn_conv_b")[..., None]),
        "conv_w": per_layer(g("L1_xattn_conv_w")), "dt_b": per_layer(g("L1_xattn_dt_proj_b")[..., None]),
        "D": per_layer(g("L1_xattn_D_param")[..., None]), "A_log": per_layer(g("L1_xattn_A_log")),
    }
    parts = {
        "bo1": cols(g("L0_xattn_bo1")), "bo2": cols(g("L0_xattn_bo2")), "bp": cols(g("L0_xattn_bp")),
        "b2_0": cols(g("L0_xattn_b2")), "g1": cols(g("L0_xattn_g1")), "be1": cols(g("L0_xattn_be1")),
        "g2": cols(g("L0_xattn_g2")), "be2": cols(g("L0_xattn_be2")), "g3": cols(g("L0_xattn_g3")),
        "be3": cols(g("L0_xattn_be3")),
        "final": cols(g("L1_xattn_final_norm_w")), "l1w": cols(g("L2_xattn_ln1_w")), "l1b": cols(g("L2_xattn_ln1_b")),
        "l2w": tall(g("L2_xattn_ln2_w")), "l2b": tall(g("L2_xattn_ln2_b")), "l3w": cols(g("L2_xattn_ln3_w")),
        "l3b": cols(g("L2_xattn_ln3_b")), "bproj": cols(g("L2_xattn_bproj")), "b1": cols(g("L2_xattn_b1")),
        "b2_2": cols(g("L2_xattn_b2")), "bq": cols(g("L3_xattn_bq")), "bk": cols(g("L3_xattn_bk")),
        "bv": cols(g("L3_xattn_bv")), "bd": cols(g("L3_xattn_bd")), "gq": cols(g("L3_xattn_g_q")),
        "beq": cols(g("L3_xattn_be_q")), "gkv": tall(g("L3_xattn_g_kv")), "bekv": tall(g("L3_xattn_be_kv")),
    }
    a = {
        "xT": g("x").transpose(2, 0, 1), "ctxT": g("ctx_768").transpose(2, 0, 1).reshape(DC, B * M),
        "layer_vec": np.concatenate([layer_parts[n] for n in LW], axis=2),
        "vec": np.concatenate([parts[n] for n, _ in VEC_SIZES], axis=1),
        "in_w": g("L1_xattn_in_proj_w").transpose(0, 2, 1), "x_w": g("L1_xattn_x_proj_w").transpose(0, 2, 1),
        "dt_w": g("L1_xattn_dt_proj_w").transpose(0, 2, 1), "out_w": g("L1_xattn_out_proj_w").transpose(0, 2, 1),
        "L3_Wq": g("L3_xattn_Wq").T, "L3_Wk": g("L3_xattn_Wk").T, "L3_Wv": g("L3_xattn_Wv").T, "L3_Wd": g("L3_xattn_Wd").T,
    }
    for n in ["L0_xattn_" + w for w in ("Wq1", "Wk1", "Wv1", "Wo1", "Wq2", "Wk2", "Wv2", "Wo2", "Wp", "W2")] + \
            ["L1_xattn_pre_w1", "L1_xattn_pre_w2"] + ["L2_xattn_" + w for w in ("Wq", "Wkv", "Wproj", "W1", "W2")]:
        a[n] = g(n)
    return {n: np.ascontiguousarray(x) for n, x in a.items()}


def kernel(**inputs):
    import concourse.bacc as bacc
    from concourse.bass_utils import run_bass_kernel_spmd

    nc = bacc.Bacc("TRN2", target_bir_lowering=False, num_devices=1)
    arrays = layouts(inputs)
    dram = {n: nc.dram_tensor(f"in_{n}", a.shape, F32, kind="ExternalInput").ap() for n, a in arrays.items()}
    out = nc.dram_tensor("out_T", (D, B, T), F32, kind="ExternalOutput").ap()
    build(nc, dram, out)
    r = run_bass_kernel_spmd(nc, [{f"in_{n}": a for n, a in arrays.items()}], core_ids=[0])
    return r.results[0]["out_T"].transpose(1, 2, 0)
```

```python
from contextlib import ExitStack

import concourse.bass as bass
from concourse import mybir

F32 = mybir.dt.float32
ALU = mybir.AluOpType
ACT = mybir.ActivationFunctionType
AX = mybir.AxisListType

P = 128
B, T, D, DC = 8, 512, 256, 192
PRE, S1 = 64, 576
KD = D // P
M = 64
H0, DH0 = 16, 64
INNER = H0 * DH0
HID = 4 * D
LAYERS, DI, DS, DTR, TAPS = 4, 512, 16, 16, 4
KI = DI // P
EPS = 1e-5
TC = 192
NCH = S1 // TC
CROWS = (P, DC - P)

VEC_SIZES = [
    ("bo1", 2), ("bo2", 2), ("bp", 16), ("b2_0", 2), ("g1", 2), ("be1", 2), ("g2", 2), ("be2", 2), ("g3", 2), ("be3", 2),
    ("final", 2),
    ("l1w", 2), ("l1b", 2), ("l2w", 2), ("l2b", 2), ("l3w", 2), ("l3b", 2), ("bproj", 2), ("b1", 8), ("b2_2", 2),
    ("bq", 2), ("bk", 2), ("bv", 2), ("bd", 2), ("gq", 2), ("beq", 2), ("gkv", 2), ("bekv", 2),
]
VEC = {}
_at = 0
for _n, _c in VEC_SIZES:
    VEC[_n] = (_at, _c)
    _at += _c
NVEC = _at


class Count:

    def __init__(self, n=0):
        self.before, self.n = 0, n

    def __call__(self, ahead=0):
        return self.before + (self.n + ahead)

    def add(self, k=1):
        self.n += k

    def round(self, i, share, start=0):
        self.before, self.n = i * share + start, 0


class Core:

    def __init__(self, nc, ctx, dram):
        self.nc, self.ctx, self.dram = nc, ctx, dram
        sb = lambda name, shape: ctx.enter_context(nc.sbuf_tensor(name, shape, F32))
        self.X = sb("X", [P, KD, B, S1])
        self.C = sb("C", [P, 2, B * M])
        self.vec = sb("vec", [P, NVEC])
        self.ident = sb("ident", [P, P])
        self.mean_d = sb("mean_d", [P, P])
        self.mean_c = sb("mean_c", [P, P])
        self.weights = [sb("weights0", [P, 8192]), sb("weights1", [P, 8192])]
        self.work = sb("work", [P, 25728])
        self.banks = ctx.enter_context(nc.psum_tensor("banks", [P, 8, 512], F32))
        self.lane_v, self.lane_s = self.banks[:, 6, :], self.banks[:, 7, :]
        self.eps = sb("eps", [P, 1])
        self.one = sb("one", [P, KI])
        self.const_ready = self.sem("const_ready")
        self.loaded = self.sem("loaded")
        self.w_loaded = [self.sem("w0_loaded"), self.sem("w1_loaded")]
        self.context_lanes, self.context_norm = Lanes(self, "context"), Norm(self, "context")
        self.w_count = [0, 0]

    def sem(self, name):
        return self.ctx.enter_context(self.nc.semaphore(name))

    def v(self, name, j=0, n=1):
        at = VEC[name][0] + j
        return self.vec[:, at:at + n]

    def area(self, at, *shape):
        n = 1
        for s in shape:
            n *= s
        names = "abcd"[:len(shape)]
        view = self.work[:, at:at + n]
        if len(shape) > 1:
            view = view.rearrange(f"p ({' '.join(names)}) -> p {' '.join(names)}", **dict(zip(names[1:], shape[1:])))
        return view, at + n


def wview(core, side, at, rows, n):
    return core.weights[side][:, at:at + rows * n].rearrange("p (k n) -> p k n", k=rows)


class Lanes:

    def __init__(self, core, stage):
        self.v_full, self.v_free = core.sem(f"{stage}_v_full"), core.sem(f"{stage}_v_free")
        self.s_full, self.s_free = core.sem(f"{stage}_s_full"), core.sem(f"{stage}_s_free")


class Norm:

    def __init__(self, core, stage):
        self.squared = core.sem(f"{stage}_squared")
        self.rstd = core.sem(f"{stage}_rstd")
        self.scaled = core.sem(f"{stage}_scaled")
        self.ready = core.sem(f"{stage}_normed")


def load_weights(e, core, side, parts):
    for at, src in parts:
        rows, cols = src.shape
        full = rows // P
        for k in range(0, full, 4):
            m = min(4, full - k)
            e.dma_start(wview(core, side, at + k * cols, m, cols), src[k * P:(k + m) * P, :].rearrange("(k p) n -> p k n", p=P)) \
                .then_inc(core.w_loaded[side], 16)
            core.w_count[side] += 16
        if rows % P:
            e.dma_start(core.weights[side][0:rows % P, at + full * cols:at + (full + 1) * cols], src[full * P:rows, :]) \
                .then_inc(core.w_loaded[side], 16)
            core.w_count[side] += 16



def norm_mean_pe(e, core, ln, V, x, mean, N):
    e.wait_ge(ln.v_free, V())
    for k, (r, ap) in enumerate(x):
        mm = e.matmul(core.lane_v[:, 0:N], mean[0:r, :], ap, start=(k == 0), stop=(k == len(x) - 1))
    mm.then_inc(ln.v_full, 1)
    V.add()


def norm_variance_pe(e, core, nm, ln, S, n, x, mean, squared, N):
    e.wait_ge(ln.s_free, S())
    e.wait_ge(nm.squared, n + 1)
    for k, (r, _) in enumerate(x):
        mm = e.matmul(core.lane_s[:, 0:N], mean[0:r, :], squared[0:r, k, :], start=(k == 0), stop=(k == len(x) - 1))
    mm.then_inc(ln.s_full, 1)
    S.add()


def norm_centre_dve(e, core, ln, V, x, centred, N):
    e.wait_ge(ln.v_full, V(1))
    for k, (r, ap) in enumerate(x):
        last = e.tensor_tensor(centred[0:r, k, :], ap, core.lane_v[0:r, 0:N], ALU.subtract)
    last.then_inc(ln.v_free, 1)
    V.add()


def norm_scale_dve(e, core, nm, ln, s_done, n, rows, centred, std, out, g):
    e.wait_ge(ln.s_free, s_done)
    e.reciprocal(std, std).then_inc(nm.rstd, 1)
    e.wait_ge(nm.rstd, n + 1)
    for k, r in enumerate(rows):
        last = e.scalar_tensor_tensor(out=out[0:r, k, :], in0=centred[0:r, k, :], scalar=core.v(g, k)[0:r, :],
                                      in1=std[0:r, :], op0=ALU.mult, op1=ALU.mult)
    last.then_inc(nm.scaled, 1)


def norm_square_act(e, nm, ln, v_done, rows, centred, squared):
    e.wait_ge(ln.v_free, v_done)
    for k, r in enumerate(rows):
        last = e.activation(squared[0:r, k, :], centred[0:r, k, :], ACT.Square)
    last.then_inc(nm.squared, 1)


def norm_root_act(e, core, ln, S, std, N):
    e.wait_ge(ln.s_full, S(1))
    e.activation(std, core.lane_s[:, 0:N], ACT.Sqrt, bias=core.eps[:]).then_inc(ln.s_free, 1)
    S.add()


def norm_bias_act(e, core, nm, n, rows, out, be):
    e.wait_ge(nm.scaled, n + 1)
    for k, r in enumerate(rows):
        last = e.activation(out[0:r, k, :], out[0:r, k, :], ACT.Identity, bias=core.v(be, k)[0:r, :])
    last.then_inc(nm.ready, 1)



def norm_pe(e, core, nm, ln, V, S, n, x, mean, squared, N):
    norm_mean_pe(e, core, ln, V, x, mean, N)
    norm_variance_pe(e, core, nm, ln, S, n, x, mean, squared, N)


def norm_dve(e, core, nm, ln, V, S, n, x, centred, std, out, g, N):
    norm_centre_dve(e, core, ln, V, x, centred, N)
    S.add()
    norm_scale_dve(e, core, nm, ln, S(), n, [r for r, _ in x], centred, std, out, g)


def norm_act(e, core, nm, ln, V, S, n, rows, centred, squared, std, out, be, N):
    V.add()
    norm_square_act(e, nm, ln, V(), rows, centred, squared)
    norm_root_act(e, core, ln, S, std, N)
    norm_bias_act(e, core, nm, n, rows, out, be)


def batches(e, body):
    with e.Fori(0, B - 1) as b:
        body(b, True)
    body(B - 1, False)


def batches_apart(e, body):
    body(0, False, True)
    with e.Fori(1, B - 1) as b:
        body(b, True, True)
    body(B - 1, True, False)


UNITS = 2
LAG = 2
PAIRS = H0 // 2


def self_attention(core):
    at = 0
    normed, at = core.area(at, KD, T)
    centred, at = core.area(at, KD, T)
    squared, at = core.area(at, KD, T)
    std, at = core.area(at, T)
    q, at = core.area(at, 8, T)
    k_, at = core.area(at, 8, T)
    v_, at = core.area(at, 4, INNER)
    probs, at = core.area(at, 4, 2, T)
    probsT, at = core.area(at, 2, 4, T)
    nmax, at = core.area(at, 4, 2)
    sums, at = core.area(at, 4, 2)
    rsum, at = core.area(at, 4, 2)
    wq, wk, wv, wo = (wview(core, 0, 2048 * j, 2 if j < 3 else 8, INNER if j < 3 else D) for j in range(4))
    ln, nm = Lanes(core, "self"), Norm(core, "self")
    s_full = core.sem("self_scores")
    nmax_ready = core.sem("self_nmax")
    exp_done = core.sem("self_exp")
    rsum_ready = core.sem("self_rsum")
    p_ready = core.sem("self_probs")
    t_full = core.sem("self_t_full")
    tv_free, ts_free = core.sem("self_tv_free"), core.sem("self_ts_free")
    x_in = lambda b: [(P, core.X[:, k, b, PRE:S1]) for k in range(KD)]
    rows = [P] * KD
    MEAN_HEAD, VARIANCE_HEAD = 4, 8
    V_SHARE, S_SHARE = 12 + PAIRS // 2 + 1 + 2, 12 + PAIRS // 2 + 1
    v_done = lambda b: b * V_SHARE + (1 + 12 + MEAN_HEAD // 4 + 1)
    s_done = lambda b: b * S_SHARE + (1 + 12 + VARIANCE_HEAD // 4 + 1)

    with core.nc.Block() as block:
        @block.sync
        def _(e):
            d = core.dram
            load_weights(e, core, 1, [(0, d["L0_xattn_Wq2"]), (2048, d["L0_xattn_Wk2"]), (4096, d["L0_xattn_Wv2"]),
                                      (6144, d["L0_xattn_Wo2"])])

        @block.tensor
        def _(e):
            V, S = Count(), Count()
            e.wait_ge(core.const_ready, CONSTS)
            e.wait_ge(core.loaded, LOADS)
            e.wait_ge(core.w_loaded[0], core.w_count[0])
            norm_pe(e, core, nm, ln, V, S, 0, x_in(0), core.mean_d, squared, T)

            def body(b, more):
                V.round(b, V_SHARE, 1)
                S.round(b, S_SHARE, 1)
                lanes = lanes_of(core, ln, V, S)
                e.wait_ge(nm.ready, b + 1)
                for w in (wq, wk):
                    for m in range(8):
                        lane, free, full, c = lanes[m % 2]
                        e.wait_ge(free, c())
                        for k in range(KD):
                            mm = e.matmul(lane, w[:, k, m * P:(m + 1) * P], normed[:, k, :], start=(k == 0), stop=(k == KD - 1))
                        mm.then_inc(full, 1)
                        c.add()
                for t in range(4):
                    for half in range(2):
                        lane, free, full, c = lanes[half]
                        e.wait_ge(free, c())
                        for k in range(KD):
                            mm = e.matmul(lane, normed[:, k, t * P:(t + 1) * P], wv[:, k, half * 512:half * 512 + 512],
                                          start=(k == 0), stop=(k == KD - 1))
                        mm.then_inc(full, 1)
                        c.add()
                e.wait_ge(ln.v_free, V())
                e.wait_ge(ln.s_free, S())
                for h in range(H0 + LAG):
                    g = h - LAG
                    for u in range(UNITS):
                        if g >= 0:
                            e.wait_ge(p_ready, b * (H0 * UNITS) + (g * UNITS + u + 1))
                            for j in range(2):
                                e.wait_ge((tv_free, ts_free)[j], b * (2 * H0) + (2 * g + u))
                                for kt in range(4):
                                    mm = e.transpose(core.banks[:, 4 + j, kt * P:(kt + 1) * P],
                                                     probs[:, 2 * (g % 2) + u, j, kt * P:(kt + 1) * P], core.ident[:])
                                mm.then_inc(t_full, 1)
                        if h < H0:
                            r = DH0 * (h % 2)
                            if h > 0:
                                e.wait_ge(exp_done, b * (H0 * UNITS) + ((h - 1) * UNITS + (u + 1)))
                            for j in range(2):
                                t = 2 * u + j
                                mm = e.matmul(core.banks[:, t, :], q[r:r + DH0, h // 2, t * P:(t + 1) * P],
                                              k_[r:r + DH0, h // 2, :], start=True, stop=True)
                            mm.then_inc(s_full, 1)
                    if g < 0:
                        continue
                    if more and g == MEAN_HEAD:
                        norm_mean_pe(e, core, ln, V, x_in(b + 1), core.mean_d, T)
                    if more and g == VARIANCE_HEAD:
                        norm_variance_pe(e, core, nm, ln, S, b + 1, x_in(b + 1), core.mean_d, squared, T)
                    if g % 2 == 1:
                        e.wait_ge(tv_free, b * (2 * H0) + 2 * (g + 1))
                        e.wait_ge(ts_free, b * (2 * H0) + 2 * (g + 1))
                        lane, free, full, c = lanes[g // 2 % 2]
                        e.wait_ge(free, c())
                        for kt in range(4):
                            for f in (g - 1, g):
                                r = DH0 * (f % 2)
                                mm = e.matmul(lane[r:r + DH0, :], v_[:, kt, f * DH0:(f + 1) * DH0], probsT[:, f % 2, kt, :],
                                              start=(kt == 0), stop=(kt == 3))
                        mm.then_inc(full, 1)
                        c.add()
                e.wait_ge(ln.v_free, V())
                e.wait_ge(ln.s_free, S())
                for m in range(KD):
                    e.wait_ge(ln.v_free, V())
                    for k in range(8):
                        mm = e.matmul(core.lane_v, wo[:, k, m * P:(m + 1) * P], q[:, k, :], start=(k == 0), stop=(k == 7))
                    mm.then_inc(ln.v_full, 1)
                    V.add()

            batches(e, body)

        @block.vector
        def _(e):
            V, S = Count(), Count()
            e.wait_ge(core.loaded, LOADS)
            norm_dve(e, core, nm, ln, V, S, 0, x_in(0), centred, std, normed, "g1", T)

            def body(b, more):
                V.round(b, V_SHARE, 1)
                for w in range(2):
                    for m in range(0, 8, 2):
                        e.wait_ge(ln.v_full, V(1))
                        if w == 0:
                            e.tensor_scalar(q[:, m, :], core.lane_v, DH0 ** -0.5, None, ALU.mult).then_inc(ln.v_free, 1)
                        else:
                            e.tensor_copy(k_[:, m, :], core.lane_v).then_inc(ln.v_free, 1)
                        V.add()
                for t in range(4):
                    e.wait_ge(ln.v_full, V(1))
                    e.tensor_copy(v_[:, t, 0:512], core.lane_v).then_inc(ln.v_free, 1)
                    V.add()
                for h in range(H0 + LAG):
                    g = h - LAG
                    for u in range(UNITS):
                        if g >= 0:
                            t = 2 * u
                            e.wait_ge(t_full, b * (4 * H0) + (4 * g + t + 1))
                            e.tensor_copy(probsT[:, g % 2, :, t * P:(t + 1) * P],
                                          core.banks[:, 4, :].rearrange("p (k q) -> p k q", k=4)).then_inc(tv_free, 1)
                        if h < H0:
                            n = b * (H0 * UNITS) + (h * UNITS + u)
                            e.wait_ge(s_full, n + 1)
                            e.tensor_reduce(nmax[:, 2 * (h % 2) + u, :], core.banks[:, 2 * u:2 * u + 2, :], AX.X, ALU.max,
                                            negate=True).then_inc(nmax_ready, 1)
                        if 0 < h <= H0:
                            n = b * (H0 * UNITS) + ((h - 1) * UNITS + u)
                            slot = 2 * ((h - 1) % 2) + u
                            e.wait_ge(exp_done, n + 1)
                            e.reciprocal(rsum[:, slot, :], sums[:, slot, :]).then_inc(rsum_ready, 1)
                            e.wait_ge(rsum_ready, n + 1)
                            for j in range(2):
                                last = e.tensor_scalar(probs[:, slot, j, :], probs[:, slot, j, :], rsum[:, slot, j:j + 1],
                                                       None, ALU.mult)
                            last.then_inc(p_ready, 1)
                    if g >= 0 and g % 4 == 1:
                        e.wait_ge(ln.v_full, V(1))
                        e.tensor_copy(q[:, g // 2, :], core.lane_v).then_inc(ln.v_free, 1)
                        V.add()
                    if more and g == MEAN_HEAD:
                        norm_centre_dve(e, core, ln, V, x_in(b + 1), centred, T)
                    if more and g == VARIANCE_HEAD + 2:
                        norm_scale_dve(e, core, nm, ln, s_done(b), b + 1, rows, centred, std, normed, "g1")
                for m in range(KD):
                    e.wait_ge(ln.v_full, V(1))
                    x = core.X[:, m, b, PRE:S1]
                    e.scalar_tensor_tensor(out=x, in0=core.lane_v, scalar=core.v("bo1", m), in1=x,
                                           op0=ALU.add, op1=ALU.add).then_inc(ln.v_free, 1)
                    V.add()

            batches(e, body)

        @block.scalar
        def _(e):
            V, S = Count(), Count()
            e.wait_ge(core.loaded, LOADS)
            e.wait_ge(core.const_ready, CONSTS)
            norm_act(e, core, nm, ln, V, S, 0, rows, centred, squared, std, normed, "be1", T)

            def body(b, more):
                S.round(b, S_SHARE, 1)
                for w in range(2):
                    for m in range(1, 8, 2):
                        e.wait_ge(ln.s_full, S(1))
                        e.activation((q, k_)[w][:, m, :], core.lane_s, ACT.Copy, scale=(DH0 ** -0.5, 1.0)[w]).then_inc(ln.s_free, 1)
                        S.add()
                for t in range(4):
                    e.wait_ge(ln.s_full, S(1))
                    e.activation(v_[:, t, 512:1024], core.lane_s, ACT.Copy).then_inc(ln.s_free, 1)
                    S.add()
                for h in range(H0 + LAG):
                    g = h - LAG
                    if g >= 0:
                        for t in (1, 3):
                            e.wait_ge(t_full, b * (4 * H0) + (4 * g + t + 1))
                            e.activation(probsT[:, g % 2, :, t * P:(t + 1) * P],
                                         core.banks[:, 5, :].rearrange("p (k q) -> p k q", k=4), ACT.Copy).then_inc(ts_free, 1)
                    if h < H0:
                        for u in range(UNITS):
                            n = b * (H0 * UNITS) + (h * UNITS + u)
                            slot = 2 * (h % 2) + u
                            e.wait_ge(nmax_ready, n + 1)
                            for j in range(2):
                                last = e.activation(probs[:, slot, j, :], core.banks[:, 2 * u + j, :], ACT.Exp,
                                                    bias=nmax[:, slot, j:j + 1],
                                                    accum_out=sums[:, slot, j:j + 1])
                            last.then_inc(exp_done, 1)
                    if g >= 0 and g % 4 == 3:
                        e.wait_ge(ln.s_full, S(1))
                        e.activation(q[:, g // 2, :], core.lane_s, ACT.Copy).then_inc(ln.s_free, 1)
                        S.add()
                    if more and g == MEAN_HEAD + 1:
                        norm_square_act(e, nm, ln, v_done(b), rows, centred, squared)
                    if more and g == VARIANCE_HEAD + 1:
                        norm_root_act(e, core, ln, S, std, T)
                    if more and g == VARIANCE_HEAD + 4:
                        norm_bias_act(e, core, nm, b + 1, rows, normed, "be1")

            batches(e, body)


def lanes_of(core, ln, V, S):
    return ((core.lane_v, ln.v_free, ln.v_full, V), (core.lane_s, ln.s_free, ln.s_full, S))


def norm_context(core, nth, g, be, out, squared, std):
    ln, nm = core.context_lanes, core.context_norm
    x = [(r, core.C[0:r, k, :]) for k, r in enumerate(CROWS)]
    N = B * M
    counts = lambda: (Count(nth), Count(nth))
    with core.nc.Block() as block:
        @block.tensor
        def _(e):
            norm_pe(e, core, nm, ln, *counts(), nth, x, core.mean_c, squared, N)

        @block.vector
        def _(e):
            norm_dve(e, core, nm, ln, *counts(), nth, x, out, std, out, g, N)

        @block.scalar
        def _(e):
            norm_act(e, core, nm, ln, *counts(), nth, CROWS, out, squared, std, out, be, N)


def cross_attention(core, name, side, weights, heads, width, norm, bias, ctx_norm, prefetch):
    hpt, inner = P // width, heads * width
    tiles, chunks = inner // P, heads // 2
    per_tile = chunks // tiles
    QT = T // P
    at = 0
    normed, at = core.area(at, KD, T)
    centred, at = core.area(at, KD, T)
    squared, at = core.area(at, KD, T)
    std, at = core.area(at, T)
    q, at = core.area(at, tiles, T)
    mixed, at = core.area(at, tiles, T)
    probs, at = core.area(at, QT, heads * M)
    probsT, at = core.area(at, chunks, T)
    kblk, at = core.area(at, tiles, hpt * M)
    vblk, at = core.area(at, chunks, P)
    kmask, at = core.area(at, hpt, M)
    vmask, at = core.area(at, per_tile, P)
    ctx2, at = core.area(at, 2, 2, M)
    rowmax, at = core.area(at, QT, heads)
    rowsum, at = core.area(at, QT, heads)
    if ctx_norm:
        context, at = core.area(at, 2, B * M)
        norm_context(core, 0, ctx_norm[0], ctx_norm[1], context, squared, std)
    else:
        context = core.C
    wq, wk, wv, wo = (wview(core, side, c, r, n) for c, r, n in weights)
    ln, nm = Lanes(core, name), Norm(core, name)
    masks_ready, vmask_ready = core.sem(f"{name}_kmask"), core.sem(f"{name}_vmask")
    ctx_ready = core.sem(f"{name}_ctx_ready")
    s_full = core.sem(f"{name}_scores")
    max_done, shifted = core.sem(f"{name}_max"), core.sem(f"{name}_shifted")
    exp_done = core.sem(f"{name}_exp")
    sum_done, rsum_ready = core.sem(f"{name}_sum"), core.sem(f"{name}_rsum")
    p_ready = core.sem(f"{name}_probs")
    t_full = core.sem(f"{name}_t_full")
    tv_free, ts_free = core.sem(f"{name}_tv_free"), core.sem(f"{name}_ts_free")
    V_GROUPS = inner // 512 if inner > 512 else 1
    v_cols = inner // V_GROUPS
    V_SHARE, S_SHARE = 1 + 1 + V_GROUPS + tiles + 2, 1 + tiles
    BEFORE = 1 + 1 + V_GROUPS
    v_start = lambda b: b * V_SHARE + (BEFORE - KD) if not isinstance(b, int) or b > 0 else BEFORE
    v_done = lambda b: v_start(b) + (tiles // 2 + 1)
    s_done = lambda b: b * S_SHARE + (1 + tiles // 2 + 1)
    v_round = lambda V, b: V.round(b, V_SHARE, BEFORE - KD) if not isinstance(b, int) or b > 0 else V.round(0, V_SHARE, BEFORE)
    rows = [P] * KD
    T_BANK = (4, 0, 2, 4)
    banks = core.banks
    out_bank = lambda m: ((core.lane_v, banks[:, 0, :]), (core.lane_s, banks[:, 1, :]))[m % 2][m // 2 % 2]
    k_bank, v_bank = banks[:, 2, :], (banks[:, 3, :], banks[:, 4, :])
    x_in = lambda b: [(P, core.X[:, k, b, PRE:S1]) for k in range(KD)]

    with core.nc.Block() as block:
        @block.sync
        def _(e):
            prefetch(e)

        @block.gpsimd
        def _(e):
            e.memset(kmask, 1.0).then_inc(masks_ready, 1)
            e.wait_ge(masks_ready, 1)
            e.affine_select(out=kmask, in_=kmask, compare_op=ALU.is_ge, fill=0.0, base=0,
                            pattern=[[-width, hpt], [0, M]], channel_multiplier=1).then_inc(masks_ready, 1)
            e.wait_ge(masks_ready, 2)
            e.affine_select(out=kmask, in_=kmask, compare_op=ALU.is_ge, fill=0.0, base=width - 1,
                            pattern=[[width, hpt], [0, M]], channel_multiplier=-1).then_inc(masks_ready, 1)

            def bring_context(b):
                for j in range(2):
                    for k, r in enumerate(CROWS):
                        own = context[0:r, k, bass.ts(b, M)]
                        last = e.tensor_tensor(ctx2[0:r, k, j, :], own, core.one[0:r, 0:1].to_broadcast([r, M]), ALU.mult)
                last.then_inc(ctx_ready, 1)

            bring_context(0)

            def body(b, earlier, more):
                if more:
                    e.wait_ge(ln.v_free, v_start(b))
                    bring_context(b + 1)
                for t in range(QT):
                    view = probs[:, t, :].rearrange("p (h m) -> p h m", h=heads)
                    e.wait_ge(rsum_ready, b * QT + (t + 1))
                    e.tensor_tensor(view, view, rowsum[:, t, :].unsqueeze(2).to_broadcast([P, heads, M]), ALU.mult) \
                        .then_inc(p_ready, 1)

            batches_apart(e, body)

        @block.tensor
        def _(e):
            V, S = Count(), Count()
            e.wait_ge(core.w_loaded[side], core.w_count[side])
            norm_pe(e, core, nm, ln, V, S, 0, x_in(0), core.mean_d, squared, T)

            def project_context(b):
                e.wait_ge(ctx_ready, b + 1)
                for m in range(tiles):
                    for k, r in enumerate(CROWS):
                        mm = e.matmul(k_bank[:, m * M:(m + 1) * M], wk[0:r, k, m * P:(m + 1) * P],
                                      ctx2[0:r, k, 0, :], start=(k == 0), stop=(k == 1))
                mm.then_inc(ln.v_full, 1)
                V.add()
                for g in range(V_GROUPS):
                    for k, r in enumerate(CROWS):
                        mm = e.matmul(v_bank[g][:, 0:v_cols], ctx2[0:r, k, :, :].rearrange("p a m -> p (a m)"),
                                      wv[0:r, k, g * v_cols:(g + 1) * v_cols], start=(k == 0), stop=(k == 1))
                    mm.then_inc(ln.v_full, 1)
                    V.add()

            project_context(0)

            def project_out(m):
                e.wait_ge(ln.v_free, V())
                e.wait_ge(ln.s_free, S())
                for k in range(tiles):
                    mm = e.matmul(core.lane_v, wo[:, k, m * P:(m + 1) * P], mixed[:, k, :], start=(k == 0), stop=(k == tiles - 1))
                mm.then_inc(ln.v_full, 1)
                V.add()

            def body(b, earlier, more):
                v_round(V, b)
                S.round(b, S_SHARE, 1)
                lanes = lanes_of(core, ln, V, S)
                e.wait_ge(nm.ready, b + 1)
                for m in range(tiles):
                    lane, free, full, c = lanes[m % 2]
                    e.wait_ge(free, c())
                    for k in range(KD):
                        mm = e.matmul(lane, wq[:, k, m * P:(m + 1) * P], normed[:, k, :], start=(k == 0), stop=(k == KD - 1))
                    mm.then_inc(full, 1)
                    c.add()
                e.wait_ge(ln.v_free, V())
                e.wait_ge(ln.s_free, S())
                for i in range(QT):
                    if i >= 2:
                        e.wait_ge(shifted, b * QT + (i - 1))
                    for m in range(tiles):
                        c0 = m * hpt * M
                        mm = e.matmul(banks[:, 2 * (i % 2) + c0 // 512, c0 % 512:c0 % 512 + hpt * M],
                                      q[:, m, i * P:(i + 1) * P], kblk[:, m, :], start=True, stop=True)
                    mm.then_inc(s_full, 1)
                    if more and i == 1:
                        norm_mean_pe(e, core, ln, V, x_in(b + 1), core.mean_d, T)
                    if more and i == 3:
                        norm_variance_pe(e, core, nm, ln, S, b + 1, x_in(b + 1), core.mean_d, squared, T)
                for t in range(QT):
                    if earlier and t in (0, 2):
                        project_out(t // 2)
                    e.wait_ge(p_ready, b * QT + (t + 1))
                    if t in (1, 2):
                        e.wait_ge(shifted, b * QT + (t + 2))
                    if t == 3:
                        e.wait_ge(tv_free, b * QT + 1)
                        e.wait_ge(ts_free, b * QT + 1)
                    for c in range(chunks):
                        mm = e.transpose(banks[:, T_BANK[t] + c // 4, c % 4 * P:(c % 4 + 1) * P],
                                         probs[:, t, c * P:(c + 1) * P], core.ident[:])
                    mm.then_inc(t_full, 1)
                e.wait_ge(tv_free, b * QT + QT)
                e.wait_ge(ts_free, b * QT + QT)
                for m in range(tiles):
                    _, free, full, c = lanes[m % 2]
                    if m // 2 != 1:
                        e.wait_ge(free, c(-1 if m // 2 > 1 else 0))
                    for j in range(per_tile):
                        mm = e.matmul(out_bank(m), vblk[:, m * per_tile + j, :], probsT[:, m * per_tile + j, :],
                                      start=(j == 0), stop=(j == per_tile - 1))
                    mm.then_inc(full, 1)
                    c.add()
                if more:
                    project_context(b + 1)

            batches_apart(e, body)
            for m in range(KD):
                project_out(m)

        @block.vector
        def _(e):
            V, S = Count(), Count()
            e.memset(vmask, 0.0).then_inc(vmask_ready, 1)
            e.wait_ge(vmask_ready, 1)
            for h in range(2):
                for c in range(per_tile):
                    f = (2 * c + h) * width
                    last = e.memset(vmask[h * M:(h + 1) * M, c, f:f + width], 1.0)
            last.then_inc(vmask_ready, 1)
            e.wait_ge(vmask_ready, 2)
            e.wait_ge(masks_ready, 3)
            norm_dve(e, core, nm, ln, V, S, 0, x_in(0), centred, std, normed, norm[0], T)

            def spread_context():
                e.wait_ge(ln.v_full, V(1))
                e.tensor_tensor(kblk.rearrange("p t (h m) -> p t h m", h=hpt),
                                k_bank[:, 0:tiles * M].rearrange("p (t m) -> p t m", t=tiles).unsqueeze(2)
                                .to_broadcast([P, tiles, hpt, M]),
                                kmask.unsqueeze(1).to_broadcast([P, tiles, hpt, M]), ALU.mult).then_inc(ln.v_free, 1)
                V.add()
                for g in range(V_GROUPS):
                    gt = v_cols // P
                    shape = [P, gt, per_tile, P]
                    e.wait_ge(ln.v_full, V(1))
                    e.tensor_tensor(vblk[:, g * gt * per_tile:(g + 1) * gt * per_tile, :].rearrange("p (t c) f -> p t c f", t=gt),
                                    v_bank[g][:, 0:v_cols].rearrange("p (t f) -> p t f", t=gt).unsqueeze(2).to_broadcast(shape),
                                    vmask.unsqueeze(1).to_broadcast(shape), ALU.mult).then_inc(ln.v_free, 1)
                    V.add()

            spread_context()

            def residual(b, m):
                e.wait_ge(ln.v_full, V(1))
                x = core.X[:, m, b, PRE:S1]
                e.scalar_tensor_tensor(out=x, in0=core.lane_v, scalar=core.v(bias, m), in1=x, op0=ALU.add, op1=ALU.add) \
                    .then_inc(ln.v_free, 1)
                V.add()

            def body(b, earlier, more):
                v_round(V, b)
                for m in range(0, tiles, 2):
                    e.wait_ge(ln.v_full, V(1))
                    e.tensor_scalar(q[:, m, :], core.lane_v, width ** -0.5, None, ALU.mult).then_inc(ln.v_free, 1)
                    V.add()
                for i in range(QT + 1):
                    if i < QT:
                        s = i
                        scores = core.banks[:, 2 * (i % 2):2 * (i % 2) + 2, :].rearrange("p a n -> p (a n)").rearrange("p (h m) -> p h m", h=heads)
                        e.wait_ge(s_full, b * QT + (i + 1))
                        e.tensor_reduce(rowmax[:, s, :], scores, AX.X, ALU.max).then_inc(max_done, 1)
                        e.wait_ge(max_done, b * QT + (i + 1))
                        e.tensor_tensor(probs[:, s, :].rearrange("p (h m) -> p h m", h=heads), scores,
                                        rowmax[:, s, :].unsqueeze(2).to_broadcast([P, heads, M]), ALU.subtract).then_inc(shifted, 1)
                    if 1 <= i <= QT:
                        t = i - 1
                        s = t
                        view = probs[:, s, :].rearrange("p (h m) -> p h m", h=heads)
                        e.wait_ge(exp_done, b * QT + (t + 1))
                        e.tensor_reduce(rowsum[:, s, :], view, AX.X, ALU.add).then_inc(sum_done, 1)
                        e.wait_ge(sum_done, b * QT + (t + 1))
                        e.reciprocal(rowsum[:, s, :], rowsum[:, s, :]).then_inc(rsum_ready, 1)
                    if more and i == 1:
                        norm_centre_dve(e, core, ln, V, x_in(b + 1), centred, T)
                for t in range(QT):
                    if earlier and t in (0, 2):
                        residual(b - 1, t // 2)
                    e.wait_ge(t_full, b * QT + (t + 1))
                    e.tensor_copy(probsT[:, 0:4, t * P:(t + 1) * P],
                                  banks[:, T_BANK[t], :].rearrange("p (c q) -> p c q", c=4)).then_inc(tv_free, 1)
                for m in range(0, tiles, 2):
                    e.wait_ge(ln.v_full, V(1))
                    e.tensor_copy(mixed[:, m, :], out_bank(m)).then_inc(ln.v_free, 1)
                    V.add()
                if more:
                    norm_scale_dve(e, core, nm, ln, s_done(b), b + 1, rows, centred, std, normed, norm[0])
                    spread_context()

            batches_apart(e, body)
            for m in range(KD):
                residual(B - 1, m)

        @block.scalar
        def _(e):
            V, S = Count(), Count()
            norm_act(e, core, nm, ln, V, S, 0, rows, centred, squared, std, normed, norm[1], T)

            def body(b, earlier, more):
                S.round(b, S_SHARE, 1)
                for m in range(1, tiles, 2):
                    e.wait_ge(ln.s_full, S(1))
                    e.activation(q[:, m, :], core.lane_s, ACT.Copy, scale=width ** -0.5).then_inc(ln.s_free, 1)
                    S.add()
                for i in range(QT):
                    e.wait_ge(shifted, b * QT + (i + 1))
                    e.activation(probs[:, i, :], probs[:, i, :], ACT.Exp).then_inc(exp_done, 1)
                    if more and i == 2:
                        norm_square_act(e, nm, ln, v_done(b), rows, centred, squared)
                    if more and i == 3:
                        norm_root_act(e, core, ln, S, std, T)
                for t in range(QT):
                    e.wait_ge(t_full, b * QT + (t + 1))
                    e.activation(probsT[:, 4:8, t * P:(t + 1) * P],
                                 banks[:, T_BANK[t] + 1, :].rearrange("p (c q) -> p c q", c=4), ACT.Copy).then_inc(ts_free, 1)
                for m in range(1, tiles, 2):
                    e.wait_ge(ln.s_full, S(1))
                    e.activation(mixed[:, m, :], out_bank(m), ACT.Copy).then_inc(ln.s_free, 1)
                    S.add()
                if more:
                    norm_bias_act(e, core, nm, b + 1, rows, normed, norm[1])

            batches_apart(e, body)


def cross_attention_0(core):
    d = core.dram
    cross_attention(core, "cross0", 1, [(0, 2, INNER), (2048, 2, INNER), (4096, 2, INNER), (6144, 8, D)], H0, DH0,
                    ("g2", "be2"), "bo2", None,
                    lambda e: load_weights(e, core, 0, [(0, d["L0_xattn_Wp"]), (4096, d["L0_xattn_W2"])]))


def feed_forward(core, name, side, w1, w2, norm, b1, b2, gated, prefetch):
    at = 0
    normed, at = core.area(at, KD, T)
    centred, at = core.area(at, KD, T)
    squared, at = core.area(at, KD, T)
    std, at = core.area(at, T)
    hidden, at = core.area(at, 8, T)
    gate, at = core.area(at, 2, T)
    ln, nm = Lanes(core, name), Norm(core, name)
    gelu_done = core.sem(f"{name}_gelu")
    V_SHARE, S_SHARE = (1 + 8 + 2, 1 + 8) if gated else (1 + 4 + 2, 1 + 4)
    x_in = lambda b: [(P, core.X[:, k, b, PRE:S1]) for k in range(KD)]
    if gated:
        groups = [g for m in range(8) for g in ((1, 8 + m), (0, m))]
    else:
        groups = [(m % 2, m) for m in range(8)]
    nth = lambda i: sum(which == groups[i][0] for which, _ in groups[:i])
    bank = lambda i: core.banks[:, 2 * groups[i][0] + nth(i) % 2, :]
    MEAN_AT, VARIANCE_AT = len(groups) // 4, len(groups) // 2
    before = lambda lane, i: sum(which == lane for which, _ in groups[:i])
    v_done = lambda b: b * V_SHARE + (1 + before(0, MEAN_AT) + 1)
    s_done = lambda b: b * S_SHARE + (1 + before(1, VARIANCE_AT) + 1)
    rows = [P] * KD

    with core.nc.Block() as block:
        @block.sync
        def _(e):
            prefetch(e)

        @block.tensor
        def _(e):
            V, S = Count(), Count()
            e.wait_ge(core.w_loaded[side], core.w_count[side])
            norm_pe(e, core, nm, ln, V, S, 0, x_in(0), core.mean_d, squared, T)

            def body(b, more):
                V.round(b, V_SHARE, 1)
                S.round(b, S_SHARE, 1)
                lanes = lanes_of(core, ln, V, S)
                e.wait_ge(nm.ready, b + 1)
                for i, (which, m) in enumerate(groups):
                    if more and i == MEAN_AT:
                        norm_mean_pe(e, core, ln, V, x_in(b + 1), core.mean_d, T)
                    if more and i == VARIANCE_AT:
                        norm_variance_pe(e, core, nm, ln, S, b + 1, x_in(b + 1), core.mean_d, squared, T)
                    _, free, full, c = lanes[which]
                    if nth(i) >= 2:
                        e.wait_ge(free, c(-1))
                    for k in range(KD):
                        mm = e.matmul(bank(i), w1[:, k, m * P:(m + 1) * P], normed[:, k, :], start=(k == 0), stop=(k == KD - 1))
                    mm.then_inc(full, 1)
                    c.add()
                e.wait_ge(ln.v_free, V())
                e.wait_ge(ln.s_free, S())
                if not gated:
                    e.wait_ge(gelu_done, 4 * b + 4)
                for m in range(KD):
                    for k in range(8):
                        mm = e.matmul((core.lane_v, core.banks[:, 4, :])[m], w2[:, k, m * P:(m + 1) * P], hidden[:, k, :], start=(k == 0), stop=(k == 7))
                    mm.then_inc(ln.v_full, 1)
                    V.add()

            batches(e, body)

        @block.vector
        def _(e):
            V, S = Count(), Count()
            norm_dve(e, core, nm, ln, V, S, 0, x_in(0), centred, std, normed, norm[0], T)

            def body(b, more):
                V.round(b, V_SHARE, 1)
                S.round(b, S_SHARE, 1)
                for i, (which, m) in enumerate(groups):
                    if more and i == MEAN_AT:
                        norm_centre_dve(e, core, ln, V, x_in(b + 1), centred, T)
                    if more and i == VARIANCE_AT:
                        S.add()
                    if which == 1:
                        S.add()
                        continue
                    e.wait_ge(ln.v_full, V(1))
                    if gated:
                        e.wait_ge(ln.s_free, S())
                        e.scalar_tensor_tensor(out=hidden[:, m, :], in0=bank(i), scalar=core.v(b1, m), in1=gate[:, m % 2, :],
                                               op0=ALU.add, op1=ALU.mult).then_inc(ln.v_free, 1)
                    else:
                        e.tensor_scalar(hidden[:, m, :], bank(i), core.v(b1, m), None, ALU.add).then_inc(ln.v_free, 1)
                    V.add()
                if more:
                    e.wait_ge(ln.s_full, S())
                    norm_scale_dve(e, core, nm, ln, s_done(b), b + 1, rows, centred, std, normed, norm[0])
                for m in range(KD):
                    e.wait_ge(ln.v_full, V(1))
                    x = core.X[:, m, b, PRE:S1]
                    e.scalar_tensor_tensor(out=x, in0=(core.lane_v, core.banks[:, 4, :])[m], scalar=core.v(b2, m), in1=x,
                                           op0=ALU.add, op1=ALU.add).then_inc(ln.v_free, 1)
                    V.add()

            batches(e, body)

        @block.scalar
        def _(e):
            V, S = Count(), Count()
            norm_act(e, core, nm, ln, V, S, 0, rows, centred, squared, std, normed, norm[1], T)

            def body(b, more):
                V.round(b, V_SHARE, 1)
                S.round(b, S_SHARE, 1)
                for i, (which, m) in enumerate(groups):
                    if more and i == MEAN_AT:
                        V.add()
                    if more and i == MEAN_AT + 1:
                        norm_square_act(e, nm, ln, v_done(b), rows, centred, squared)
                    if more and i == VARIANCE_AT:
                        norm_root_act(e, core, ln, S, std, T)
                    if which == 1:
                        e.wait_ge(ln.s_full, S(1))
                        if gated:
                            if m - 8 >= 2:
                                e.wait_ge(ln.v_free, V(-1))
                            to = gate[:, m % 2, :]
                        else:
                            to = hidden[:, m, :]
                        e.activation(to, bank(i), ACT.Gelu, bias=core.v(b1, m)).then_inc(ln.s_free, 1)
                        S.add()
                    else:
                        V.add()
                        if not gated:
                            e.wait_ge(ln.v_free, V())
                            e.activation(hidden[:, m, :], hidden[:, m, :], ACT.Gelu).then_inc(gelu_done, 1)
                if more:
                    norm_bias_act(e, core, nm, b + 1, rows, normed, norm[1])

            batches(e, body)


def feed_forward_0(core):
    d = core.dram
    feed_forward(core, "ff0", 0, wview(core, 0, 0, 2, 2048), wview(core, 0, 4096, 8, D), ("g3", "be3"), "bp", "b2_0", True,
                 lambda e: load_mamba(e, core, 0))


def cross_attention_2(core):
    cross_attention(core, "cross2", 0, [(0, 2, D), (512, 2, D), (1024, 2, D), (1536, 2, D)], 16, 16,
                    ("l1w", "l1b"), "bproj", ("l2w", "l2b"), lambda e: load_last(e, core))


def feed_forward_2(core):
    feed_forward(core, "ff2", 0, wview(core, 0, 2048, 2, HID), wview(core, 0, 4096, 8, D), ("l3w", "l3b"), "b1", "b2_2", False,
                 lambda e: None)


def load_second(e, core):
    d = core.dram
    kv = d["L2_xattn_Wkv"]
    load_weights(e, core, 0, [(0, d["L2_xattn_Wq"]), (512, kv[:, 0:D]), (1024, kv[:, D:2 * D]), (1536, d["L2_xattn_Wproj"]),
                              (2048, d["L2_xattn_W1"]), (4096, d["L2_xattn_W2"])])


def load_last(e, core):
    d = core.dram
    load_weights(e, core, 1, [(0, d["L3_Wq"]), (512, d["L3_Wk"]), (1024, d["L3_Wv"]), (1536, d["L3_Wd"])])


def last_attention(core):
    at = 0
    normed, at = core.area(at, KD, T)
    centred, at = core.area(at, KD, T)
    squared, at = core.area(at, KD, T)
    std, at = core.area(at, T)
    context, at = core.area(at, 2, B * M)
    q, at = core.area(at, KD, T)
    kT, at = core.area(at, KD, M)
    v_, at = core.area(at, D)
    ctx1, at = core.area(at, 2, M)
    probs, at = core.area(at, 4, M)
    probsT, at = core.area(at, T)
    mixed, at = core.area(at, KD, T)
    rowmax, at = core.area(at, 4)
    rowsum, at = core.area(at, 4)
    name = "last"
    norm_context(core, 1, "gkv", "bekv", context, squared, std)
    wq, wk, wv, wd = (wview(core, 1, 512 * j, 2, D) for j in range(4))
    ln, nm = Lanes(core, name), Norm(core, name)
    ctx_ready = core.sem(f"{name}_ctx_ready")
    s_full = core.sem(f"{name}_scores")
    max_done, shifted = core.sem(f"{name}_max"), core.sem(f"{name}_shifted")
    exp_done = core.sem(f"{name}_exp")
    sum_done, rsum_ready, p_ready = core.sem(f"{name}_sum"), core.sem(f"{name}_rsum"), core.sem(f"{name}_probs")
    t_full, t_free = core.sem(f"{name}_t_full"), core.sem(f"{name}_t_free")
    V_SHARE, S_SHARE = 1 + 2 + 1 + 1 + 2, 1 + 1 + 1
    x_in = lambda b: [(P, core.X[:, k, b, PRE:S1]) for k in range(KD)]
    QT = T // P
    rows = [P] * KD
    V_BEFORE, S_BEFORE = 3, 1
    v_done = lambda b: b * V_SHARE + (V_BEFORE + 2)
    s_done = lambda b: b * S_SHARE + (S_BEFORE + 2)

    with core.nc.Block() as block:
        @block.gpsimd
        def _(e):
            def bring_context(b):
                for k, r in enumerate(CROWS):
                    own = context[0:r, k, bass.ts(b, M)]
                    last = e.tensor_tensor(ctx1[0:r, k, :], own, core.one[0:r, 0:1].to_broadcast([r, M]), ALU.mult)
                last.then_inc(ctx_ready, 1)

            bring_context(0)
            with e.Fori(0, B - 1) as b:
                e.wait_ge(ln.v_free, b * V_SHARE + V_BEFORE)
                bring_context(b + 1)

        @block.tensor
        def _(e):
            V, S = Count(), Count()
            e.wait_ge(core.w_loaded[1], core.w_count[1])
            norm_pe(e, core, nm, ln, V, S, 0, x_in(0), core.mean_d, squared, T)

            def project_context(b):
                e.wait_ge(ctx_ready, b + 1)
                e.wait_ge(ln.v_free, V())
                for m in range(KD):
                    for k, r in enumerate(CROWS):
                        mm = e.matmul(core.lane_v[:, m * M:(m + 1) * M], wk[0:r, k, m * P:(m + 1) * P], ctx1[0:r, k, :],
                                      start=(k == 0), stop=(k == 1))
                mm.then_inc(ln.v_full, 1)
                V.add()
                e.wait_ge(ln.v_free, V())
                for k, r in enumerate(CROWS):
                    mm = e.matmul(core.lane_v[0:M, 0:D], ctx1[0:r, k, :], wv[0:r, k, :], start=(k == 0), stop=(k == 1))
                mm.then_inc(ln.v_full, 1)
                V.add()

            project_context(0)

            def body(b, more):
                V.round(b, V_SHARE, V_BEFORE)
                S.round(b, S_SHARE, S_BEFORE)
                lanes = lanes_of(core, ln, V, S)
                e.wait_ge(nm.ready, b + 1)
                for m in range(KD):
                    lane, free, full, c = lanes[m % 2]
                    e.wait_ge(free, c())
                    for k in range(KD):
                        mm = e.matmul(lane, wq[:, k, m * P:(m + 1) * P], normed[:, k, :], start=(k == 0), stop=(k == KD - 1))
                    mm.then_inc(full, 1)
                    c.add()
                e.wait_ge(ln.v_free, V())
                e.wait_ge(ln.s_free, S())
                for t in range(QT):
                    for k in range(KD):
                        mm = e.matmul(core.banks[:, 0, t * M:(t + 1) * M], q[:, k, t * P:(t + 1) * P], kT[:, k, :],
                                      start=(k == 0), stop=(k == KD - 1))
                mm.then_inc(s_full, 1)
                if more:
                    norm_mean_pe(e, core, ln, V, x_in(b + 1), core.mean_d, T)
                    norm_variance_pe(e, core, nm, ln, S, b + 1, x_in(b + 1), core.mean_d, squared, T)
                e.wait_ge(p_ready, b + 1)
                for t in range(QT):
                    mm = e.matmul(core.banks[0:M, 4, t * P:(t + 1) * P], probs[:, t, :], core.ident[:], start=True, stop=True)
                mm.then_inc(t_full, 1)
                e.wait_ge(t_free, b + 1)
                for m in range(KD):
                    lane, free, full, c = lanes[m % 2]
                    e.wait_ge(free, c())
                    e.matmul(lane, v_[0:M, m * P:(m + 1) * P], probsT[0:M, :], start=True, stop=True).then_inc(full, 1)
                    c.add()
                if more:
                    project_context(b + 1)
                e.wait_ge(ln.v_free, V())
                e.wait_ge(ln.s_free, S())
                for m in range(KD):
                    for k in range(KD):
                        mm = e.matmul((core.lane_v, core.banks[:, 0, :])[m], wd[:, k, m * P:(m + 1) * P], mixed[:, k, :], start=(k == 0), stop=(k == KD - 1))
                    mm.then_inc(ln.v_full, 1)
                    V.add()

            batches(e, body)

        @block.vector
        def _(e):
            V, S = Count(), Count()
            norm_dve(e, core, nm, ln, V, S, 0, x_in(0), centred, std, normed, "gq", T)

            def copy_context():
                e.wait_ge(ln.v_full, V(1))
                for m in range(KD):
                    last = e.tensor_scalar(kT[:, m, :], core.lane_v[:, m * M:(m + 1) * M], core.v("bk", m), None, ALU.add)
                last.then_inc(ln.v_free, 1)
                V.add()
                e.wait_ge(ln.v_full, V(1))
                e.tensor_copy(v_[0:M, :], core.lane_v[0:M, 0:D]).then_inc(ln.v_free, 1)
                V.add()

            copy_context()

            def body(b, more):
                V.round(b, V_SHARE, V_BEFORE)
                e.wait_ge(ln.v_full, V(1))
                e.tensor_scalar(q[:, 0, :], core.lane_v, core.v("bq", 0), None, ALU.add).then_inc(ln.v_free, 1)
                V.add()
                scores = core.banks[:, 0, 0:QT * M].rearrange("p (t m) -> p t m", t=QT)
                e.wait_ge(s_full, b + 1)
                e.tensor_reduce(rowmax, scores, AX.X, ALU.max).then_inc(max_done, 1)
                e.wait_ge(max_done, b + 1)
                e.tensor_tensor(probs, scores, rowmax.unsqueeze(2).to_broadcast([P, QT, M]), ALU.subtract).then_inc(shifted, 1)
                if more:
                    norm_centre_dve(e, core, ln, V, x_in(b + 1), centred, T)
                e.wait_ge(exp_done, b + 1)
                e.tensor_reduce(rowsum, probs, AX.X, ALU.add).then_inc(sum_done, 1)
                e.wait_ge(sum_done, b + 1)
                e.reciprocal(rowsum, rowsum).then_inc(rsum_ready, 1)
                e.wait_ge(rsum_ready, b + 1)
                e.tensor_tensor(probs, probs, rowsum.unsqueeze(2).to_broadcast([P, QT, M]), ALU.mult).then_inc(p_ready, 1)
                e.wait_ge(t_full, b + 1)
                e.tensor_copy(probsT[0:M, :], core.banks[0:M, 4, :]).then_inc(t_free, 1)
                e.wait_ge(ln.v_full, V(1))
                e.tensor_scalar(mixed[:, 0, :], core.lane_v, core.v("bv", 0), None, ALU.add).then_inc(ln.v_free, 1)
                V.add()
                if more:
                    copy_context()
                    norm_scale_dve(e, core, nm, ln, s_done(b), b + 1, rows, centred, std, normed, "gq")
                for m in range(KD):
                    e.wait_ge(ln.v_full, V(1))
                    x = core.X[:, m, b, PRE:S1]
                    e.scalar_tensor_tensor(out=x, in0=(core.lane_v, core.banks[:, 0, :])[m], scalar=core.v("bd", m), in1=x,
                                           op0=ALU.add, op1=ALU.add).then_inc(ln.v_free, 1)
                    V.add()

            batches(e, body)

        @block.scalar
        def _(e):
            V, S = Count(), Count()
            norm_act(e, core, nm, ln, V, S, 0, rows, centred, squared, std, normed, "beq", T)

            def body(b, more):
                S.round(b, S_SHARE, S_BEFORE)
                e.wait_ge(ln.s_full, S(1))
                e.activation(q[:, 1, :], core.lane_s, ACT.Identity, bias=core.v("bq", 1)).then_inc(ln.s_free, 1)
                S.add()
                e.wait_ge(shifted, b + 1)
                e.activation(probs, probs, ACT.Exp).then_inc(exp_done, 1)
                if more:
                    norm_square_act(e, nm, ln, v_done(b), rows, centred, squared)
                    norm_root_act(e, core, ln, S, std, T)
                e.wait_ge(ln.s_full, S(1))
                e.activation(mixed[:, 1, :], core.lane_s, ACT.Identity, bias=core.v("bv", 1)).then_inc(ln.s_free, 1)
                S.add()
                if more:
                    norm_bias_act(e, core, nm, b + 1, rows, normed, "beq")

            batches(e, body)


CHUNKS = B * NCH
STEPS = LAYERS * CHUNKS
BODY = 12
SET = BODY // 2
UN, US = 16, 4
PLAN = {
    "pe": {"conv_01": 0, "out": 1, "conv_23": 2, "z_01": 2, "z_23": 4, "xdbl": 5, "dt": 7, "mean": 11, "x_01": 12, "x_23": 12},
    "act": {"x_01": 4, "square": 5, "x_23": 6, "silu": 7, "xdbl": 8, "z_23": 9, "dt": 10, "exp": 11, "log": 11, "root": 11, "raw": 15},
    "dve": {"residual": 5, "z_01": 6, "dt": 10, "one": 11, "scale": 12, "total": 12, "finish": 12, "raw": 15, "gates": (8, 10, 14)},
    "pool": {"rest": 12, "dt_x": 15},
}
CREDIT = UN
LW = {"norm": (0, 2), "conv_b": (2, 4), "conv_w": (6, 16), "dt_b": (22, 4), "D": (26, 4), "A_log": (30, 64)}
NLW = 94
W_LOADS = 5
FAR = 1e25
A_MAX = -1e-22
MW = (0, 2048, 2240, 2752, 3776)


def load_layer(e, core, side, layer, sem):
    d, w = core.dram, core.weights[1]
    o = [4096 * side + c for c in MW]
    view = lambda c, k, n: w[:, c:c + k * n].rearrange("p (k n) -> p k n", k=k)
    one = lambda a: a[bass.ds(layer, 1)].rearrange("l r n -> (l r) n")
    tiles = lambda a: one(a).rearrange("(k p) n -> p k n", p=P)
    e.dma_start(view(o[0], KD, 2 * DI), tiles(d["in_w"])).then_inc(sem, 16)
    e.dma_start(view(o[1], KI, 48), tiles(d["x_w"])).then_inc(sem, 16)
    e.dma_start(w[0:DTR, o[2]:o[2] + DI], one(d["dt_w"])).then_inc(sem, 16)
    e.dma_start(view(o[3], KI, D), tiles(d["out_w"])).then_inc(sem, 16)
    e.dma_start(w[:, o[4]:o[4] + NLW], one(d["layer_vec"])).then_inc(sem, 16)


def load_mamba(e, core, _):
    core.side_loaded = [core.sem("side0_loaded"), core.sem("side1_loaded")]
    for side in range(2):
        load_layer(e, core, side, 0, core.side_loaded[side])


def prepend(core):
    w1, w2 = wview(core, 0, 6144, 2, D), wview(core, 0, 6656, 2, D)
    hidden, _ = core.area(0, KD, B * M)
    ln = Lanes(core, "pre")
    with core.nc.Block() as block:
        @block.sync
        def _(e):
            load_weights(e, core, 0, [(6144, core.dram["L1_xattn_pre_w1"]), (6656, core.dram["L1_xattn_pre_w2"])])

        @block.tensor
        def _(e):
            e.wait_ge(core.w_loaded[0], core.w_count[0])
            for m in range(KD):
                e.wait_ge(ln.s_free, m)
                for k, r in enumerate(CROWS):
                    mm = e.matmul(core.lane_s, w1[0:r, k, m * P:(m + 1) * P], core.C[0:r, k, :], start=(k == 0), stop=(k == 1))
                mm.then_inc(ln.s_full, 1)
            e.wait_ge(ln.s_free, KD)
            for m in range(KD):
                e.wait_ge(ln.v_free, m)
                for k in range(KD):
                    mm = e.matmul(core.lane_v, w2[:, k, m * P:(m + 1) * P], hidden[:, k, :], start=(k == 0), stop=(k == KD - 1))
                mm.then_inc(ln.v_full, 1)

        @block.scalar
        def _(e):
            for m in range(KD):
                e.wait_ge(ln.s_full, m + 1)
                e.activation(hidden[:, m, :], core.lane_s, ACT.Silu).then_inc(ln.s_free, 1)

        @block.vector
        def _(e):
            for m in range(KD):
                e.wait_ge(ln.v_full, m + 1)
                e.tensor_copy(core.X[:, m, :, 0:PRE], core.lane_v.rearrange("p (b t) -> p b t", b=B)).then_inc(ln.v_free, 1)


def mamba(core):
    at = 0
    bc, at = core.area(at, 2, 2 * DS, TC)
    x, at = core.area(at, 2, KI, TC)
    z, at = core.area(at, 2, KI, TC)
    u, at = core.area(at, 2, KI, TC)
    dt, at = core.area(at, 2, KI, TC + 1)
    t1, at = core.area(at, KI, TC)
    t2, at = core.area(at, KI, TC)
    t3, at = core.area(at, KI, TC)
    fed, at = core.area(at, 4, US, TC + 1)
    normed, at = core.area(at, KD, TC)
    squared, at = core.area(at, KD, TC)
    rstd, at = core.area(at, TC)
    xdbl, at = core.area(at, TC)
    state, at = core.area(at, KI, DS)
    decay, at = core.area(at, 2, KI * DS)
    zero, at = core.area(at, 1)
    log_1, at = core.area(at, 1)
    spread = core.weights[0]
    diag = spread[:, 0:4096].rearrange("p (s k j n) -> p s k j n", s=2, k=KI, j=TAPS)
    hc = spread[:, 4096:7168].rearrange("p (q s t) -> p q s t", q=4, s=US)
    raw = spread[:, 7168:7168 + KI * (TC + 3)].rearrange("p (k t) -> p k t", k=KI)
    banks = core.banks
    da = [banks[:, 2 * s:2 * s + 2, :].rearrange("p a n -> p (a n)")[:, 0:US * (TC + 1)] for s in range(2)]
    da4 = [a.rearrange("p (s t) -> p s t", s=US) for a in da]
    ybank = [banks[:, 4, 0:TC], banks[:, 5, 0:TC]]
    lane_v2 = core.lane_v[:, 0:2 * TC].rearrange("p (m t) -> p m t", m=2)
    lane_s2 = core.lane_s[:, 0:2 * TC].rearrange("p (m t) -> p m t", m=2)
    w = core.weights[1]
    in_w, x_w, dt_w, out_w, vecs = [], [], [], [], []
    for side in range(2):
        o = [4096 * side + c for c in MW]
        in_w.append(w[:, o[0]:o[0] + 2048].rearrange("p (k n) -> p k n", k=KD))
        x_w.append(w[:, o[1]:o[1] + 192].rearrange("p (k n) -> p k n", k=KI))
        dt_w.append(w[0:DTR, o[2]:o[2] + DI])
        out_w.append(w[:, o[3]:o[3] + 1024].rearrange("p (k n) -> p k n", k=KI))
        vecs.append(w[:, o[4]:o[4] + NLW])
    lv = lambda side, name, j: vecs[side][:, LW[name][0] + j:LW[name][0] + j + 1]

    ln = Lanes(core, "mamba")
    S = lambda name: core.sem(f"mamba_{name}")
    set_up = S("set_up")
    side_ready = S("side_ready")
    a_exp = S("a_exp")
    squared_ready, rstd_ln, rstd_ready, normed_ready = S("squared"), S("rstd_ln"), S("rstd"), S("normed")
    carried = S("carried")
    silu_done = S("silu")
    bc_stored, bc_ready = S("bc_stored"), S("bc_ready")
    soft_abs, soft_exp, soft_ln = S("soft_abs"), S("soft_exp"), S("soft_ln")
    soft_one, soft_rest, soft_sum = S("soft_one"), S("soft_rest"), S("soft_sum")
    dt_ready, u_ready = S("dt_ready"), S("u_ready")
    exp_done, fed_ready, scanned, unit_done, summed = S("exp"), S("fed"), S("scanned"), S("unit_done"), S("summed")
    y_skip, gated = S("y_skip"), S("gated")
    scratch = core.nc.dram_tensor("mamba_bc", (2, 2 * DS, TC), F32, kind="Internal").ap()

    FIRST = -2

    def v_after(n, k):
        return k - 4 if isinstance(n, int) and n == FIRST else 6 * n + (7 + k)

    s_after = lambda n, k: 5 * n + (6 + k)
    unit = lambda n, i: n * UN + i

    def at_step(l, half, j):
        n = (l * 2 + half) * BODY + j
        return n, j % 2, j // SET, half * 4 + j // NCH, j % NCH

    def following(l, half, j, d):
        j += d
        if j < BODY:
            return at_step(l, half, j)[1:]
        j -= BODY
        return j % 2, 0, half * -4 + (4 + j // NCH), j % NCH

    def preceding(l, half, j):
        if j > 0:
            return at_step(l, half, j - 1)[1:]
        return 1, 1, half * -4 + 7, NCH - 1

    X = lambda b, c: core.X[:, :, b, c * TC:(c + 1) * TC]

    PE_AT, ACT_AT, DVE_AT, POOL_AT = PLAN["pe"], PLAN["act"], PLAN["dve"], PLAN["pool"]

    def placed(at, **pieces):
        by_unit = {}
        for name, piece in pieces.items():
            by_unit.setdefault(at[name], []).append(piece)
        return by_unit

    def late_pe(e, n, p, side, b, c):
        def convolve(m0):
            def go():
                e.wait_ge(ln.s_free, s_after(n, m0 // 2))
                if m0 == 0:
                    e.wait_ge(ln.v_free, v_after(n - 1, 6))
                for m in range(2):
                    for j in range(TAPS):
                        mm = e.matmul(lane_s2[:, m, :], diag[:, side, m0 + m, j, :], raw[:, m0 + m, j:j + TC],
                                      start=(j == 0), stop=(j == TAPS - 1))
                mm.then_inc(ln.s_full, 1)
            return go

        def project_z(m0):
            def go():
                e.wait_ge(ln.v_free, v_after(n, 1 + m0 // 2))
                for m in range(2):
                    for k in range(KD):
                        f = DI + (m0 + m) * P
                        mm = e.matmul(lane_v2[:, m, :], in_w[side][:, k, f:f + P], normed[:, k, :], start=(k == 0), stop=(k == KD - 1))
                mm.then_inc(ln.v_full, 1)
            return go

        def project_x():
            e.wait_ge(silu_done, n + 2)
            e.wait_ge(ln.s_free, s_after(n, 2))
            for k in range(KI):
                mm = e.matmul(core.lane_s[0:48, 0:TC], x_w[side][:, k, :], x[:, p, k, :], start=(k == 0), stop=(k == KI - 1))
            mm.then_inc(ln.s_full, 1)

        def project_dt():
            e.wait_ge(ln.s_free, s_after(n, 3))
            e.wait_ge(ln.v_free, v_after(n, 3))
            for m in range(KI):
                mm = e.matmul((lane_v2, lane_s2)[m // 2][:, m % 2, :], dt_w[side][:, m * P:(m + 1) * P], xdbl[0:DTR, :],
                              start=True, stop=True)
                if m % 2 == 1:
                    mm.then_inc((ln.v_full, ln.s_full)[m // 2], 1)

        return placed(PE_AT, conv_01=convolve(0), conv_23=convolve(2), z_01=project_z(0), xdbl=project_x, z_23=project_z(2), dt=project_dt)

    def early_pe(e, n, p, side, b, c):
        def mean():
            e.wait_ge(ln.v_free, v_after(n, 4))
            e.wait_ge(squared_ready, n + 3)
            for k in range(KD):
                mm = e.matmul(core.lane_v[:, 0:TC], core.mean_d[:], squared[:, k, :], start=(k == 0), stop=(k == KD - 1))
            mm.then_inc(ln.v_full, 1)

        def project_in(m0):
            def go():
                if m0 == 0:
                    e.wait_ge(normed_ready, n + 3)
                lane, free, full, count = ((lane_v2, ln.v_free, ln.v_full, v_after(n, 5)), (lane_s2, ln.s_free, ln.s_full, s_after(n, 4)))[m0 // 2]
                e.wait_ge(free, count)
                for m in range(2):
                    for k in range(KD):
                        mm = e.matmul(lane[:, m, :], in_w[side][:, k, (m0 + m) * P:(m0 + m + 1) * P], normed[:, k, :],
                                      start=(k == 0), stop=(k == KD - 1))
                mm.then_inc(full, 1)
            return go

        return placed(PE_AT, mean=mean, x_01=project_in(0), x_23=project_in(2))

    def late_act(e, n, p, side, b, c):
        def copy_x(m0):
            def go():
                if m0 == 0:
                    e.wait_ge(ln.v_full, v_after(n, 1))
                e.wait_ge(ln.s_full, s_after(n, 1 + m0 // 2))
                for m in range(2):
                    last = e.activation(x[:, p, m0 + m, :], lane_s2[:, m, :], ACT.Identity, bias=lv(side, "conv_b", m0 + m))
                last.then_inc(ln.s_free, 1)
            return go

        def silu():
            e.wait_ge(ln.s_free, s_after(n, 2))
            e.activation(x[:, p], x[:, p], ACT.Silu).then_inc(silu_done, 1)
            if not (isinstance(n, int) and n < 0):
                e.activation(z[:, 1 - p], z[:, 1 - p], ACT.Silu)

        def copy_z():
            e.wait_ge(ln.v_full, v_after(n, 3))
            e.activation(z[:, p, 2:4, :], lane_v2, ACT.Copy).then_inc(ln.v_free, 1)

        def copy_xdbl():
            e.wait_ge(ln.s_full, s_after(n, 3))
            e.wait_ge(bc_stored, 16 * (n + 1))
            e.activation(xdbl[0:48, :], core.lane_s[0:48, 0:TC], ACT.Copy).then_inc(ln.s_free, 1)

        def bias_dt():
            e.wait_ge(ln.s_full, s_after(n, 4))
            for m in range(2):
                last = e.activation(dt[:, p, 2 + m, 1:], lane_s2[:, m, :], ACT.Identity, bias=lv(side, "dt_b", 2 + m))
            last.then_inc(ln.s_free, 1)

        def exp():
            e.wait_ge(ln.v_free, v_after(n, 4))
            e.wait_ge(ln.s_free, s_after(n, 4))
            e.wait_ge(soft_rest, n + 1)
            e.activation(t1, dt[:, p, :, 1:], ACT.Abs).then_inc(soft_abs, 1)
            e.wait_ge(soft_abs, n + 2)
            e.activation(t1, t1, ACT.Exp, scale=-1.0).then_inc(soft_exp, 1)

        def log():
            e.wait_ge(soft_exp, n + 2)
            e.wait_ge(dt_ready, n + 1)
            e.activation(t2, t1, ACT.Ln, bias=1.0).then_inc(soft_ln, 1)

        return placed(ACT_AT, x_01=copy_x(0), x_23=copy_x(2), silu=silu, z_23=copy_z, xdbl=copy_xdbl, dt=bias_dt, exp=exp, log=log)

    def early_act(e, n, p, side, b, c):
        def square():
            if not (isinstance(n, int) and n == FIRST):
                e.wait_ge(ln.v_full, v_after(n - 1, 5))
            e.activation(squared, X(b, c), ACT.Square).then_inc(squared_ready, 1)

        def inverse_root():
            e.wait_ge(ln.v_full, v_after(n, 5))
            e.activation(rstd, core.lane_v[:, 0:TC], ACT.Ln, bias=core.eps[:]).then_inc(ln.v_free, 1)
            e.wait_ge(ln.v_free, v_after(n, 5))
            e.activation(rstd, rstd, ACT.Exp, scale=-0.5).then_inc(rstd_ready, 1)

        def copy_raw():
            e.wait_ge(ln.s_full, s_after(n, 5))
            e.wait_ge(carried, n + 3)
            e.activation(raw[:, 2:4, 3:], lane_s2, ACT.Copy).then_inc(ln.s_free, 1)

        return placed(ACT_AT, square=square, root=inverse_root, raw=copy_raw)

    def late_dve(e, n, p, side, b, c):
        def copy_z():
            e.wait_ge(ln.v_full, v_after(n, 2))
            e.tensor_copy(z[:, p, 0:2, :], lane_v2).then_inc(ln.v_free, 1)

        def bias_dt():
            e.wait_ge(ln.v_full, v_after(n, 4))
            for m in range(2):
                last = e.tensor_scalar(dt[:, p, m, 1:], lane_v2[:, m, :], lv(side, "dt_b", m), None, ALU.add)
            last.then_inc(ln.v_free, 1)

        def one():
            e.wait_ge(soft_exp, n + 2)
            e.tensor_scalar(t3, t1, 1.0, 1.0, ALU.add, ALU.subtract).then_inc(soft_one, 1)

        def total():
            e.wait_ge(soft_rest, n + 2)
            e.wait_ge(soft_ln, n + 2)
            e.scalar_tensor_tensor(out=t2, in0=t2, scalar=log_1, in1=t3, op0=ALU.subtract, op1=ALU.add).then_inc(soft_sum, 1)

        def finish_dt():
            e.wait_ge(soft_sum, n + 2)
            e.wait_ge(ln.s_free, s_after(n, 4))
            e.scalar_tensor_tensor(out=dt[:, p, :, 1:], in0=dt[:, p, :, 1:], scalar=0.0, in1=t2, op0=ALU.max, op1=ALU.add) \
                .then_inc(dt_ready, 1)

        return placed(DVE_AT, z_01=copy_z, dt=bias_dt, one=one, total=total, finish=finish_dt)

    def early_dve(e, n, p, side, b, c):
        def scale():
            e.wait_ge(rstd_ready, n + 3)
            for k in range(KD):
                last = e.scalar_tensor_tensor(out=normed[:, k, :], in0=core.X[:, k, b, c * TC:(c + 1) * TC],
                                              scalar=lv(side, "norm", k), in1=rstd, op0=ALU.mult, op1=ALU.mult)
            last.then_inc(normed_ready, 1)

        def carry():
            if not (isinstance(n, int) and n == FIRST):
                e.wait_ge(ln.s_full, s_after(n, 2))
            if c == 0:
                e.memset(raw[:, :, 0:3], 0.0).then_inc(carried, 1)
            else:
                e.tensor_copy(raw[:, :, 0:3], raw[:, :, TC:TC + 3]).then_inc(carried, 1)
            e.wait_ge(carried, n + 3)
            e.wait_ge(ln.v_full, v_after(n, 6))
            e.tensor_copy(raw[:, 0:2, 3:], lane_v2).then_inc(ln.v_free, 1)

        return placed(DVE_AT, scale=scale, raw=carry)

    def late_pool(e, n, p):
        def rest():
            e.wait_ge(soft_one, n + 2)
            e.tensor_tensor(t3, t1, t3, ALU.subtract).then_inc(soft_rest, 1)

        def times_x():
            e.wait_ge(dt_ready, n + 2)
            e.wait_ge(silu_done, n + 2)
            e.tensor_tensor(u[:, p], dt[:, p, :, 1:], x[:, p], ALU.mult).then_inc(u_ready, 1)

        return placed(POOL_AT, rest=rest, dt_x=times_x)

    def late_sp(e, n, p):
        e.wait_ge(ln.s_free, s_after(n, 3))
        e.wait_ge(bc_ready, 16 * (n + 1))
        e.dma_start(scratch[p], xdbl[DTR:DTR + 2 * DS, :]).then_inc(bc_stored, 16)
        e.wait_ge(bc_stored, 16 * (n + 2))
        if not (isinstance(n, int) and n < 0):
            e.wait_ge(unit_done, (n + 1) * CREDIT)
        e.dma_start(bc[:, p], scratch[p].partition_broadcast(P)).then_inc(bc_ready, 16)

    def side_act(e, m, side, loads):
        e.wait_ge(core.side_loaded[side], loads)
        e.wait_ge(side_ready, 2 * m)
        e.activation(decay[:, side, :], vecs[side][:, LW["A_log"][0]:LW["A_log"][0] + KI * DS], ACT.Exp).then_inc(a_exp, 1)

    def side_dve(e, m, side, loads):
        e.wait_ge(core.side_loaded[side], loads)
        for k in range(KI):
            for j in range(TAPS):
                last = e.tensor_scalar(diag[:, side, k, j, :], core.ident[:], lv(side, "conv_w", TAPS * k + j), None, ALU.mult)
        last.then_inc(side_ready, 1)
        e.wait_ge(a_exp, m + 1)
        e.tensor_scalar(decay[:, side, :], decay[:, side, :], -1.0, A_MAX, ALU.mult, ALU.min).then_inc(side_ready, 1)

    def project_out(e, n, p, side):
        e.wait_ge(gated, KI * n + KI)
        e.wait_ge(ln.v_free, v_after(n, 0))
        for m in range(KD):
            for k in range(KI):
                mm = e.matmul(lane_v2[:, m, :], out_w[side][:, k, m * P:(m + 1) * P], x[:, p, k, :], start=(k == 0), stop=(k == KI - 1))
        mm.then_inc(ln.v_full, 1)

    def gate(e, n, k, p, side):
        e.wait_ge(summed, n * UN + (CREDIT + UN // KI * (k + 1)))
        e.scalar_tensor_tensor(out=x[:, p, k, :], in0=x[:, p, k, :], scalar=lv(side, "D", k), in1=ybank[k % 2],
                               op0=ALU.mult, op1=ALU.add).then_inc(y_skip, 1)
        e.wait_ge(y_skip, KI * n + (k + 2))
        e.tensor_tensor(x[:, p, k, :], x[:, p, k, :], z[:, p, k, :], ALU.mult).then_inc(gated, 1)

    def residual(e, n, b, c):
        e.wait_ge(ln.v_full, v_after(n, 1))
        e.tensor_tensor(X(b, c), X(b, c), lane_v2, ALU.add).then_inc(ln.v_free, 1)

    def in_order(*parts):
        return {i: [piece for part in parts for piece in part.get(i, [])] for i in range(UN)}

    def before_first(late, early):
        for parts in (early(FIRST, 0, 0, 0, 0),), (late(-1, 0, 0, 0, 0), early(-1, 1, 0, 0, 1)):
            for pieces in in_order(*parts).values():
                for piece in pieces:
                    piece()

    def pieces_of(late, early, e, l, half, j):
        n = at_step(l, half, j)[0]
        return in_order(late(e, n, *following(l, half, j, 1)), early(e, n, *following(l, half, j, 2)))

    LOAD = 16 * W_LOADS
    SETTING = 8
    with core.nc.Block() as block:
        @block.sync
        def _(e):
            late_sp(e, -1, 0)
            with e.Fori(0, LAYERS) as l:
                with e.Fori(0, 2) as half:
                    for j in range(BODY):
                        n = at_step(l, half, j)[0]
                        p = following(l, half, j, 1)[0]
                        if j % SET == 1:
                            e.wait_ge(ln.v_free, v_after(n - 1, 1))
                        late_sp(e, n, p)
                        if j == 1:
                            load_layer(e, core, 1, l, core.side_loaded[1])
                        if j == SET + 1:
                            load_layer(e, core, 0, (l + half) % LAYERS, core.side_loaded[0])
            e.wait_ge(bc_ready, 16 * (STEPS + 1))
            for side in range(2):
                e.wait_ge(core.side_loaded[side], (2 * LAYERS + 1) * LOAD)

        @block.tensor
        def _(e):
            e.wait_ge(side_ready, 2)
            e.wait_ge(core.side_loaded[1], LOAD)
            e.wait_ge(set_up, 5)
            e.matmul(ybank[1], core.ident[:], x[:, 1, 0, :], start=True, stop=True).then_inc(summed, 1)
            before_first(lambda *a: late_pe(e, *a), lambda *a: early_pe(e, *a))
            with e.Fori(0, LAYERS) as l:
                with e.Fori(0, 2) as half:
                    for j in range(BODY):
                        n, p, side, b, c = at_step(l, half, j)
                        pieces = pieces_of(late_pe, early_pe, e, l, half, j)
                        for i in range(UN):
                            if i == PE_AT["out"]:
                                pp, ps, _, _ = preceding(l, half, j)
                                project_out(e, n, pp, ps)
                            if i == SETTING + 1 and j % SET == SET - 2:
                                e.wait_ge(side_ready, 2 * ((l * 2 + half) * 2 + (j // SET + 2)))
                            for piece in pieces[i]:
                                piece()
                            k, q = i // 4, i % 4
                            if q == 0:
                                e.wait_ge(gated, KI * n + (KI + k - 1))
                            e.wait_ge(unit_done, n * UN + (CREDIT + i + 1))
                            for s in range(US):
                                mm = e.matmul(ybank[k % 2], core.ident[:], hc[:, q, s, :], start=(q == 0 and s == 0),
                                              stop=(q == 3 and s == US - 1))
                            mm.then_inc(summed, 1)
            project_out(e, STEPS, 1, 1)

        @block.vector
        def _(e):
            e.memset(state, 0.0).then_inc(set_up, 1)
            e.memset(x[:, 1], 0.0).then_inc(set_up, 1)
            e.memset(z[:, 1], 0.0).then_inc(set_up, 1)
            e.memset(zero, 0.0).then_inc(set_up, 1)
            e.memset(dt[:, :, :, 0:1], FAR).then_inc(set_up, 1)
            scrap = t2[:, 0, :]
            for i in range(CREDIT):
                e.memset(scrap[:, 4 * i:4 * i + 1], 0.0).then_inc(unit_done, 1)
                if i > 0:
                    e.memset(scrap[:, 4 * i + 1:4 * i + 2], 0.0).then_inc(summed, 1)
                if 0 < i < KI:
                    e.memset(scrap[:, 4 * i + 2:4 * i + 3], 0.0).then_inc(gated, 1)
            e.wait_ge(core.side_loaded[1], LOAD)
            side_dve(e, 0, 0, LOAD)
            before_first(lambda *a: late_dve(e, *a), lambda *a: early_dve(e, *a))
            with e.Fori(0, LAYERS) as l:
                with e.Fori(0, 2) as half:
                    for j in range(BODY):
                        n, p, side, b, c = at_step(l, half, j)
                        pp, ps, pb, pc = preceding(l, half, j)
                        pieces = pieces_of(late_dve, early_dve, e, l, half, j)
                        for i in range(UN):
                            k, q = i // 4, i % 4
                            if i == DVE_AT["residual"]:
                                residual(e, n, pb, pc)
                            if i == SETTING and j % SET == SET - 2:
                                m = (l * 2 + half) * 2 + (j // SET + 1)
                                side_dve(e, m, following(l, half, j, 2)[1], (l * 2 + half + 2) * LOAD)
                            for piece in pieces[i]:
                                piece()
                            e.wait_ge(exp_done, unit(n, i) + 1)
                            e.wait_ge(fed_ready, unit(n, i) + 1)
                            e.tensor_tensor_scan(da[i % 2], da[i % 2], fed[:, q].rearrange("p s t -> p (s t)"), 0.0,
                                                 ALU.mult, ALU.add).then_inc(scanned, 1)
                            if i == 1:
                                gate(e, n - 1, KI - 1, pp, ps)
                            if i in DVE_AT["gates"]:
                                gate(e, n, DVE_AT["gates"].index(i), p, side)
                            e.wait_ge(scanned, unit(n, i) + 1)
                            keep = state[:, k, q * US:(q + 1) * US]
                            if c < NCH - 1:
                                e.tensor_copy(keep, da4[i % 2][:, :, TC])
                            else:
                                e.memset(keep, 0.0)
                            e.wait_ge(summed, n * UN + (CREDIT + i - 3))
                            e.tensor_tensor(hc[:, q], da4[i % 2][:, :, 1:], bc[:, p, DS + q * US:DS + (q + 1) * US, :],
                                            ALU.mult).then_inc(unit_done, 1)
            gate(e, STEPS - 1, KI - 1, 1, 1)
            residual(e, STEPS, B - 1, NCH - 1)

        @block.scalar
        def _(e):
            e.wait_ge(set_up, 5)
            e.activation(log_1, zero, ACT.Ln, bias=1.0)
            side_act(e, 0, 0, LOAD)
            before_first(lambda *a: late_act(e, *a), lambda *a: early_act(e, *a))
            with e.Fori(0, LAYERS) as l:
                with e.Fori(0, 2) as half:
                    for j in range(BODY):
                        n, p, side, b, c = at_step(l, half, j)
                        pieces = pieces_of(late_act, early_act, e, l, half, j)
                        if j % SET == 0:
                            e.wait_ge(side_ready, 2 * ((l * 2 + half) * 2 + (j // SET + 1)))
                        for i in range(UN):
                            k, q = i // 4, i % 4
                            if i == 0:
                                e.wait_ge(dt_ready, n + 1)
                            e.wait_ge(unit_done, n * UN + (CREDIT + i - 1))
                            for s in range(US):
                                f = k * DS + q * US + s
                                last = e.activation(da4[i % 2][:, s, :], dt[:, p, k, :], ACT.Exp, scale=decay[:, side, f:f + 1])
                            last.then_inc(exp_done, 1)
                            if i == SETTING and j % SET == SET - 2:
                                m = (l * 2 + half) * 2 + (j // SET + 1)
                                side_act(e, m, following(l, half, j, 2)[1], (l * 2 + half + 2) * LOAD)
                            for piece in pieces[i]:
                                piece()

        @block.gpsimd
        def _(e):
            for pieces in in_order(late_pool(e, -1, 0)).values():
                for piece in pieces:
                    piece()
            with e.Fori(0, LAYERS) as l:
                with e.Fori(0, 2) as half:
                    for j in range(BODY):
                        n, p, side, b, c = at_step(l, half, j)
                        pieces = late_pool(e, n, 1 - p)
                        e.wait_ge(bc_ready, 16 * (n + 1))
                        e.wait_ge(u_ready, n + 1)
                        for i in range(UN):
                            k, q = i // 4, i % 4
                            e.wait_ge(unit_done, n * UN + (CREDIT + i - 3))
                            kept = state[:, k, q * US:(q + 1) * US]
                            e.tensor_tensor(fed[:, q, :, 0], kept, core.one[:, 0:US], ALU.mult)
                            e.tensor_tensor(fed[:, q, :, 1:], u[:, p, k, :].unsqueeze(1).to_broadcast([P, US, TC]),
                                            bc[:, p, q * US:(q + 1) * US, :], ALU.mult).then_inc(fed_ready, 1)
                            for piece in pieces.get(i, []):
                                piece()


def final_norm(core):
    squared, at = core.area(0, KD, T)
    std, at = core.area(at, T)
    s_full, s_free = core.sem("final_s_full"), core.sem("final_s_free")
    squared_ready, inverted = core.sem("final_squared"), core.sem("final_inverted")
    scaled = core.sem("final_scaled")
    with core.nc.Block() as block:
        @block.sync
        def _(e):
            load_second(e, core)

        @block.tensor
        def _(e):
            with e.Fori(0, B) as b:
                e.wait_ge(squared_ready, b + 1)
                e.wait_ge(s_free, b)
                for k in range(KD):
                    mm = e.matmul(core.lane_s, core.mean_d[:], squared[:, k, :], start=(k == 0), stop=(k == KD - 1))
                mm.then_inc(s_full, 1)

        @block.scalar
        def _(e):
            with e.Fori(0, B) as b:
                e.wait_ge(s_full, b)
                e.activation(squared, core.X[:, :, b, PRE:S1], ACT.Square).then_inc(squared_ready, 1)
                e.wait_ge(s_full, b + 1)
                e.wait_ge(scaled, b)
                e.activation(std, core.lane_s, ACT.Sqrt, bias=core.eps[:]).then_inc(s_free, 1)

        @block.vector
        def _(e):
            with e.Fori(0, B) as b:
                e.wait_ge(s_free, b + 1)
                e.reciprocal(std, std).then_inc(inverted, 1)
                e.wait_ge(inverted, b + 1)
                for k in range(KD):
                    x = core.X[:, k, b, PRE:S1]
                    last = e.scalar_tensor_tensor(out=x, in0=x, scalar=core.v("final", k), in1=std, op0=ALU.mult, op1=ALU.mult)
                last.then_inc(scaled, 1)


CONSTS = 6
LOADS = 16 * 5


def start(core):
    d = core.dram
    c_ready = core.const_ready
    with core.nc.Block() as block:
        @block.sync
        def _(e):
            e.dma_start(core.vec[:], d["vec"]).then_inc(core.loaded, 16)
            for k in range(KD):
                e.dma_start(core.X[:, k, :, PRE:S1], d["xT"][k * P:(k + 1) * P]).then_inc(core.loaded, 16)
            load_weights(e, core, 0, [(0, d["L0_xattn_Wq1"]), (2048, d["L0_xattn_Wk1"]), (4096, d["L0_xattn_Wv1"]),
                                      (6144, d["L0_xattn_Wo1"])])
            e.dma_start(core.C[:, 0, :], d["ctxT"][0:P]).then_inc(core.loaded, 16)
            e.dma_start(core.C[0:DC - P, 1, :], d["ctxT"][P:DC]).then_inc(core.loaded, 16)

        @block.gpsimd
        def _(e):
            e.memset(core.mean_d[:], 1.0 / D).then_inc(c_ready, 1)
            e.memset(core.mean_c[:], 1.0 / DC).then_inc(c_ready, 1)
            e.memset(core.eps[:], EPS).then_inc(c_ready, 1)
            e.memset(core.ident[:], 0.0).then_inc(c_ready, 1)
            e.memset(core.one[:], 1.0).then_inc(c_ready, 1)
            e.wait_ge(c_ready, 5)
            e.affine_select(out=core.ident[:], in_=core.ident[:], compare_op=ALU.not_equal, fill=1.0, base=0,
                            pattern=[[-1, P]], channel_multiplier=1).then_inc(c_ready, 1)


def finish(core, out):
    stored = core.sem("stored")
    with core.nc.Block() as block:
        @block.sync
        def _(e):
            for k in range(KD):
                e.dma_start(out[k * P:(k + 1) * P], core.X[:, k, :, PRE:S1]).then_inc(stored, 16)
            e.wait_ge(stored, 16 * KD)


STAGES = [self_attention, cross_attention_0, feed_forward_0, prepend, mamba, final_norm, cross_attention_2, feed_forward_2,
          last_attention]


def build(nc, dram, out):
    with ExitStack() as ctx:
        core = Core(nc, ctx, dram)
        start(core)
        for stage in STAGES:
            stage(core)
        finish(core, out)


def layouts(i):
    import numpy as np

    cols = lambda a, w=P: np.asarray(a).reshape(-1, w).T

    def tall(a):
        return np.concatenate([np.asarray(a), np.zeros(2 * P - DC, np.float32)]).reshape(2, P).T

    g = lambda n: np.asarray(i[n])

    def per_layer(a):
        return a.reshape(LAYERS, -1, P, a.shape[-1]).transpose(0, 2, 1, 3).reshape(LAYERS, P, -1)

    layer_parts = {
        "norm": per_layer(g("L1_xattn_norm_w")[..., None]), "conv_b": per_layer(g("L1_xattn_conv_b")[..., None]),
        "conv_w": per_layer(g("L1_xattn_conv_w")), "dt_b": per_layer(g("L1_xattn_dt_proj_b")[..., None]),
        "D": per_layer(g("L1_xattn_D_param")[..., None]), "A_log": per_layer(g("L1_xattn_A_log")),
    }
    parts = {
        "bo1": cols(g("L0_xattn_bo1")), "bo2": cols(g("L0_xattn_bo2")), "bp": cols(g("L0_xattn_bp")),
        "b2_0": cols(g("L0_xattn_b2")), "g1": cols(g("L0_xattn_g1")), "be1": cols(g("L0_xattn_be1")),
        "g2": cols(g("L0_xattn_g2")), "be2": cols(g("L0_xattn_be2")), "g3": cols(g("L0_xattn_g3")),
        "be3": cols(g("L0_xattn_be3")),
        "final": cols(g("L1_xattn_final_norm_w")), "l1w": cols(g("L2_xattn_ln1_w")), "l1b": cols(g("L2_xattn_ln1_b")),
        "l2w": tall(g("L2_xattn_ln2_w")), "l2b": tall(g("L2_xattn_ln2_b")), "l3w": cols(g("L2_xattn_ln3_w")),
        "l3b": cols(g("L2_xattn_ln3_b")), "bproj": cols(g("L2_xattn_bproj")), "b1": cols(g("L2_xattn_b1")),
        "b2_2": cols(g("L2_xattn_b2")), "bq": cols(g("L3_xattn_bq")), "bk": cols(g("L3_xattn_bk")),
        "bv": cols(g("L3_xattn_bv")), "bd": cols(g("L3_xattn_bd")), "gq": cols(g("L3_xattn_g_q")),
        "beq": cols(g("L3_xattn_be_q")), "gkv": tall(g("L3_xattn_g_kv")), "bekv": tall(g("L3_xattn_be_kv")),
    }
    a = {
        "xT": g("x").transpose(2, 0, 1), "ctxT": g("ctx_768").transpose(2, 0, 1).reshape(DC, B * M),
        "layer_vec": np.concatenate([layer_parts[n] for n in LW], axis=2),
        "vec": np.concatenate([parts[n] for n, _ in VEC_SIZES], axis=1),
        "in_w": g("L1_xattn_in_proj_w").transpose(0, 2, 1), "x_w": g("L1_xattn_x_proj_w").transpose(0, 2, 1),
        "dt_w": g("L1_xattn_dt_proj_w").transpose(0, 2, 1), "out_w": g("L1_xattn_out_proj_w").transpose(0, 2, 1),
        "L3_Wq": g("L3_xattn_Wq").T, "L3_Wk": g("L3_xattn_Wk").T, "L3_Wv": g("L3_xattn_Wv").T, "L3_Wd": g("L3_xattn_Wd").T,
    }
    for n in ["L0_xattn_" + w for w in ("Wq1", "Wk1", "Wv1", "Wo1", "Wq2", "Wk2", "Wv2", "Wo2", "Wp", "W2")] + \
            ["L1_xattn_pre_w1", "L1_xattn_pre_w2"] + ["L2_xattn_" + w for w in ("Wq", "Wkv", "Wproj", "W1", "W2")]:
        a[n] = g(n)
    return {n: np.ascontiguousarray(x) for n, x in a.items()}


def kernel(**inputs):
    import concourse.bacc as bacc
    from concourse.bass_utils import run_bass_kernel_spmd

    nc = bacc.Bacc("TRN2", target_bir_lowering=False, num_devices=1)
    arrays = layouts(inputs)
    dram = {n: nc.dram_tensor(f"in_{n}", a.shape, F32, kind="ExternalInput").ap() for n, a in arrays.items()}
    out = nc.dram_tensor("out_T", (D, B, T), F32, kind="ExternalOutput").ap()
    build(nc, dram, out)
    r = run_bass_kernel_spmd(nc, [{f"in_{n}": a for n, a in arrays.items()}], core_ids=[0])
    return r.results[0]["out_T"].transpose(1, 2, 0)
```
